# Optimizing a Trainium2 kernel written in Bass

```python
import numpy as np
import jax
import jax.numpy as jnp

def _softmax(x, axis=-1):
    return jax.nn.softmax(x, axis=axis)

def _gelu(x):
    return jax.nn.gelu(x, approximate=True)

def _silu(x):
    return jax.nn.silu(x)

def _sigmoid(x):
    return jax.nn.sigmoid(x)

def _layernorm(x, axis=-1, eps=1e-05):
    m = jnp.mean(x, axis=axis, keepdims=True)
    v = jnp.var(x, axis=axis, keepdims=True)
    return (x - m) / jnp.sqrt(v + eps)

def _scatter_add(tgt, idx, src, axis=0):
    return tgt.at[idx].add(src)

def _segment_sum(src, seg, n):
    return jax.ops.segment_sum(src, seg, n)
kernel_name = 'mk_seq_preln_d2_jaxref_r8_6862c2'

def setup_inputs(seed: int=0):
    np.random.seed(seed)
    _w = jnp.asarray

    def _L0_attn_setup():
        import jax, jax.numpy as jnp
        import numpy as np
        import math
        B, T, C, H, K = (2, 512, 256, 16, 4)
        D = C // H

        def _ln(t, g, b, eps=1e-05):
            m = t.mean(-1, keepdims=True)
            v = t.var(-1, keepdims=True)
            return (t - m) / jnp.sqrt(v + eps) * g + b

        def _l2n(t, eps=1e-12):
            return t / jnp.maximum(jnp.linalg.norm(t, axis=-1, keepdims=True), eps)
        key = jax.random.key(seed)
        ks = jax.random.split(key, 16)
        s = 0.02
        target = 1.0 - np.exp(np.linspace(math.log(1 - 0.9), math.log(1 - 0.999), H))
        gamma_b = jnp.asarray(np.log(target / (1 - target)), dtype=jnp.float32)
        inp = {'x': jax.random.normal(ks[0], (B, T, C), jnp.float32), 'Wq': jax.random.normal(ks[1], (C, C), jnp.float32) * s, 'Wk': jax.random.normal(ks[2], (C, C), jnp.float32) * s, 'Wv': jax.random.normal(ks[3], (C, C), jnp.float32) * s, 'Wo': jax.random.normal(ks[4], (C, C), jnp.float32) * s, 'conv_w': jax.random.normal(ks[5], (C, 1, K), jnp.float32) * s, 'conv_b': jnp.zeros((C,), jnp.float32), 'ig_w': jax.random.normal(ks[6], (C, C), jnp.float32) * s, 'ig_b': jnp.full((C,), -3.0, jnp.float32), 'og_w': jax.random.normal(ks[7], (C, C), jnp.float32) * s, 'og_b': jnp.zeros((C,), jnp.float32), 'gamma_w': jax.random.normal(ks[8], (H, C), jnp.float32) * (s * 0.1), 'gamma_b': gamma_b, 'vn_g': jnp.ones((D,), jnp.float32), 'vn_b': jnp.zeros((D,), jnp.float32), 'gn_g': jnp.ones((C,), jnp.float32), 'gn_b': jnp.zeros((C,), jnp.float32), 'mn_g': jnp.ones((D,), jnp.float32), 'mn_b': jnp.zeros((D,), jnp.float32)}
        return inp
    _L0_attn_in = _L0_attn_setup()

    def _L0_ffn_setup():
        import jax, jax.numpy as jnp
        import numpy as np
        H = 256
        NH = 16
        NOPE = 128
        ROPE = 64
        VD = 128
        QHD = NOPE + ROPE
        E = 16
        I = 176
        TOPK = 4
        NSH = 2
        SHI = I * NSH
        EPS = 1e-06
        B, S = (2, 128)

        def rmsnorm(x, w):
            return x * jax.lax.rsqrt(jnp.mean(x * x, axis=-1, keepdims=True) + EPS) * w
        key = jax.random.key(seed)
        ks = jax.random.split(key, 12)
        sd = lambda fan_in: 1.0 / np.sqrt(fan_in)
        return {'hidden_states': jax.random.normal(ks[0], (B, S, H), jnp.float32), 'positions': jnp.broadcast_to(jnp.arange(S, dtype=jnp.int32), (B, S)), 'ln1_w': jnp.ones((H,), jnp.float32), 'ln2_w': jnp.ones((H,), jnp.float32), 'q_w': jax.random.normal(ks[1], (NH * QHD, H), jnp.float32) * sd(H), 'kv_w': jax.random.normal(ks[2], (NH * (NOPE + VD) + ROPE, H), jnp.float32) * sd(H), 'o_w': jax.random.normal(ks[3], (H, NH * VD), jnp.float32) * sd(NH * VD), 'gate_w': jax.random.normal(ks[4], (E, H), jnp.float32) * sd(H), 'w1': jax.random.normal(ks[5], (E, 2 * I, H), jnp.float32) * sd(H), 'w2': jax.random.normal(ks[6], (E, H, I), jnp.float32) * sd(I), 'sh_gu_w': jax.random.normal(ks[7], (2 * SHI, H), jnp.float32) * sd(H), 'sh_down_w': jax.random.normal(ks[8], (H, SHI), jnp.float32) * sd(SHI)}
    _L0_ffn_in = _L0_ffn_setup()

    def _L1_attn_setup():
        import jax, jax.numpy as jnp
        import numpy as np
        EPS = 1e-05
        CHUNK = 64

        def _short_conv(x, w):
            K = w.shape[1]
            T = x.shape[1]
            xp = jnp.pad(x, ((0, 0), (K - 1, 0), (0, 0)))
            y = sum((xp[:, i:i + T, :] * w[:, i] for i in range(K)))
            return jax.nn.silu(y)

        def _l2norm(x):
            return x * jax.lax.rsqrt(jnp.sum(x * x, -1, keepdims=True) + 1e-06)

        def _forward(hidden_states, Wq, Wk, Wv, conv_q, conv_k, conv_v, Wf1, Wf2, Wb, A_log, dt_bias, Wg, bg, o_norm_w, Wo):
            B, T, _ = hidden_states.shape
            H = A_log.shape[0]
            x = hidden_states
            q = _short_conv(x @ Wq, conv_q)
            k = _short_conv(x @ Wk, conv_k)
            v = _short_conv(x @ Wv, conv_v)
            Dk = q.shape[-1] // H
            Dv = v.shape[-1] // H
            q = _l2norm(q.reshape(B, T, H, Dk))
            k = _l2norm(k.reshape(B, T, H, Dk))
            v = v.reshape(B, T, H, Dv)
            beta = jax.nn.sigmoid(x @ Wb)
            g = (x @ Wf1 @ Wf2).reshape(B, T, H, Dk)
            g = -jnp.exp(A_log)[:, None] * jax.nn.softplus(g + dt_bias.reshape(H, Dk))
            gexp = jnp.exp(g)
            scale = Dk ** (-0.5)

            def step(S, inp):
                q_t, k_t, v_t, ge_t, b_t = inp
                S = S * ge_t[..., None]
                kv = jnp.einsum('bhk,bhkv->bhv', k_t, S)
                upd = (v_t - kv) * b_t[..., None]
                S = S + jnp.einsum('bhk,bhv->bhkv', k_t, upd)
                o_t = jnp.einsum('bhk,bhkv->bhv', q_t, S) * scale
                return (S, o_t)

            @jax.checkpoint
            def chunk_fn(S, chunk):
                return jax.lax.scan(step, S, chunk)

            def tm(a):
                a = jnp.moveaxis(a, 1, 0)
                return a.reshape((T // CHUNK, CHUNK) + a.shape[1:])
            S0 = jnp.zeros((B, H, Dk, Dv), dtype=q.dtype)
            _, o = jax.lax.scan(chunk_fn, S0, (tm(q), tm(k), tm(v), tm(gexp), tm(beta)))
            o = jnp.moveaxis(o.reshape((T, B, H, Dv)), 0, 1)
            gate_o = (x @ Wg + bg).reshape(B, T, H, Dv)
            on = o * jax.lax.rsqrt(jnp.mean(o * o, -1, keepdims=True) + EPS) * o_norm_w
            on = on * jax.nn.silu(gate_o)
            return on.reshape(B, T, H * Dv) @ Wo
        key = jax.random.key(seed)
        ks = jax.random.split(key, 16)
        B, T, D = (2, 256, 256)
        H, Dk, Dv, K = (16, 128, 128, 4)
        n = jax.random.normal
        return {'hidden_states': n(ks[0], (B, T, D), jnp.float32), 'Wq': n(ks[1], (D, H * Dk), jnp.float32) * D ** (-0.5), 'Wk': n(ks[2], (D, H * Dk), jnp.float32) * D ** (-0.5), 'Wv': n(ks[3], (D, H * Dv), jnp.float32) * D ** (-0.5), 'conv_q': n(ks[4], (H * Dk, K), jnp.float32) * 0.5, 'conv_k': n(ks[5], (H * Dk, K), jnp.float32) * 0.5, 'conv_v': n(ks[6], (H * Dv, K), jnp.float32) * 0.5, 'Wf1': n(ks[7], (D, Dv), jnp.float32) * D ** (-0.5), 'Wf2': n(ks[8], (Dv, H * Dk), jnp.float32) * Dv ** (-0.5), 'Wb': n(ks[9], (D, H), jnp.float32) * D ** (-0.5), 'A_log': jnp.log(jax.random.uniform(ks[10], (H,), jnp.float32, 1.0, 16.0)), 'dt_bias': jnp.zeros((H * Dk,), jnp.float32), 'Wg': n(ks[11], (D, H * Dv), jnp.float32) * D ** (-0.5), 'bg': jnp.zeros((H * Dv,), jnp.float32), 'o_norm_w': jnp.ones((Dv,), jnp.float32), 'Wo': n(ks[12], (H * Dv, D), jnp.float32) * (H * Dv) ** (-0.5)}
    _L1_attn_in = _L1_attn_setup()

    def _L1_ffn_setup():
        import jax, jax.numpy as jnp
        import numpy as np
        DIM_IN = 256
        DIM_HIDDEN = 1024
        key = jax.random.key(seed)
        k_x, k_g, k_u, k_d = jax.random.split(key, 4)
        s_in = 1.0 / np.sqrt(DIM_IN)
        s_hid = 1.0 / np.sqrt(DIM_HIDDEN)
        x = jax.random.normal(k_x, (4, 256, DIM_IN), dtype=jnp.float32)
        w_gate = jax.random.uniform(k_g, (DIM_HIDDEN, DIM_IN), jnp.float32, -s_in, s_in)
        w_up = jax.random.uniform(k_u, (DIM_HIDDEN, DIM_IN), jnp.float32, -s_in, s_in)
        w_down = jax.random.uniform(k_d, (DIM_IN, DIM_HIDDEN), jnp.float32, -s_hid, s_hid)
        return {'x': x, 'w_gate': w_gate, 'w_up': w_up, 'w_down': w_down}
    _L1_ffn_in = _L1_ffn_setup()
    _d = {'L0_attn_x': _L0_attn_in['x'], 'L0_attn_Wq': _L0_attn_in['Wq'], 'L0_attn_Wk': _L0_attn_in['Wk'], 'L0_attn_Wv': _L0_attn_in['Wv'], 'L0_attn_Wo': _L0_attn_in['Wo'], 'L0_attn_conv_w': _L0_attn_in['conv_w'], 'L0_attn_conv_b': _L0_attn_in['conv_b'], 'L0_attn_ig_w': _L0_attn_in['ig_w'], 'L0_attn_ig_b': _L0_attn_in['ig_b'], 'L0_attn_og_w': _L0_attn_in['og_w'], 'L0_attn_og_b': _L0_attn_in['og_b'], 'L0_attn_gamma_w': _L0_attn_in['gamma_w'], 'L0_attn_gamma_b': _L0_attn_in['gamma_b'], 'L0_attn_vn_g': _L0_attn_in['vn_g'], 'L0_attn_vn_b': _L0_attn_in['vn_b'], 'L0_attn_gn_g': _L0_attn_in['gn_g'], 'L0_attn_gn_b': _L0_attn_in['gn_b'], 'L0_attn_mn_g': _L0_attn_in['mn_g'], 'L0_attn_mn_b': _L0_attn_in['mn_b'], 'L0_ffn_positions': _L0_ffn_in['positions'], 'L0_ffn_ln1_w': _L0_ffn_in['ln1_w'], 'L0_ffn_ln2_w': _L0_ffn_in['ln2_w'], 'L0_ffn_q_w': _L0_ffn_in['q_w'], 'L0_ffn_kv_w': _L0_ffn_in['kv_w'], 'L0_ffn_o_w': _L0_ffn_in['o_w'], 'L0_ffn_gate_w': _L0_ffn_in['gate_w'], 'L0_ffn_w1': _L0_ffn_in['w1'], 'L0_ffn_w2': _L0_ffn_in['w2'], 'L0_ffn_sh_gu_w': _L0_ffn_in['sh_gu_w'], 'L0_ffn_sh_down_w': _L0_ffn_in['sh_down_w'], 'L1_attn_Wq': _L1_attn_in['Wq'], 'L1_attn_Wk': _L1_attn_in['Wk'], 'L1_attn_Wv': _L1_attn_in['Wv'], 'L1_attn_conv_q': _L1_attn_in['conv_q'], 'L1_attn_conv_k': _L1_attn_in['conv_k'], 'L1_attn_conv_v': _L1_attn_in['conv_v'], 'L1_attn_Wf1': _L1_attn_in['Wf1'], 'L1_attn_Wf2': _L1_attn_in['Wf2'], 'L1_attn_Wb': _L1_attn_in['Wb'], 'L1_attn_A_log': _L1_attn_in['A_log'], 'L1_attn_dt_bias': _L1_attn_in['dt_bias'], 'L1_attn_Wg': _L1_attn_in['Wg'], 'L1_attn_bg': _L1_attn_in['bg'], 'L1_attn_o_norm_w': _L1_attn_in['o_norm_w'], 'L1_attn_Wo': _L1_attn_in['Wo'], 'L1_ffn_w_gate': _L1_ffn_in['w_gate'], 'L1_ffn_w_up': _L1_ffn_in['w_up'], 'L1_ffn_w_down': _L1_ffn_in['w_down']}
    _x0 = _d['L0_attn_x']
    _d['L0_attn_x'] = jax.random.normal(jax.random.fold_in(jax.random.key(seed), 1), (4, 512, 256), dtype=_x0.dtype)
    del _x0
    return _d

def reference(L0_attn_x, L0_attn_Wq, L0_attn_Wk, L0_attn_Wv, L0_attn_Wo, L0_attn_conv_w, L0_attn_conv_b, L0_attn_ig_w, L0_attn_ig_b, L0_attn_og_w, L0_attn_og_b, L0_attn_gamma_w, L0_attn_gamma_b, L0_attn_vn_g, L0_attn_vn_b, L0_attn_gn_g, L0_attn_gn_b, L0_attn_mn_g, L0_attn_mn_b, L0_ffn_positions, L0_ffn_ln1_w, L0_ffn_ln2_w, L0_ffn_q_w, L0_ffn_kv_w, L0_ffn_o_w, L0_ffn_gate_w, L0_ffn_w1, L0_ffn_w2, L0_ffn_sh_gu_w, L0_ffn_sh_down_w, L1_attn_Wq, L1_attn_Wk, L1_attn_Wv, L1_attn_conv_q, L1_attn_conv_k, L1_attn_conv_v, L1_attn_Wf1, L1_attn_Wf2, L1_attn_Wb, L1_attn_A_log, L1_attn_dt_bias, L1_attn_Wg, L1_attn_bg, L1_attn_o_norm_w, L1_attn_Wo, L1_ffn_w_gate, L1_ffn_w_up, L1_ffn_w_down):

    def _L0_attn_ref(x, Wq, Wk, Wv, Wo, conv_w, conv_b, ig_w, ig_b, og_w, og_b, gamma_w, gamma_b, vn_g, vn_b, gn_g, gn_b, mn_g, mn_b):
        import jax, jax.numpy as jnp
        import numpy as np
        import math
        B, T, C, H, K = (2, 512, 256, 16, 4)
        D = C // H

        def _ln(t, g, b, eps=1e-05):
            m = t.mean(-1, keepdims=True)
            v = t.var(-1, keepdims=True)
            return (t - m) / jnp.sqrt(v + eps) * g + b

        def _l2n(t, eps=1e-12):
            return t / jnp.maximum(jnp.linalg.norm(t, axis=-1, keepdims=True), eps)
        Bs, Ts, Cs = x.shape
        Hs = gamma_w.shape[0]
        Ds = Cs // Hs
        Ks = conv_w.shape[-1]
        xt = jnp.transpose(x, (0, 2, 1))
        xc = jax.lax.conv_general_dilated(xt, conv_w, window_strides=(1,), padding=[(Ks - 1, 0)], dimension_numbers=('NCH', 'OIH', 'NCH'), feature_group_count=Cs)
        xc = jax.nn.silu(jnp.transpose(xc + conv_b[None, :, None], (0, 2, 1)))
        q = _l2n((x @ Wq.T).reshape(Bs, Ts, Hs, Ds))
        k = _l2n((x @ Wk.T).reshape(Bs, Ts, Hs, Ds))
        v = _ln((x @ Wv.T).reshape(Bs, Ts, Hs, Ds), vn_g, vn_b)
        i_gate = jax.nn.sigmoid(xc @ ig_w.T + ig_b).reshape(Bs, Ts, Hs, Ds)
        gamma = jax.nn.sigmoid(xc @ gamma_w.T + gamma_b)[..., None]
        a = jnp.broadcast_to(gamma, (Bs, Ts, Hs, Ds))
        b = i_gate * k * v

        def comb(left, right):
            aL, bL = left
            aR, bR = right
            return (aL * aR, bL * aR + bR)
        _, mem = jax.lax.associative_scan(comb, (a, b), axis=1)
        out = _ln(mem, mn_g, mn_b) * q
        o = out.reshape(Bs * Ts, Hs, Ds)
        m = o.mean(-1, keepdims=True)
        var = o.var(-1, keepdims=True)
        o = (o - m) / jnp.sqrt(var + 1e-05)
        o = o.reshape(Bs * Ts, Cs) * gn_g + gn_b
        o = o.reshape(Bs, Ts, Cs)
        o = o * jax.nn.sigmoid(xc @ og_w.T + og_b)
        return o @ Wo.T

    def _L0_ffn_ref(hidden_states, positions, ln1_w, ln2_w, q_w, kv_w, o_w, gate_w, w1, w2, sh_gu_w, sh_down_w):
        import jax, jax.numpy as jnp
        import numpy as np
        H = 256
        NH = 16
        NOPE = 128
        ROPE = 64
        VD = 128
        QHD = NOPE + ROPE
        E = 16
        I = 176
        TOPK = 4
        NSH = 2
        SHI = I * NSH
        EPS = 1e-06
        B, S = (2, 128)

        def rmsnorm(x, w):
            return x * jax.lax.rsqrt(jnp.mean(x * x, axis=-1, keepdims=True) + EPS) * w
        b, s, h = hidden_states.shape
        x = rmsnorm(hidden_states, ln1_w)
        q = jnp.einsum('bsh,dh->bsd', x, q_w).reshape(b, s, NH, QHD)[..., :NOPE]
        kv = jnp.einsum('bsh,dh->bsd', x, kv_w)
        k = kv[..., :NH * NOPE].reshape(b, s, NH, NOPE)
        v = kv[..., NH * NOPE:NH * (NOPE + VD)].reshape(b, s, NH, VD)
        scale = QHD ** (-0.5)
        scores = jnp.einsum('bqnd,bknd->bnqk', q, k) * scale
        causal = jnp.tril(jnp.ones((s, s), bool))
        scores = jnp.where(causal, scores, -1000000000.0)
        p = jax.nn.softmax(scores, axis=-1)
        attn = jnp.einsum('bnqk,bknd->bqnd', p, v).reshape(b, s, NH * VD)
        attn_out = jnp.einsum('bsd,hd->bsh', attn, o_w)
        hid = hidden_states + attn_out
        x2 = rmsnorm(hid, ln2_w).reshape(-1, h)
        logits = x2 @ gate_w.T
        probs = jax.nn.softmax(logits, axis=-1)
        top_w, top_i = jax.lax.top_k(probs, TOPK)
        top_w = top_w / jnp.sum(top_w, axis=-1, keepdims=True)
        wfull = jnp.sum(jax.nn.one_hot(top_i, E, dtype=x2.dtype) * top_w[..., None], axis=1)
        gu = jnp.einsum('th,eih->tei', x2, w1)
        g, u = (gu[..., :I], gu[..., I:])
        act = jax.nn.silu(g) * u
        down = jnp.einsum('tei,ehi->teh', act, w2)
        routed = jnp.einsum('te,teh->th', wfull, down)
        sgu = x2 @ sh_gu_w.T
        sg, su = (sgu[..., :SHI], sgu[..., SHI:])
        shared = jax.nn.silu(sg) * su @ sh_down_w.T
        return hid + (routed + shared).reshape(b, s, h)

    def _L1_attn_ref(hidden_states, Wq, Wk, Wv, conv_q, conv_k, conv_v, Wf1, Wf2, Wb, A_log, dt_bias, Wg, bg, o_norm_w, Wo):
        import jax, jax.numpy as jnp
        import numpy as np
        EPS = 1e-05
        CHUNK = 64

        def _short_conv(x, w):
            K = w.shape[1]
            T = x.shape[1]
            xp = jnp.pad(x, ((0, 0), (K - 1, 0), (0, 0)))
            y = sum((xp[:, i:i + T, :] * w[:, i] for i in range(K)))
            return jax.nn.silu(y)

        def _l2norm(x):
            return x * jax.lax.rsqrt(jnp.sum(x * x, -1, keepdims=True) + 1e-06)

        def _forward(hidden_states, Wq, Wk, Wv, conv_q, conv_k, conv_v, Wf1, Wf2, Wb, A_log, dt_bias, Wg, bg, o_norm_w, Wo):
            B, T, _ = hidden_states.shape
            H = A_log.shape[0]
            x = hidden_states
            q = _short_conv(x @ Wq, conv_q)
            k = _short_conv(x @ Wk, conv_k)
            v = _short_conv(x @ Wv, conv_v)
            Dk = q.shape[-1] // H
            Dv = v.shape[-1] // H
            q = _l2norm(q.reshape(B, T, H, Dk))
            k = _l2norm(k.reshape(B, T, H, Dk))
            v = v.reshape(B, T, H, Dv)
            beta = jax.nn.sigmoid(x @ Wb)
            g = (x @ Wf1 @ Wf2).reshape(B, T, H, Dk)
            g = -jnp.exp(A_log)[:, None] * jax.nn.softplus(g + dt_bias.reshape(H, Dk))
            gexp = jnp.exp(g)
            scale = Dk ** (-0.5)

            def step(S, inp):
                q_t, k_t, v_t, ge_t, b_t = inp
                S = S * ge_t[..., None]
                kv = jnp.einsum('bhk,bhkv->bhv', k_t, S)
                upd = (v_t - kv) * b_t[..., None]
                S = S + jnp.einsum('bhk,bhv->bhkv', k_t, upd)
                o_t = jnp.einsum('bhk,bhkv->bhv', q_t, S) * scale
                return (S, o_t)

            @jax.checkpoint
            def chunk_fn(S, chunk):
                return jax.lax.scan(step, S, chunk)

            def tm(a):
                a = jnp.moveaxis(a, 1, 0)
                return a.reshape((T // CHUNK, CHUNK) + a.shape[1:])
            S0 = jnp.zeros((B, H, Dk, Dv), dtype=q.dtype)
            _, o = jax.lax.scan(chunk_fn, S0, (tm(q), tm(k), tm(v), tm(gexp), tm(beta)))
            o = jnp.moveaxis(o.reshape((T, B, H, Dv)), 0, 1)
            gate_o = (x @ Wg + bg).reshape(B, T, H, Dv)
            on = o * jax.lax.rsqrt(jnp.mean(o * o, -1, keepdims=True) + EPS) * o_norm_w
            on = on * jax.nn.silu(gate_o)
            return on.reshape(B, T, H * Dv) @ Wo
        return _forward(hidden_states, Wq, Wk, Wv, conv_q, conv_k, conv_v, Wf1, Wf2, Wb, A_log, dt_bias, Wg, bg, o_norm_w, Wo)

    def _L1_ffn_ref(x, w_gate, w_up, w_down):
        import jax, jax.numpy as jnp
        import numpy as np
        DIM_IN = 256
        DIM_HIDDEN = 1024
        gate = jnp.einsum('bsd,hd->bsh', x, w_gate)
        up = jnp.einsum('bsd,hd->bsh', x, w_up)
        gated = jax.nn.silu(gate) * up
        return jnp.einsum('bsh,dh->bsd', gated, w_down)
    x = L0_attn_x
    x = x + _L0_attn_ref(_layernorm(x, axis=-1), L0_attn_Wq, L0_attn_Wk, L0_attn_Wv, L0_attn_Wo, L0_attn_conv_w, L0_attn_conv_b, L0_attn_ig_w, L0_attn_ig_b, L0_attn_og_w, L0_attn_og_b, L0_attn_gamma_w, L0_attn_gamma_b, L0_attn_vn_g, L0_attn_vn_b, L0_attn_gn_g, L0_attn_gn_b, L0_attn_mn_g, L0_attn_mn_b)
    x = x + _L0_ffn_ref(_layernorm(x, axis=-1), L0_ffn_positions, L0_ffn_ln1_w, L0_ffn_ln2_w, L0_ffn_q_w, L0_ffn_kv_w, L0_ffn_o_w, L0_ffn_gate_w, L0_ffn_w1, L0_ffn_w2, L0_ffn_sh_gu_w, L0_ffn_sh_down_w)
    x = x + _L1_attn_ref(_layernorm(x, axis=-1), L1_attn_Wq, L1_attn_Wk, L1_attn_Wv, L1_attn_conv_q, L1_attn_conv_k, L1_attn_conv_v, L1_attn_Wf1, L1_attn_Wf2, L1_attn_Wb, L1_attn_A_log, L1_attn_dt_bias, L1_attn_Wg, L1_attn_bg, L1_attn_o_norm_w, L1_attn_Wo)
    x = x + _L1_ffn_ref(_layernorm(x, axis=-1), L1_ffn_w_gate, L1_ffn_w_up, L1_ffn_w_down)
    return x

_drawn_inputs = setup_inputs


def setup_inputs(seed=0):
    import zlib

    import numpy as np

    out = dict(_drawn_inputs(seed))
    spreads = {'L0_attn_conv_b': (0.0, 0.8),
     'L0_attn_ig_b': (-3.0, 0.2),
     'L0_attn_og_b': (0.0, 0.631),
     'L0_attn_vn_g': (1.0, 0.2),
     'L0_attn_vn_b': (0.0, 0.363),
     'L0_attn_gn_g': (1.0, 0.2),
     'L0_attn_gn_b': (0.0, 0.304),
     'L0_attn_mn_g': (1.0, 0.2),
     'L0_attn_mn_b': (0.0, 0.328),
     'L0_ffn_ln1_w': (1.0, 0.2),
     'L0_ffn_ln2_w': (1.0, 0.2),
     'L1_attn_dt_bias': (0.0, 2.0),
     'L1_attn_bg': (0.0, 0.457),
     'L1_attn_o_norm_w': (1.0, 0.2)}
    factors = {'L0_attn_conv_w': 8.0,
     'L0_attn_ig_w': 8.0,
     'L0_attn_og_w': 8.0,
     'L0_attn_gamma_w': 27.784,
     'L1_attn_Wf1': 2.987,
     'L1_attn_Wf2': 3.003,
     'L1_attn_A_log': 3.085}
    for name, (base, spread) in spreads.items():
        noise = np.random.default_rng([zlib.crc32(name.encode()), seed]).standard_normal(out[name].shape)
        drawn = base * np.exp(spread * noise) if base else spread * noise
        out[name] = jnp.asarray(drawn.astype(out[name].dtype))
    for name, factor in factors.items():
        out[name] = (out[name] * factor).astype(out[name].dtype)
    return out
```

```python
from contextlib import ExitStack

import numpy as np

import concourse.bass as bass
from concourse import mybir
from concourse.alu_op_type import AluOpType as ALU

F32 = mybir.dt.float32
U32 = mybir.dt.uint32
ACT = mybir.ActivationFunctionType
AXX = mybir.AxisListType.X

P = 128
B, T, C = 4, 512, 256
N = B * T
KC = C // P
TILE = 512
NT = N // TILE
HEADS = 16
KTAPS = 4
D0 = C // HEADS

EYE, MEAN_C, MEAN_D, MEAN_P, ONES, CAUSAL_OUT = range(6)
N_MATS = 6
(ZERO, EPS5, EPS6, L2BACK, QSCALE, ODD0) = range(6)
EVEN0 = ODD0 + 7
ONE = EVEN0 + 7
N_SMALL = ONE + 1

L0_MATS = 7
(W_Q, W_K, W_V, W_I, W_OG, W_GAM, W_O) = range(L0_MATS)
(V_TAP0, V_TAP1, V_TAP2, V_TAP3, V_CONVB, V_IB, V_OB, V_GB, V_VG, V_VB, V_MG, V_MB, V_GG, V_GNB, V_LN1,
 V_LN2, V_ON, V_COUNT) = range(18)

QHD, VD = 192, 128
ATTN_SCALE = float(QHD) ** -0.5
ATTN_W = 3 * KC * P + C

E, I, TOPK, SHI = 16, 176, 4, 352
FF0 = E * I + SHI
J0 = (FF0 + P - 1) // P
FF1 = 1024
J1 = FF1 // P
SELROWS = E + 1

CH = 128
NC_ = T // CH
LEVELS = 7
(H_CQ, H_CK, H_CV, H_DT, H_BG, H_ALOG, H_ON, H_COLS) = (0, 4, 8, 12, 13, 14, 15, 16)
KDA_W = 4 * KC * P + P + C + H_COLS


class Signals:

    def __init__(self, nc):
        self.nc, self.sems = nc, []

    def __enter__(self):
        return self

    def __call__(self, name):
        self.sems.append(self.nc.alloc_semaphore(name))
        return self.sems[-1]

    def __exit__(self, *_):
        self.nc.clear_and_free_semaphores(self.sems)
        self.nc.all_engine_barrier()


class Tally:

    def __init__(self, sem, per):
        self.sem, self.per = sem, per

    def prime(self, eng):
        eng.sem_inc(self.sem, self.per)

    def now(self, turn, n=None):
        return self.sem, turn * self.per + (self.per + (self.per if n is None else n))

    def last(self, turn, n=None):
        return self.sem, turn * self.per + (self.per if n is None else n)


def bcast(ap, dim, count):
    wide = ap.unsqueeze(dim)
    shape = list(wide.shape)
    shape[dim] = count
    return wide.broadcast_to(shape)


def norm_stage(nc, name, K, src, dst, centred, eps_col, weight_col):
    with ExitStack() as ctx:
        signals = ctx.enter_context(Signals(nc))
        def sb(n, shape):
            return ctx.enter_context(nc.sbuf_tensor(f"{name}_{n}", shape, F32))

        def sem(n):
            return signals(f"{name}_{n}")

        squares = sb("squares", [P, KC, N])
        logvar = sb("logvar", [P, N])
        rstd = sb("rstd", [P, N])
        ps_mean = [ctx.enter_context(nc.psum_tensor(f"{name}_psm{t}", [P, TILE], F32)) for t in range(NT)]
        ps_var = [ctx.enter_context(nc.psum_tensor(f"{name}_psv{t}", [P, TILE], F32)) for t in range(NT)]
        mean_ready, centre_ready, square_ready, var_ready = (sem(n) for n in ("mean", "centre", "square", "var"))
        logvar_ready, rstd_ready, normed = (sem(n) for n in ("logvar", "rstd", "normed"))
        block = ctx.enter_context(nc.Block())
        mean_mat = K.mats[:, MEAN_C, :]
        body = dst if centred else src

        def tok(t):
            return slice(t * TILE, (t + 1) * TILE)

        @block.tensor
        def _(pe):
            if centred:
                for t in range(NT):
                    for k in range(KC):
                        mm = nc.tensor.matmul(ps_mean[t][:], mean_mat, src[:, k, tok(t)], start=k == 0, stop=k == KC - 1)
                    mm.then_inc(mean_ready, 1)
            for t in range(NT):
                pe.wait_ge(square_ready, t + 1)
                for k in range(KC):
                    mm = nc.tensor.matmul(ps_var[t][:], mean_mat, squares[:, k, tok(t)], start=k == 0, stop=k == KC - 1)
                mm.then_inc(var_ready, 1)

        @block.scalar
        def _(act):
            for t in range(NT):
                if centred:
                    act.wait_ge(centre_ready, t + 1)
                nc.scalar.activation(squares[:, :, tok(t)], body[:, :, tok(t)], ACT.Square).then_inc(square_ready, 1)
            for t in range(NT):
                act.wait_ge(var_ready, t + 1)
                nc.scalar.activation(logvar[:, tok(t)], ps_var[t][:], ACT.Ln, bias=K.small[:, eps_col:eps_col + 1]).then_inc(logvar_ready, 1)
                act.wait_ge(logvar_ready, t + 1)
                nc.scalar.activation(rstd[:, tok(t)], logvar[:, tok(t)], ACT.Exp, scale=-0.5).then_inc(rstd_ready, 1)

        @block.vector
        def _(dve):
            if centred:
                for t in range(NT):
                    dve.wait_ge(mean_ready, t + 1)
                    nc.vector.tensor_tensor(dst[:, :, tok(t)], src[:, :, tok(t)], bcast(ps_mean[t][:], 1, KC), ALU.subtract).then_inc(centre_ready, 1)
            for t in range(NT):
                dve.wait_ge(rstd_ready, t + 1)
                if centred:
                    nc.vector.tensor_tensor(dst[:, :, tok(t)], dst[:, :, tok(t)], bcast(rstd[:, tok(t)], 1, KC), ALU.mult).then_inc(normed, 1)
                else:
                    for k in range(KC):
                        nc.vector.scalar_tensor_tensor(dst[:, k, tok(t)], src[:, k, tok(t)], K.vec[:, weight_col, k:k + 1], rstd[:, tok(t)], ALU.mult, ALU.mult).then_inc(normed, 1)


def memory_stage(nc, K, X, XN, weights_dram):
    with ExitStack() as ctx:
        signals = ctx.enter_context(Signals(nc))
        def sb(n, shape=(P, KC, T)):
            return ctx.enter_context(nc.sbuf_tensor("mem_" + n, list(shape), F32))

        def tallies(names):
            return [Tally(signals("mem_" + n), 1) for n in names.split()]

        w = sb("w", [P, L0_MATS, KC, C])
        conv, xc, q_raw, k_raw, v_raw, q_sq, k_sq, v_sq = (sb(f"b{n}") for n in range(8))
        q_rs, k_rs, v_rs, q, k, v, ig, gam, og = (sb(f"c{n}") for n in range(9))
        mem, mem_sq, mem_rs, out, out_sq, out_rs = (sb(f"d{n}") for n in range(6))
        pa, pb, pc, pd = (ctx.enter_context(nc.psum_tensor(f"mem_p{i}", [P, KC, T], F32)) for i in range(4))
        (q_lin, k_lin, v_lin, q_sum, k_sum, v_mean, v_var, ig_lin, gam_lin, og_lin, mem_mean, mem_var, out_mean,
         out_var, o_lin) = pe_made = tallies("q_lin k_lin v_lin q_sum k_sum v_mean v_var ig_lin gam_lin og_lin mem_mean mem_var out_mean out_var o_lin")
        (q_got, k_got, v_got, q_sqd, k_sqd, v_sqd, xc_got, q_log, q_rsd, k_log, k_rsd, v_log, v_rsd, ig_got, gam_got,
         og_got, mem_sqd, mem_log, mem_rsd, out_sqd, out_log, out_rsd) = act_made = tallies(
            "q_got k_got v_got q_sqd k_sqd v_sqd xc_got q_log q_rsd k_log k_rsd v_log v_rsd ig_got gam_got og_got mem_sqd mem_log mem_rsd out_sqd out_log out_rsd")
        (q_floor, k_floor, v_cent, q_nrm, k_nrm, v_nrm, v_aff, kv, ikv, scanned, mem_cent, mem_nrm, mem_aff,
         mem_q, out_cent, out_nrm, out_aff, gated, added) = dve_made = tallies(
            "q_floor k_floor v_cent q_nrm k_nrm v_nrm v_aff kv ikv scanned mem_cent mem_nrm mem_aff mem_q out_cent out_nrm out_aff gated added")
        conv_step = Tally(signals("mem_conv_step"), KTAPS)
        w_in = signals("mem_w_in")
        block = ctx.enter_context(nc.Block())
        head_mean = K.mats[:, MEAN_D, :]
        zero, eps5 = K.small[:, ZERO:ZERO + 1], K.small[:, EPS5:EPS5 + 1]
        floor_back = K.small[:, L2BACK:L2BACK + 1]

        def col(n, h):
            return K.vec[:, n, h:h + 1]

        def linear(out, mat, rhs):
            for m in range(KC):
                for c in range(KC):
                    mm = nc.tensor.matmul(out[:, m, :], w[:, mat, c, m * P:(m + 1) * P], rhs(c), start=c == 0, stop=c == KC - 1)
            return mm

        def head_means(out, of):
            for m in range(KC):
                mm = nc.tensor.matmul(out[:, m, :], head_mean, of[:, m, :], start=True, stop=True)
            return mm

        @block.sync
        def _(sp):
            sp.dma_start(w[:], weights_dram[:]).then_inc(w_in, 16)

        @block.tensor
        def _(pe):
            for x in pe_made:
                x.prime(pe)
            pe.wait_ge(w_in, 16)
            with pe.Fori(0, B) as b:
                def xn(c):
                    return XN[:, c, bass.ds(b * T, T)]

                pe.wait_ge(*added.last(b))
                linear(pa, W_Q, xn).then_inc(q_lin.sem, 1)
                linear(pb, W_K, xn).then_inc(k_lin.sem, 1)
                linear(pc, W_V, xn).then_inc(v_lin.sem, 1)
                pe.wait_ge(*q_sqd.now(b))
                head_means(pd, q_sq).then_inc(q_sum.sem, 1)
                pe.wait_ge(*q_got.now(b))
                pe.wait_ge(*k_sqd.now(b))
                head_means(pa, k_sq).then_inc(k_sum.sem, 1)
                pe.wait_ge(*k_got.now(b))
                pe.wait_ge(*v_got.now(b))
                head_means(pb, v_raw).then_inc(v_mean.sem, 1)
                pe.wait_ge(*v_sqd.now(b))
                head_means(pc, v_sq).then_inc(v_var.sem, 1)
                pe.wait_ge(*xc_got.now(b))
                pe.wait_ge(*q_floor.now(b))
                linear(pd, W_I, lambda c: xc[:, c, :]).then_inc(ig_lin.sem, 1)
                pe.wait_ge(*k_floor.now(b))
                linear(pa, W_GAM, lambda c: xc[:, c, :]).then_inc(gam_lin.sem, 1)
                pe.wait_ge(*v_cent.now(b))
                linear(pb, W_OG, lambda c: xc[:, c, :]).then_inc(og_lin.sem, 1)
                pe.wait_ge(*scanned.now(b))
                pe.wait_ge(*v_log.now(b))
                head_means(pc, mem).then_inc(mem_mean.sem, 1)
                pe.wait_ge(*mem_sqd.now(b))
                pe.wait_ge(*ig_got.now(b))
                head_means(pd, mem_sq).then_inc(mem_var.sem, 1)
                pe.wait_ge(*mem_q.now(b))
                pe.wait_ge(*gam_got.now(b))
                head_means(pa, out).then_inc(out_mean.sem, 1)
                pe.wait_ge(*out_sqd.now(b))
                pe.wait_ge(*og_got.now(b))
                head_means(pb, out_sq).then_inc(out_var.sem, 1)
                pe.wait_ge(*gated.now(b))
                linear(pc, W_O, lambda c: out[:, c, :]).then_inc(o_lin.sem, 1)

        @block.scalar
        def _(act):
            for x in act_made:
                x.prime(act)
            with act.Fori(0, B) as b:
                act.wait_ge(*q_lin.now(b))
                nc.scalar.activation(q_sq[:], pa[:], ACT.Square).then_inc(q_sqd.sem, 1)
                nc.scalar.activation(q_raw[:], pa[:], ACT.Copy).then_inc(q_got.sem, 1)
                act.wait_ge(*k_lin.now(b))
                nc.scalar.activation(k_sq[:], pb[:], ACT.Square).then_inc(k_sqd.sem, 1)
                nc.scalar.activation(k_raw[:], pb[:], ACT.Copy).then_inc(k_got.sem, 1)
                act.wait_ge(*v_lin.now(b))
                nc.scalar.activation(v_raw[:], pc[:], ACT.Copy).then_inc(v_got.sem, 1)
                act.wait_ge(*conv_step.now(b))
                nc.scalar.activation(xc[:], conv[:], ACT.Silu).then_inc(xc_got.sem, 1)
                act.wait_ge(*v_cent.now(b))
                nc.scalar.activation(v_sq[:], v[:], ACT.Square).then_inc(v_sqd.sem, 1)
                for lin, dst, bias, got in ((ig_lin, ig, V_IB, ig_got), (gam_lin, gam, V_GB, gam_got), (og_lin, og, V_OB, og_got)):
                    src = {V_IB: pd, V_GB: pa, V_OB: pb}[bias]
                    act.wait_ge(*lin.now(b))
                    for h in range(KC):
                        a = nc.scalar.activation(dst[:, h, :], src[:, h, :], ACT.Sigmoid, bias=col(bias, h))
                    a.then_inc(got.sem, 1)
                for floored, log, rs, logged, rsd in ((q_floor, q_rs, q_rs, q_log, q_rsd), (k_floor, k_rs, k_rs, k_log, k_rsd)):
                    act.wait_ge(*floored.now(b))
                    nc.scalar.activation(log[:], log[:], ACT.Ln, scale=2.0 ** 40 * D0, bias=zero).then_inc(logged.sem, 1)
                    act.wait_ge(*logged.now(b))
                    nc.scalar.activation(rs[:], log[:], ACT.Exp, scale=-0.5, bias=floor_back).then_inc(rsd.sem, 1)
                act.wait_ge(*v_var.now(b))
                nc.scalar.activation(v_rs[:], pc[:], ACT.Ln, bias=eps5).then_inc(v_log.sem, 1)
                act.wait_ge(*v_log.now(b))
                nc.scalar.activation(v_rs[:], v_rs[:], ACT.Exp, scale=-0.5).then_inc(v_rsd.sem, 1)
                for cent, body, sq, sqd, var, src, rs, logged, rsd in (
                        (mem_cent, mem, mem_sq, mem_sqd, mem_var, pd, mem_rs, mem_log, mem_rsd),
                        (out_cent, out, out_sq, out_sqd, out_var, pb, out_rs, out_log, out_rsd)):
                    act.wait_ge(*cent.now(b))
                    nc.scalar.activation(sq[:], body[:], ACT.Square).then_inc(sqd.sem, 1)
                    act.wait_ge(*var.now(b))
                    nc.scalar.activation(rs[:], src[:], ACT.Ln, bias=eps5).then_inc(logged.sem, 1)
                    act.wait_ge(*logged.now(b))
                    nc.scalar.activation(rs[:], rs[:], ACT.Exp, scale=-0.5).then_inc(rsd.sem, 1)

        @block.vector
        def _(dve):
            for x in dve_made + [conv_step]:
                x.prime(dve)

            def affine(dst, src, g, bias, sem):
                for h in range(KC):
                    v_ = nc.vector.tensor_scalar(dst[:, h, :], src[:, h, :], col(g, h), col(bias, h), ALU.mult, ALU.add)
                v_.then_inc(sem, 1)

            with dve.Fori(0, B) as b:
                dve.wait_ge(*added.last(b))
                for h in range(KC):
                    c_ = nc.vector.tensor_scalar(conv[:, h, :], XN[:, h, bass.ds(b * T, T)], col(V_TAP3, h), col(V_CONVB, h), ALU.mult, ALU.add)
                c_.then_inc(conv_step.sem, 1)
                for s in range(1, KTAPS):
                    dve.wait_ge(*conv_step.now(b, s))
                    for h in range(KC):
                        c_ = nc.vector.scalar_tensor_tensor(conv[:, h, s:T], XN[:, h, bass.ds(b * T, T - s)], col(V_TAP3 - s, h), conv[:, h, s:T], ALU.mult, ALU.add)
                    c_.then_inc(conv_step.sem, 1)
                dve.wait_ge(*q_sum.now(b))
                nc.vector.tensor_scalar(q_rs[:], pd[:], 1e-24 / D0, None, ALU.max).then_inc(q_floor.sem, 1)
                dve.wait_ge(*k_sum.now(b))
                nc.vector.tensor_scalar(k_rs[:], pa[:], 1e-24 / D0, None, ALU.max).then_inc(k_floor.sem, 1)
                dve.wait_ge(*v_mean.now(b))
                dve.wait_ge(*v_got.now(b))
                nc.vector.tensor_tensor(v[:], v_raw[:], pb[:], ALU.subtract).then_inc(v_cent.sem, 1)
                dve.wait_ge(*q_rsd.now(b))
                dve.wait_ge(*q_got.now(b))
                nc.vector.tensor_tensor(q[:], q_raw[:], q_rs[:], ALU.mult).then_inc(q_nrm.sem, 1)
                dve.wait_ge(*k_rsd.now(b))
                dve.wait_ge(*k_got.now(b))
                nc.vector.tensor_tensor(k[:], k_raw[:], k_rs[:], ALU.mult).then_inc(k_nrm.sem, 1)
                dve.wait_ge(*v_rsd.now(b))
                dve.wait_ge(*v_sqd.now(b))
                dve.wait_ge(*v_cent.now(b))
                nc.vector.tensor_tensor(v[:], v[:], v_rs[:], ALU.mult).then_inc(v_nrm.sem, 1)
                dve.wait_ge(*v_nrm.now(b))
                affine(v, v, V_VG, V_VB, v_aff.sem)
                dve.wait_ge(*v_aff.now(b))
                dve.wait_ge(*k_nrm.now(b))
                nc.vector.tensor_tensor(k[:], k[:], v[:], ALU.mult).then_inc(kv.sem, 1)
                dve.wait_ge(*kv.now(b))
                dve.wait_ge(*ig_got.now(b))
                nc.vector.tensor_tensor(ig[:], ig[:], k[:], ALU.mult).then_inc(ikv.sem, 1)
                dve.wait_ge(*ikv.now(b))
                dve.wait_ge(*gam_got.now(b))
                for h in range(KC):
                    s_ = nc.vector.tensor_tensor_scan(mem[:, h, :], gam[:, h, :], ig[:, h, :], 0.0, ALU.mult, ALU.add)
                s_.then_inc(scanned.sem, 1)
                dve.wait_ge(*mem_mean.now(b))
                dve.wait_ge(*scanned.now(b))
                nc.vector.tensor_tensor(mem[:], mem[:], pc[:], ALU.subtract).then_inc(mem_cent.sem, 1)
                dve.wait_ge(*mem_rsd.now(b))
                dve.wait_ge(*mem_cent.now(b))
                nc.vector.tensor_tensor(mem[:], mem[:], mem_rs[:], ALU.mult).then_inc(mem_nrm.sem, 1)
                dve.wait_ge(*mem_nrm.now(b))
                affine(mem, mem, V_MG, V_MB, mem_aff.sem)
                dve.wait_ge(*mem_aff.now(b))
                dve.wait_ge(*q_nrm.now(b))
                nc.vector.tensor_tensor(out[:], mem[:], q[:], ALU.mult).then_inc(mem_q.sem, 1)
                dve.wait_ge(*out_mean.now(b))
                dve.wait_ge(*mem_q.now(b))
                nc.vector.tensor_tensor(out[:], out[:], pa[:], ALU.subtract).then_inc(out_cent.sem, 1)
                dve.wait_ge(*out_rsd.now(b))
                dve.wait_ge(*out_cent.now(b))
                nc.vector.tensor_tensor(out[:], out[:], out_rs[:], ALU.mult).then_inc(out_nrm.sem, 1)
                dve.wait_ge(*out_nrm.now(b))
                affine(out, out, V_GG, V_GNB, out_aff.sem)
                dve.wait_ge(*out_aff.now(b))
                dve.wait_ge(*og_got.now(b))
                nc.vector.tensor_tensor(out[:], out[:], og[:], ALU.mult).then_inc(gated.sem, 1)
                dve.wait_ge(*o_lin.now(b))
                nc.vector.tensor_tensor(X[:, :, bass.ds(b * T, T)], X[:, :, bass.ds(b * T, T)], pc[:], ALU.add).then_inc(added.sem, 1)


def attention_stage(nc, K, HID, XN, weights_dram):
    QT = T // P
    UNITS = 2 * B
    TURNS = HEADS // 2
    with ExitStack() as ctx:
        signals = ctx.enter_context(Signals(nc))
        def sb(n, shape):
            return ctx.enter_context(nc.sbuf_tensor("att_" + n, shape, F32))

        def pb(n):
            return ctx.enter_context(nc.psum_tensor("att_" + n, [P, TILE], F32))

        def tally(n, per):
            return Tally(signals("att_" + n), per)

        w = [sb(f"w{s}", [P, ATTN_W]) for s in range(2)]
        w_qkv = [x[:, 0:3 * KC * P].rearrange("p (m c n) -> p m c n", m=3, c=KC) for x in w]
        w_o = [x[:, 3 * KC * P:ATTN_W] for x in w]
        q, k = (sb(n, [P, 2, T]) for n in ("q", "k"))
        v = sb("v", [P, 3, QT, VD])
        prob = sb("prob", [P, 2, T])
        probT = sb("probT", [P, 2, QT, T])
        negmax, total, inv = (sb(n, [P, 2, QT]) for n in ("negmax", "total", "inv"))
        o = sb("o", [P, 2, T])
        ps_lin, ps_s, ps_t = ([pb(f"{n}{i}") for i in range(2)] for n in ("lin", "s", "t"))
        ps_pv, ps_o = pb("pv"), pb("o_ps")
        lin, got = tally("lin", 3 * UNITS), tally("got", 3 * UNITS)
        scored, masked, maxed, expd, normed = (tally(n, QT * UNITS) for n in ("scored", "masked", "maxed", "expd", "normed"))
        inverted, turned, spread = (tally(n, QT * UNITS) for n in ("inverted", "turned", "spread"))
        pv_done, o_got = tally("pv_done", UNITS), tally("o_got", UNITS)
        o_lin, added = tally("o_lin", KC * UNITS), tally("added", KC * UNITS)
        w_in = [tally(f"w_in{s}", 16) for s in range(2)]
        block = ctx.enter_context(nc.Block())
        causal, eye = K.mats[:, CAUSAL_OUT, :], K.mats[:, EYE, :]

        @block.sync
        def _(sp):
            for x in w_in:
                x.prime(sp)
            with sp.Fori(0, TURNS) as t:
                for s in range(2):
                    sp.wait_ge(*o_lin.last(t, KC * B * (s + 1)))
                    sp.dma_start(w[s][:], weights_dram[bass.ds(t * 2 + s, 1), :, :].rearrange("o p n -> p (o n)")).then_inc(w_in[s].sem, 16)

        @block.tensor
        def _(pe):
            for x in (lin, scored, turned, pv_done, o_lin):
                x.prime(pe)
            with pe.Fori(0, TURNS) as t:
                def project(u, m):
                    n, b = 3 * u + m, u % B
                    wm = w_qkv[u // B]
                    if u % B == 0 and m == 0:
                        pe.wait_ge(*w_in[u // B].now(t))
                    if n >= 2:
                        pe.wait_ge(*got.now(t, n - 1))
                    else:
                        pe.wait_ge(*got.last(t, 3 * UNITS - 1 + n))
                    out = ps_lin[n % 2]
                    if m < 2:
                        for c in range(KC):
                            mm = nc.tensor.matmul(out[:], wm[:, m, c, :], XN[:, c, b * T:(b + 1) * T], start=c == 0, stop=c == KC - 1)
                    else:
                        for j in range(QT):
                            for c in range(KC):
                                mm = nc.tensor.matmul(out[:, j * VD:(j + 1) * VD], XN[:, c, b * T + j * P:b * T + (j + 1) * P], wm[:, m, c, :],
                                                      start=c == 0, stop=c == KC - 1)
                    mm.then_inc(lin.sem, 1)

                def score(u, i):
                    n = QT * u + i
                    if i == 0:
                        pe.wait_ge(*got.now(t, 3 * u + 2))
                    if n >= 2:
                        pe.wait_ge(*expd.now(t, n - 1))
                    else:
                        pe.wait_ge(*expd.last(t, QT * UNITS - 1 + n))
                    nc.tensor.matmul(ps_s[n % 2][:, 0:(i + 1) * P], q[:, u % 2, i * P:(i + 1) * P], k[:, u % 2, 0:(i + 1) * P],
                                     start=True, stop=True).then_inc(scored.sem, 1)

                def turn(u, i):
                    n = QT * u + i
                    pe.wait_ge(*normed.now(t, n + 1))
                    if n >= 2:
                        pe.wait_ge(*spread.now(t, n - 1))
                    else:
                        pe.wait_ge(*spread.last(t, QT * UNITS - 1 + n))
                    for j in range(i + 1):
                        mm = nc.tensor.transpose(ps_t[n % 2][:, j * P:(j + 1) * P], prob[:, n % 2, j * P:(j + 1) * P], eye)
                    mm.then_inc(turned.sem, 1)

                def values(u):
                    pe.wait_ge(*got.now(t, 3 * u + 3))
                    pe.wait_ge(*spread.now(t, QT * (u + 1)))
                    if u >= 1:
                        pe.wait_ge(*o_got.now(t, u))
                    else:
                        pe.wait_ge(*o_got.last(t, UNITS))
                    for j in range(QT):
                        mm = nc.tensor.matmul(ps_pv[:, j * P:T], v[:, u % 3, j, :], probT[:, u % 2, j, j * P:T], start=j == 0, stop=j == QT - 1)
                    mm.then_inc(pv_done.sem, 1)

                def output(u):
                    pe.wait_ge(*o_got.now(t, u + 1))
                    for c in range(KC):
                        n = KC * u + c
                        if n >= 1:
                            pe.wait_ge(*added.now(t, n))
                        else:
                            pe.wait_ge(*added.last(t, KC * UNITS))
                        nc.tensor.matmul(ps_o[:], w_o[u // B][:, c * P:(c + 1) * P], o[:, u % 2, :], start=True, stop=True).then_inc(o_lin.sem, 1)

                for m in range(3):
                    project(0, m)
                for u in range(UNITS):
                    more = u + 1 < UNITS
                    score(u, 0)
                    score(u, 1)
                    if more:
                        project(u + 1, 0)
                    turn(u, 0)
                    score(u, 2)
                    if u >= 1:
                        values(u - 1)
                    turn(u, 1)
                    score(u, 3)
                    if more:
                        project(u + 1, 1)
                    turn(u, 2)
                    if u >= 1:
                        output(u - 1)
                    if more:
                        project(u + 1, 2)
                    turn(u, 3)
                values(UNITS - 1)
                output(UNITS - 1)

        @block.scalar
        def _(act):
            for x in (got, expd, o_got):
                x.prime(act)
            with act.Fori(0, TURNS) as t:
                def take(u, m):
                    n = 3 * u + m
                    act.wait_ge(*lin.now(t, n + 1))
                    src = ps_lin[n % 2]
                    if m == 0:
                        act.wait_ge(*(scored.now(t, QT * (u - 1)) if u >= 2 else scored.last(t, QT * (UNITS - 1 + u))))
                        a = nc.scalar.activation(q[:, u % 2, :], src[:], ACT.Copy, scale=ATTN_SCALE)
                    elif m == 1:
                        a = nc.scalar.activation(k[:, u % 2, :], src[:], ACT.Copy)
                    else:
                        act.wait_ge(*(pv_done.now(t, u - 2) if u >= 3 else pv_done.last(t, UNITS)))
                        a = nc.scalar.activation(v[:, u % 3, :, :].rearrange("p j n -> p (j n)"), src[:], ACT.Copy)
                    a.then_inc(got.sem, 1)

                def exponent(u, i):
                    n = QT * u + i
                    act.wait_ge(*maxed.now(t, n + 1))
                    if n >= 2:
                        act.wait_ge(*turned.now(t, n - 1))
                        act.wait_ge(*inverted.now(t, n - 1))
                    else:
                        act.wait_ge(*turned.last(t, QT * UNITS - 1 + n))
                        act.wait_ge(*inverted.last(t, QT * UNITS - 1 + n))
                    nc.scalar.activation(prob[:, n % 2, 0:(i + 1) * P], ps_s[n % 2][:, 0:(i + 1) * P], ACT.Exp, bias=negmax[:, u % 2, i:i + 1],
                                         accum_out=total[:, u % 2, i:i + 1]).then_inc(expd.sem, 1)

                def out(u):
                    act.wait_ge(*pv_done.now(t, u + 1))
                    act.wait_ge(*(o_lin.now(t, KC * (u - 1)) if u >= 2 else o_lin.last(t, KC * (UNITS - 1 + u))))
                    nc.scalar.activation(o[:, u % 2, :], ps_pv[:], ACT.Copy).then_inc(o_got.sem, 1)

                for m in range(3):
                    take(0, m)
                for u in range(UNITS):
                    more = u + 1 < UNITS
                    exponent(u, 0)
                    exponent(u, 1)
                    if more:
                        take(u + 1, 0)
                    if u >= 1:
                        out(u - 1)
                    exponent(u, 2)
                    exponent(u, 3)
                    if more:
                        take(u + 1, 1)
                        take(u + 1, 2)
                out(UNITS - 1)

        @block.gpsimd
        def _(pool):
            normed.prime(pool)
            with pool.Fori(0, TURNS) as t:
                for n in range(QT * UNITS):
                    u, i = n // QT, n % QT
                    pool.wait_ge(*inverted.now(t, n + 1))
                    part = prob[:, n % 2, 0:(i + 1) * P]
                    nc.gpsimd.tensor_tensor(part, part, inv[:, u % 2, i:i + 1].broadcast_to([P, (i + 1) * P]), ALU.mult).then_inc(normed.sem, 1)

        @block.vector
        def _(dve):
            for x in (masked, maxed, inverted, spread, added):
                x.prime(dve)
            with dve.Fori(0, TURNS) as t:
                def most(u, i):
                    n = QT * u + i
                    dve.wait_ge(*scored.now(t, n + 1))
                    diag = ps_s[n % 2][:, i * P:(i + 1) * P]
                    nc.vector.tensor_tensor(diag, diag, causal, ALU.add).then_inc(masked.sem, 1)
                    dve.wait_ge(*masked.now(t, n + 1))
                    nc.vector.tensor_reduce(negmax[:, u % 2, i:i + 1], ps_s[n % 2][:, 0:(i + 1) * P], AXX, ALU.max, negate=True).then_inc(maxed.sem, 1)

                def invert(u, i):
                    n = QT * u + i
                    dve.wait_ge(*expd.now(t, n + 1))
                    dve.wait_ge(*(normed.now(t, n - 2 * QT + 1) if n >= 2 * QT else normed.last(t, QT * UNITS - 2 * QT + 1 + n)))
                    nc.vector.reciprocal(inv[:, u % 2, i:i + 1], total[:, u % 2, i:i + 1]).then_inc(inverted.sem, 1)

                def keep(u, i):
                    n = QT * u + i
                    dve.wait_ge(*turned.now(t, n + 1))
                    if i == 0:
                        dve.wait_ge(*(pv_done.now(t, u - 1) if u >= 2 else pv_done.last(t, UNITS - 1 + u)))
                    nc.vector.tensor_copy(probT[:, u % 2, 0:i + 1, i * P:(i + 1) * P],
                                          ps_t[n % 2][:, 0:(i + 1) * P].rearrange("p (j q) -> p j q", q=P)).then_inc(spread.sem, 1)

                def add(u):
                    b = u % B
                    for c in range(KC):
                        dve.wait_ge(*o_lin.now(t, KC * u + c + 1))
                        part = HID[:, c, b * T:(b + 1) * T]
                        dve.wait_ge(*(added.now(t, KC * (u - B) + c + 1) if u >= B else added.last(t, KC * (u + B) + c + 1)))
                        nc.vector.tensor_tensor(part, part, ps_o[:], ALU.add).then_inc(added.sem, 1)

                for u in range(UNITS):
                    most(u, 0)
                    most(u, 1)
                    invert(u, 0)
                    invert(u, 1)
                    keep(u, 0)
                    most(u, 2)
                    invert(u, 2)
                    keep(u, 1)
                    most(u, 3)
                    invert(u, 3)
                    keep(u, 2)
                    if u >= 1:
                        add(u - 1)
                    keep(u, 3)
                add(UNITS - 1)


def swiglu_stage(nc, name, K, X, XN, blocks, up_dram, down_dram, HID=None, gate_dram=None, expert_dram=None, before_dram=None):
    LOADS = 5
    TT = N // P
    with ExitStack() as ctx:
        signals = ctx.enter_context(Signals(nc))
        def sb(n, shape):
            return ctx.enter_context(nc.sbuf_tensor(f"{name}_{n}", shape, F32))

        def sem(n):
            return signals(f"{name}_{n}")

        def tally(n, per):
            return Tally(sem(n), per)

        up = sb("up", [P, blocks, KC, 2, P])
        down = sb("down", [P, blocks, C])
        silu, hid = sb("silu", [P, 2, TILE]), sb("hid", [P, 2, TILE])
        ps_g, ps_u, ps_w, ps_out = ([ctx.enter_context(nc.psum_tensor(f"{name}_{n}{i}", [P, TILE], F32)) for i in range(2)] for n in "guwo")
        edges = [blocks * i // LOADS for i in range(LOADS + 1)]
        loads = [sem(f"load{i}") for i in range(LOADS)]
        gate_lin, up_lin, weigh_lin, silud, made = (tally(n, blocks) for n in ("gate_lin", "up_lin", "weigh_lin", "silud", "made"))
        weighed, used = tally("weighed", blocks), tally("used", blocks)
        added = tally("added", KC)
        if HID is not None:
            added_hid = tally("added_hid", KC)
            gate_w = sb("gate_w", [P, KC, E])
            expert_of = sb("expert_of", [SELROWS, blocks, P])
            earlier = sb("earlier", [P, E, E])
            logit, expo, weight = (sb(n, [P, TT, E]) for n in ("logit", "expo", "weight"))
            greater, equal = (sb(n, [P, TT, E, E]) for n in ("greater", "equal"))
            rank = sb("rank", [P, TT, E])
            top, total, inv = (sb(n, [P, TT]) for n in ("top", "total", "inv"))
            route = sb("route", [P, TT, SELROWS])
            routeT = sb("routeT", [SELROWS, N])
            router_in, logits, exps, routed, routeT_ready = (sem(n) for n in ("router_in", "logits", "exps", "routed", "routeT_ready"))
            chain = sem("chain")
        block = ctx.enter_context(nc.Block())

        @block.sync
        def _(sp):
            if HID is not None:
                sp.dma_start(gate_w[:], gate_dram[:]).then_inc(router_in, 16)
                sp.dma_start(expert_of[:], expert_dram[:]).then_inc(router_in, 16)
                sp.dma_start(earlier[:], before_dram[:]).then_inc(router_in, 16)
            for i in range(LOADS):
                a, z = edges[i], edges[i + 1]
                sp.dma_start(up[:, a:z], up_dram[:, a:z]).then_inc(loads[i], 16)
                sp.dma_start(down[:, a:z], down_dram[:, a:z]).then_inc(loads[i], 16)

        @block.tensor
        def _(pe):
            for x in (gate_lin, up_lin, weigh_lin, used):
                x.prime(pe)
            if HID is not None:
                pe.wait_ge(router_in, 48)
                for t in range(TT):
                    for c in range(KC):
                        mm = nc.tensor.matmul(ps_w[0][:, t * E:(t + 1) * E], XN[:, c, t * P:(t + 1) * P], gate_w[:, c, :], start=c == 0, stop=c == KC - 1)
                mm.then_inc(logits, 1)
                pe.wait_ge(routed, 1)
                for g in range(NT):
                    out = (ps_w[1], ps_g[0], ps_g[1], ps_u[0])[g]
                    for t in range(TILE // P):
                        mm = nc.tensor.transpose(out[0:SELROWS, t * P:(t + 1) * P], route[:, g * (TILE // P) + t, :], K.mats[:, EYE, :])
                    mm.then_inc(logits, 1)
                pe.wait_ge(routeT_ready, NT)
            for i in range(LOADS):
                pe.wait_ge(loads[i], 32)
            with pe.Fori(0, NT) as t:
                def free(tl, j):
                    pe.wait_ge(*(tl.now(t, j - 1) if j >= 2 else tl.last(t, blocks - 1 + j)))

                def open_(j):
                    free(silud, j)
                    for c in range(KC):
                        mm = nc.tensor.matmul(ps_g[j % 2][:], up[:, j, c, 0, :], XN[:, c, bass.ds(t * TILE, TILE)], start=c == 0, stop=c == KC - 1)
                    mm.then_inc(gate_lin.sem, 1)
                    free(made if HID is None else weighed, j)
                    for c in range(KC):
                        mm = nc.tensor.matmul(ps_u[j % 2][:], up[:, j, c, 1, :], XN[:, c, bass.ds(t * TILE, TILE)], start=c == 0, stop=c == KC - 1)
                    mm.then_inc(up_lin.sem, 1)
                    if HID is not None:
                        nc.tensor.matmul(ps_w[j % 2][:], expert_of[:, j, :], routeT[:, bass.ds(t * TILE, TILE)], start=True, stop=True).then_inc(weigh_lin.sem, 1)

                def close(j):
                    pe.wait_ge(*(weighed if HID is not None else made).now(t, j + 1))
                    if j == 0:
                        pe.wait_ge(*added.last(t))
                    for m in range(KC):
                        mm = nc.tensor.matmul(ps_out[m][:], down[:, j, m * P:(m + 1) * P], hid[:, j % 2, :], start=j == 0, stop=j == blocks - 1)
                    mm.then_inc(used.sem, 1)

                open_(0)
                for j in range(1, blocks):
                    open_(j)
                    close(j - 1)
                close(blocks - 1)

        @block.scalar
        def _(act):
            silud.prime(act)
            if HID is not None:
                act.wait_ge(chain, 2)
                nc.scalar.activation(expo[:], expo[:], ACT.Exp).then_inc(exps, 1)
                for g in range(NT):
                    act.wait_ge(logits, 2 + g)
                    src = (ps_w[1], ps_g[0], ps_g[1], ps_u[0])[g]
                    nc.scalar.activation(routeT[:, g * TILE:(g + 1) * TILE], src[0:SELROWS, :], ACT.Copy).then_inc(routeT_ready, 1)
            with act.Fori(0, NT) as t:
                for j in range(blocks):
                    act.wait_ge(*gate_lin.now(t, j + 1))
                    act.wait_ge(*(made.now(t, j - 1) if j >= 2 else made.last(t, blocks - 1 + j)))
                    nc.scalar.activation(silu[:, j % 2, :], ps_g[j % 2][:], ACT.Silu).then_inc(silud.sem, 1)

        @block.vector
        def _(dve):
            for x in [made, weighed, added] + ([added_hid] if HID is not None else []):
                x.prime(dve)
            if HID is not None:
                steps = [0]

                def link(ins):
                    steps[0] += 1
                    ins.then_inc(chain, 1)
                    dve.wait_ge(chain, steps[0])

                dve.wait_ge(logits, 1)
                dve.wait_ge(router_in, 48)
                all_logits = ps_w[0][:, 0:TT * E].rearrange("p (t e) -> p t e", e=E)
                link(nc.vector.tensor_reduce(top[:], all_logits, AXX, ALU.max))
                link(nc.vector.tensor_tensor(expo[:], all_logits, bcast(top[:], 2, E), ALU.subtract))
                link(nc.vector.tensor_copy(logit[:], all_logits))
                other, own = bcast(logit[:], 2, E), bcast(logit[:], 3, E)
                nc.vector.tensor_tensor(greater[:], other, own, ALU.is_gt)
                link(nc.vector.tensor_tensor(equal[:], other, own, ALU.is_equal))
                link(nc.vector.tensor_tensor(equal[:], equal[:], bcast(earlier[:], 1, TT), ALU.mult))
                link(nc.vector.tensor_tensor(greater[:], greater[:], equal[:], ALU.add))
                link(nc.vector.tensor_reduce(rank[:], greater[:], AXX, ALU.add))
                dve.wait_ge(exps, 1)
                link(nc.vector.scalar_tensor_tensor(weight[:], rank[:], float(TOPK) - 0.5, expo[:], ALU.is_lt, ALU.mult))
                link(nc.vector.tensor_reduce(total[:], weight[:], AXX, ALU.add))
                link(nc.vector.reciprocal(inv[:], total[:]))
                link(nc.vector.memset(route[:, :, E:SELROWS], 1.0))
                nc.vector.tensor_tensor(route[:, :, 0:E], weight[:], bcast(inv[:], 2, E), ALU.mult).then_inc(routed, 1)
            with dve.Fori(0, NT) as t:
                for j in range(blocks):
                    dve.wait_ge(*up_lin.now(t, j + 1))
                    dve.wait_ge(*silud.now(t, j + 1))
                    dve.wait_ge(*(used.now(t, j - 1) if j >= 2 else used.last(t, blocks - 1 + j)))
                    nc.vector.tensor_tensor(hid[:, j % 2, :], silu[:, j % 2, :], ps_u[j % 2][:], ALU.mult).then_inc(made.sem, 1)
                    if HID is not None:
                        dve.wait_ge(*weigh_lin.now(t, j + 1))
                        dve.wait_ge(*made.now(t, j + 1))
                        nc.vector.tensor_tensor(hid[:, j % 2, :], hid[:, j % 2, :], ps_w[j % 2][:], ALU.mult).then_inc(weighed.sem, 1)
                dve.wait_ge(*used.now(t))
                for m in range(KC):
                    part = X[:, m, bass.ds(t * TILE, TILE)]
                    nc.vector.tensor_tensor(part, part, ps_out[m][:], ALU.add).then_inc(added.sem, 1)
                if HID is not None:
                    for m in range(KC):
                        part = X[:, m, bass.ds(t * TILE, TILE)]
                        dve.wait_ge(*added.now(t, m + 1))
                        nc.vector.tensor_tensor(part, part, HID[:, m, bass.ds(t * TILE, TILE)], ALU.add).then_inc(added_hid.sem, 1)

def delta_inputs_stage(nc, K, XN, F1, f1_dram, b_dram, beta_dram):
    with ExitStack() as ctx:
        signals = ctx.enter_context(Signals(nc))
        w_f1 = ctx.enter_context(nc.sbuf_tensor("dp_w_f1", [P, KC, P], F32))
        w_b = ctx.enter_context(nc.sbuf_tensor("dp_w_b", [P, KC, HEADS], F32))
        beta = ctx.enter_context(nc.sbuf_tensor("dp_beta", [HEADS, N], F32))
        ps_f = [ctx.enter_context(nc.psum_tensor(f"dp_f{t}", [P, TILE], F32)) for t in range(NT)]
        ps_b = [ctx.enter_context(nc.psum_tensor(f"dp_b{t}", [P, TILE], F32)) for t in range(NT)]
        w_in, lin, f1_got, beta_got, stored = (signals("dp_" + n) for n in ("w_in", "lin", "f1_got", "beta_got", "stored"))
        block = ctx.enter_context(nc.Block())

        @block.sync
        def _(sp):
            sp.dma_start(w_f1[:], f1_dram[:]).then_inc(w_in, 16)
            sp.dma_start(w_b[:], b_dram[:]).then_inc(w_in, 16)
            sp.wait_ge(beta_got, NT)
            sp.dma_start(beta_dram[0:HEADS, :], beta[:]).then_inc(stored, 16)
            sp.dma_start(beta_dram[HEADS:HEADS + 1, :], beta[0:1, :]).then_inc(stored, 16)
            sp.wait_ge(stored, 32)

        @block.tensor
        def _(pe):
            pe.wait_ge(w_in, 32)
            for t in range(NT):
                for c in range(KC):
                    mm = nc.tensor.matmul(ps_b[t][0:HEADS, :], w_b[:, c, :], XN[:, c, t * TILE:(t + 1) * TILE], start=c == 0, stop=c == KC - 1)
                mm.then_inc(lin, 1)
            for t in range(NT):
                for c in range(KC):
                    mm = nc.tensor.matmul(ps_f[t][:], w_f1[:, c, :], XN[:, c, t * TILE:(t + 1) * TILE], start=c == 0, stop=c == KC - 1)
                mm.then_inc(lin, 1)

        @block.scalar
        def _(act):
            for t in range(NT):
                act.wait_ge(lin, t + 1)
                nc.scalar.activation(beta[:, t * TILE:(t + 1) * TILE], ps_b[t][0:HEADS, :], ACT.Sigmoid).then_inc(beta_got, 1)
            for t in range(NT):
                act.wait_ge(lin, NT + t + 1)
                nc.scalar.activation(F1[:, t * TILE:(t + 1) * TILE], ps_f[t][:], ACT.Copy).then_inc(f1_got, 1)


class PairTally:

    def __init__(self, sem, per):
        self.sem, self.per = sem, per

    def prime(self, eng):
        eng.sem_inc(self.sem, 2 * self.per)

    def at(self, head, off, n=None):
        return self.sem, head * (2 * self.per) + ((off + 2) * self.per + (self.per if n is None else n))


def delta_stage(nc, K, X, XN, dram):
    PB = B // 2
    PT = PB * T
    G = PB * NC_
    HALF = CH // 2
    STEPS = LEVELS + 2
    (Q0, K0, V0, GT0, G0, QS0, KS0, VT0) = range(0, 16, 2)
    with ExitStack() as ctx:
        signals = ctx.enter_context(Signals(nc))
        def sb(n, shape):
            return ctx.enter_context(nc.sbuf_tensor("dl_" + n, shape, F32))

        def pb(n):
            return ctx.enter_context(nc.psum_tensor("dl_" + n, [P, TILE], F32))

        F1 = sb("F1", [P, N])
        beta_dram = nc.dram_tensor("beta_rows", [HEADS + 1, N], F32, kind="Internal").ap()
        delta_inputs_stage(nc, K, XN, F1, dram["delta_f1"], dram["delta_b"], beta_dram)

        all_tallies = {}

        def tallies(engine, **per):
            made = {n: PairTally(signals("dl_" + n), c) for n, c in per.items()}
            all_tallies.setdefault(engine, []).extend(made.values())
            return made.values()

        w_p = sb("w_p", [P, 4, KC, P])
        w_f2 = sb("w_f2", [P, P])
        w_c = sb("w_c", [P, H_COLS])
        w_o = sb("w_o", [P, C])
        beta = sb("beta", [P, N])
        level_mask = sb("level_mask", [P, LEVELS, HALF])
        raw = sb("raw", [P, 3, T])
        kq = [sb(f"kq{p}", [P, 2, PT]) for p in range(2)]
        ks = [sb(f"ks{p}", [P, PT]) for p in range(2)]
        dec = [[sb(f"dec{p}_{l}", [P, PT >> l]) for l in range(LEVELS + 1)] for p in range(2)]
        vc = sb("vc", [P, PT])
        vtok = [sb(f"vtok{p}", [P, G, P]) for p in range(2)]
        gate = [sb(f"gate{p}", [P, PT]) for p in range(2)]
        sq, rs = sb("sq", [P, 2, T]), sb("rs", [P, 4, T])
        soft, softln, relu, less = (sb(n, [P, PB, T]) for n in ("soft", "softln", "relu", "less"))
        nega = sb("nega", [P, 2])
        mt = [sb(f"mt{i}", [P, G, CH]) for i in range(2)]
        z, tm = sb("z", [P, G, CH]), sb("tm", [P, G, CH])
        tt = [sb(f"tt{p}", [P, G, CH]) for p in range(2)]
        bt = [sb(f"bt{p}", [P, G, CH]) for p in range(2)]
        kst = sb("kst", [P, G, P])
        r, u, state = (sb(n, [P, PB, P]) for n in ("r", "u", "state"))
        o = sb("o", [P, PB, T])
        osq, ors = sb("osq", [P, PB, T]), sb("ors", [P, PB, T])
        bank_a, bank_k, bank_t, bank_c = ([pb(f"{n}{i}") for i in range(2)] for n in "aktc")

        a_lin, b_kk, b_zl, b_tl, c_kt, c_rl, c_ul, c_ol, c_sl, c_nl, c_wl = tallies(
            "pe", a_lin=16, b_kk=2 * (LEVELS + 1), b_zl=2 * LEVELS, b_tl=2 * LEVELS, c_kt=PB, c_rl=NC_ - 1, c_ul=NC_, c_ol=NC_,
            c_sl=NC_ - 1, c_nl=PB, c_wl=PB * KC)
        (a_took, a_silu, a_sq, a_rs, a_abs, a_soft, a_ln, a_nega, a_dec, b_init, b_zed, c_kst, c_u, c_o, c_sq, c_log, c_rs) = tallies(
            "act", a_took=16, a_silu=6, a_sq=4, a_rs=4, a_abs=PB, a_soft=PB, a_ln=PB, a_nega=2, a_dec=PB, b_init=2, b_zed=2 * LEVELS,
            c_kst=PB, c_u=NC_, c_o=NC_, c_sq=PB, c_log=PB, c_rs=PB)
        a_conv, a_less, b_m, b_got, b_tm, b_tt, c_r, c_s, c_nrm, c_add = tallies(
            "dve", a_conv=6 * KTAPS, a_less=PB, b_m=2 * LEVELS, b_got=2 * (LEVELS + 1), b_tm=2 * (LEVELS - 1), b_tt=2 * LEVELS, c_r=NC_ - 1,
            c_s=PB * (NC_ - 1), c_nrm=PB, c_add=PB * KC)
        a_sp, a_nrm, a_nrm_k, a_ks, b_kq, b_ks, b_dec, c_gate = tallies(
            "pool", a_sp=3 * PB, a_nrm=PB, a_nrm_k=PB, a_ks=PB, b_kq=2 * (LEVELS + 1), b_ks=2 * LEVELS, b_dec=2 * LEVELS, c_gate=PB)
        w_in = Tally(signals("dl_w_in"), 64)
        w_o_in = Tally(signals("dl_w_o_in"), 16)
        mask_in = signals("dl_mask_in")
        cleared = signals("dl_cleared")
        block = ctx.enter_context(nc.Block())
        eye, ones, mean = K.mats[:, EYE, :], K.mats[:, ONES, :], K.mats[:, MEAN_P, :]
        zero, eps5, eps6, qscale = (K.small[:, n:n + 1] for n in (ZERO, EPS5, EPS6, QSCALE))

        def tok(b):
            return slice(b * T, (b + 1) * T)

        def chunks(ap, b):
            return ap[:, b * NC_:(b + 1) * NC_]

        def half_cols(ap, b, l, second):
            half = 1 << l
            return chunks(ap, b).rearrange("p g (n two h) -> p g n two h", two=2, h=half)[:, :, :, second, :]

        def half_flat(ap, b, l, second):
            half = 1 << l
            return chunks(ap, b).rearrange("p g (n two h) -> p (g n) two h", two=2, h=half)[:, :, second, :]

        @block.sync
        def _(sp):
            w_in.prime(sp)
            w_o_in.prime(sp)
            w = dram["delta_w"]

            def load_projections(head):
                def row(a, z):
                    return w[bass.ds(head, 1), :, a:z].rearrange("o p n -> p (o n)")
                a, z = 4 * KC * P, 4 * KC * P + P
                sp.dma_start(w_p[:].rearrange("p m c n -> p (m c n)"), row(0, a)).then_inc(w_in.sem, 16)
                sp.dma_start(w_f2[:], row(a, z)).then_inc(w_in.sem, 16)
                sp.dma_start(w_c[:], row(z + C, z + C + H_COLS)).then_inc(w_in.sem, 16)
                sp.dma_start(beta[:], beta_dram[bass.ds(head, 1), :].broadcast_to([P, N])).then_inc(w_in.sem, 16)

            sp.dma_start(level_mask[:], dram["level_mask"][:]).then_inc(mask_in, 16)
            load_projections(0)
            with sp.Fori(0, HEADS) as h:
                sp.wait_ge(*c_wl.at(h, -1))
                sp.dma_start(w_o[:], w[bass.ds(h, 1), :, 4 * KC * P + P:4 * KC * P + P + C].rearrange("o p n -> p (o n)")).then_inc(w_o_in.sem, 16)
                sp.wait_ge(*a_lin.at(h, 1))
                sp.wait_ge(*a_dec.at(h, 1))
                sp.wait_ge(*a_ks.at(h, 1))
                sp.wait_ge(*a_conv.at(h, 1))
                load_projections(h + 1)

        @block.tensor
        def _(pe):
            for x in all_tallies["pe"]:
                x.prime(pe)

            def A(h, off, s, k):
                p = off % 2
                if s == 0 and k == 0 and p == 0:
                    pe.wait_ge(*w_in.now(h + off // 2 if off else h))
                order = [Q0, K0, V0, GT0, G0, QS0, KS0, VT0, None]
                e0 = order[s]
                if e0 is None or k > 1:
                    return
                e, b = e0 + k, k
                gb = p * PB + b
                if e >= 2:
                    pe.wait_ge(*a_took.at(h, off, e - 1))
                else:
                    pe.wait_ge(*a_took.at(h, off - 1, 15 + e))
                out = bank_a[b]
                if e0 in (Q0, K0, V0, GT0):
                    for c in range(KC):
                        mm = nc.tensor.matmul(out[:], w_p[:, e0 // 2, c, :], XN[:, c, gb * T:(gb + 1) * T], start=c == 0, stop=c == KC - 1)
                elif e0 == G0:
                    mm = nc.tensor.matmul(out[:], w_f2[:], F1[:, gb * T:(gb + 1) * T], start=True, stop=True)
                elif e0 in (QS0, KS0):
                    n = e - QS0
                    pe.wait_ge(*a_sq.at(h, off, n + 1))
                    mm = nc.tensor.matmul(out[:], ones, sq[:, n % 2, :], start=True, stop=True)
                else:
                    pe.wait_ge(*a_silu.at(h, off, 5 + b))
                    for c in range(NC_):
                        mm = nc.tensor.transpose(out[:, c * P:(c + 1) * P], vc[:, b * T + c * P:b * T + (c + 1) * P], eye)
                mm.then_inc(a_lin.sem, 1)

            def Bp(h, off, s, k):
                p = off % 2
                if k == 0 and s <= LEVELS:
                    for b in range(PB):
                        n = 2 * s + b
                        if s == 0:
                            pe.wait_ge(*a_ks.at(h, off, b + 1))
                            pe.wait_ge(*a_nrm.at(h, off, b + 1))
                            pe.wait_ge(*b_got.at(h, off - 1, 2 * LEVELS + b + 1))
                        else:
                            pe.wait_ge(*b_kq.at(h, off, n - 1))
                            if s >= 2:
                                pe.wait_ge(*b_ks.at(h, off, n - 3))
                            pe.wait_ge(*b_got.at(h, off, n - 1))
                        for c in range(NC_):
                            at = slice(b * T + c * CH, b * T + (c + 1) * CH)
                            if s == 0:
                                mm = nc.tensor.matmul(bank_k[b][:, c * CH:(c + 1) * CH], ks[p][:, at], kq[p][:, 1, at], start=True, stop=True)
                            else:
                                second = kq[p][:, :, at].rearrange("p m (n two h) -> p m n two h", two=2, h=1 << s - 1)[:, :, :, 1, :]
                                mm = nc.tensor.matmul(bank_k[b][:, c * CH:(c + 1) * CH], ks[p][:, at], second, start=True, stop=True)
                        mm.then_inc(b_kk.sem, 1)
                l = s - 2
                if k == 1 and l >= 0:
                    for b in range(PB):
                        n = 2 * l + b
                        pe.wait_ge(*b_m.at(h, off, n + 1))
                        if l == 0:
                            pe.wait_ge(*b_init.at(h, off))
                            pe.wait_ge(*b_tt.at(h, off - 1, 2 * (LEVELS - 1) + b + 1))
                        else:
                            pe.wait_ge(*b_tt.at(h, off, n - 1))
                            pe.wait_ge(*b_tm.at(h, off, n - 1))
                        firsts = half_cols(tm, b, l, 0)
                        for c in range(NC_):
                            mm = nc.tensor.matmul(bank_t[b][:, c * HALF:(c + 1) * HALF], chunks(mt[l % 2], b)[:, c, :], firsts[:, c], start=True, stop=True)
                        mm.then_inc(b_zl.sem, 1)
                if k == 2 and l >= 0:
                    for b in range(PB):
                        n = 2 * l + b
                        pe.wait_ge(*b_zed.at(h, off, n + 1))
                        zf, ts = half_cols(z, b, l, 0), half_cols(tt[p], b, l, 1)
                        for c in range(NC_):
                            if l < LEVELS - 1:
                                nc.tensor.matmul(bank_t[b][:, c * HALF:(c + 1) * HALF], chunks(tt[p], b)[:, c, :], zf[:, c], start=True, stop=True)
                            mm = nc.tensor.matmul(bank_t[b][:, (NC_ + c) * HALF:(NC_ + c + 1) * HALF], chunks(z, b)[:, c, :], ts[:, c], start=True, stop=True)
                        mm.then_inc(b_tl.sem, 1)

            def Cp(h, off, s, k):
                p = off % 2
                ci = s - 1
                if s == 0 and k < PB:
                    b = k
                    pe.wait_ge(*b_ks.at(h, off, 2 * (LEVELS - 1) + b + 1))
                    pe.wait_ge(*c_add.at(h, off - 1, PB * KC - 1 + b))
                    for c in range(NC_):
                        mm = nc.tensor.transpose(bank_c[b][:, c * P:(c + 1) * P], ks[p][:, b * T + c * P:b * T + (c + 1) * P], eye)
                    mm.then_inc(c_kt.sem, 1)
                if 0 <= ci < NC_:
                    def at(b):
                        return slice(b * T + ci * CH, b * T + (ci + 1) * CH)
                    if k == 0 and ci == 0:
                        pe.wait_ge(*b_kq.at(h, off))
                        pe.wait_ge(*b_tt.at(h, off))
                        pe.wait_ge(*a_took.at(h, off))
                    if k == 0 and ci > 0:
                        pe.wait_ge(*c_s.at(h, off, PB * ci))
                        pe.wait_ge(*c_o.at(h, off, ci))
                        for b in range(PB):
                            mm = nc.tensor.matmul(bank_c[0][:, b * P:(b + 1) * P], kq[p][:, 0, at(b)], state[:, b, :], start=True, stop=True)
                        mm.then_inc(c_rl.sem, 1)
                    if k == 1:
                        if ci > 0:
                            pe.wait_ge(*c_r.at(h, off, ci))
                        else:
                            pe.wait_ge(*c_kst.at(h, off, 2))
                        for b in range(PB):
                            mm = nc.tensor.matmul(bank_c[1][:, b * P:(b + 1) * P], chunks(tt[p], b)[:, ci, :], r[:, b, :] if ci else chunks(vtok[p], b)[:, ci, :],
                                                  start=True, stop=True)
                        mm.then_inc(c_ul.sem, 1)
                    if k == 2:
                        pe.wait_ge(*c_u.at(h, off, ci + 1))
                        if ci == 0:
                            pe.wait_ge(*c_kst.at(h, off, 1))
                        if ci < NC_ - 1:
                            for b in range(PB):
                                mm = nc.tensor.matmul(bank_c[1][:, b * P:(b + 1) * P], chunks(kst, b)[:, ci, :], u[:, b, :], start=True, stop=True)
                            mm.then_inc(c_sl.sem, 1)
                        for b in range(PB):
                            if ci:
                                nc.tensor.matmul(bank_c[0][:, b * P:(b + 1) * P], state[:, b, :], kq[p][:, 1, at(b)], start=True, stop=False)
                            mm = nc.tensor.matmul(bank_c[0][:, b * P:(b + 1) * P], u[:, b, :], chunks(bt[p], b)[:, ci, :], start=ci == 0, stop=True)
                        mm.then_inc(c_ol.sem, 1)
                if s == NC_ + 1 and k < PB:
                    b = k
                    pe.wait_ge(*c_sq.at(h, off, b + 1))
                    nc.tensor.matmul(bank_c[b][:], mean, osq[:, b, :], start=True, stop=True).then_inc(c_nl.sem, 1)
                if s in (NC_ + 2, NC_ + 3) and k < KC:
                    b, m = s - NC_ - 2, k
                    n = b * KC + m
                    pe.wait_ge(*c_gate.at(h, off, b + 1))
                    if n == 0:
                        pe.wait_ge(*w_o_in.now(h))
                    if n < 2:
                        pe.wait_ge(*c_log.at(h, off, n + 1))
                    else:
                        pe.wait_ge(*c_add.at(h, off, n - 1))
                    nc.tensor.matmul(bank_c[m][:], w_o[:, m * P:(m + 1) * P], o[:, b, :], start=True, stop=True).then_inc(c_wl.sem, 1)

            for s in range(STEPS):
                for k in range(3):
                    A(0, 0, s, k)
            with pe.Fori(0, HEADS) as h:
                for s in range(STEPS):
                    for k in range(3):
                        Bp(h, 0, s, k)
                        A(h, 1, s, k)
                for s in range(STEPS):
                    for k in range(3):
                        Bp(h, 1, s, k)
                        Cp(h, 0, s, k)
                for s in range(STEPS):
                    for k in range(3):
                        Cp(h, 1, s, k)
                        A(h, 2, s, k)

        @block.scalar
        def _(act):
            for x in all_tallies["act"]:
                x.prime(act)

            def column(n):
                return w_c[:, n:n + 1]

            def A(h, off, s, k):
                p = off % 2
                b = k
                def take(e):
                    act.wait_ge(*a_lin.at(h, off, e + 1))
                if s == 0 and k == 0 and p == 0:
                    act.wait_ge(*w_in.now(h + off // 2 if off else h))
                if s <= 2 and k < PB:
                    n = 2 * s + b
                    take(n)
                    if n >= 3:
                        act.wait_ge(*a_conv.at(h, off, KTAPS * (n - 2)))
                    else:
                        act.wait_ge(*a_conv.at(h, off - 1, KTAPS * (n + 4)))
                    nc.scalar.activation(raw[:, n % 3, :], bank_a[b][:], ACT.Copy).then_inc(a_took.sem, 1)
                if 1 <= s <= 3 and k < PB:
                    n = 2 * (s - 1) + b
                    act.wait_ge(*a_conv.at(h, off, KTAPS * (n + 1)))
                    y = (kq[p][:, 1, tok(b)], kq[p][:, 0, tok(b)], vc[:, tok(b)])[s - 1]
                    nc.scalar.activation(y, y, ACT.Silu).then_inc(a_silu.sem, 1)
                if s == 3 and k < PB:
                    take(GT0 + b)
                    act.wait_ge(*c_gate.at(h, off - 2, b + 1))
                    nc.scalar.activation(gate[p][:, tok(b)], bank_a[b][:], ACT.Silu, bias=column(H_BG)).then_inc(a_took.sem, 1)
                if s == 4 and k < PB:
                    take(G0 + b)
                    act.wait_ge(*a_dec.at(h, off - 1, b + 1))
                    nc.scalar.activation(soft[:, b, :], bank_a[b][:], ACT.Abs, bias=column(H_DT)).then_inc(a_abs.sem, 1)
                    act.wait_ge(*a_sp.at(h, off - 1))
                    nc.scalar.activation(relu[:, b, :], bank_a[b][:], ACT.Relu, bias=column(H_DT)).then_inc(a_took.sem, 1)
                    n = b
                    act.wait_ge(*a_silu.at(h, off, n + 1))
                    act.wait_ge(*a_lin.at(h, off - 1, KS0 + b + 1))
                    nc.scalar.activation(sq[:, b, :], kq[p][:, 1, tok(b)], ACT.Square).then_inc(a_sq.sem, 1)
                if s == 5 and k < PB:
                    take(QS0 + b)
                    act.wait_ge(*a_nrm.at(h, off - 1, b + 1))
                    nc.scalar.activation(rs[:, b, :], bank_a[b][:], ACT.Ln, bias=eps6).then_inc(a_took.sem, 1)
                    act.wait_ge(*a_took.at(h, off, QS0 + b + 1))
                    nc.scalar.activation(rs[:, b, :], rs[:, b, :], ACT.Exp, scale=-0.5, bias=qscale).then_inc(a_rs.sem, 1)
                    act.wait_ge(*a_silu.at(h, off, 2 + b + 1))
                    nc.scalar.activation(sq[:, b, :], kq[p][:, 0, tok(b)], ACT.Square).then_inc(a_sq.sem, 1)
                    act.wait_ge(*a_abs.at(h, off, b + 1))
                    nc.scalar.activation(soft[:, b, :], soft[:, b, :], ACT.Exp, scale=-1.0).then_inc(a_soft.sem, 1)
                    act.wait_ge(*a_soft.at(h, off, b + 1))
                    nc.scalar.activation(softln[:, b, :], soft[:, b, :], ACT.Ln, bias=K.small[:, ONE:ONE + 1]).then_inc(a_ln.sem, 1)
                if s == 6 and k < PB:
                    take(KS0 + b)
                    act.wait_ge(*a_nrm_k.at(h, off - 1, b + 1))
                    nc.scalar.activation(rs[:, 2 + b, :], bank_a[b][:], ACT.Ln, bias=eps6).then_inc(a_took.sem, 1)
                    act.wait_ge(*a_took.at(h, off, KS0 + b + 1))
                    nc.scalar.activation(rs[:, 2 + b, :], rs[:, 2 + b, :], ACT.Exp, scale=-0.5, bias=zero).then_inc(a_rs.sem, 1)
                if s == 6 and k == 2:
                    act.wait_ge(*a_dec.at(h, off - 1))
                    nc.scalar.activation(nega[:, 0:1], column(H_ALOG), ACT.Exp).then_inc(a_nega.sem, 1)
                    act.wait_ge(*a_nega.at(h, off, 1))
                    nc.scalar.activation(nega[:, 1:2], nega[:, 0:1], ACT.Copy, scale=-1.0).then_inc(a_nega.sem, 1)
                if s == 7 and k < PB:
                    take(VT0 + b)
                    act.wait_ge(*c_r.at(h, off - 2))
                    act.wait_ge(*c_ul.at(h, off - 2, 1))
                    nc.scalar.activation(chunks(vtok[p], b).rearrange("p g n -> p (g n)"), bank_a[b][:], ACT.Copy).then_inc(a_took.sem, 1)
                    act.wait_ge(*a_nega.at(h, off))
                    act.wait_ge(*a_sp.at(h, off, 3 * (b + 1)))
                    act.wait_ge(*b_dec.at(h, off - 2, 2 + b))
                    act.wait_ge(*b_ks.at(h, off - 2, 2 + b))
                    act.wait_ge(*b_kq.at(h, off - 2, 4))
                    nc.scalar.activation(dec[p][0][:, tok(b)], soft[:, b, :], ACT.Exp, scale=nega[:, 1:2]).then_inc(a_dec.sem, 1)

            def Bp(h, off, s, k):
                p = off % 2
                l = s - 2
                if s == 1 and k == 2:
                    act.wait_ge(*b_tl.at(h, off - 1))
                    nc.scalar.activation(tm[:], bcast(eye, 1, G), ACT.Copy).then_inc(b_init.sem, 1)
                    act.wait_ge(*c_ul.at(h, off - 2))
                    nc.scalar.activation(tt[p][:], bcast(eye, 1, G), ACT.Copy).then_inc(b_init.sem, 1)
                if k == 1 and l >= 0:
                    for b in range(PB):
                        n = 2 * l + b
                        act.wait_ge(*b_zl.at(h, off, n + 1))
                        act.wait_ge(*(b_tl.at(h, off, n - 1) if l else b_tl.at(h, off - 1, 2 * (LEVELS - 1) + b + 1)))
                        nc.scalar.activation(half_cols(z, b, l, 0), bank_t[b][:, 0:NC_ * HALF].rearrange("p (g n h) -> p g n h", g=NC_, h=1 << l),
                                             ACT.Copy, scale=K.small[:, ODD0 + l:ODD0 + l + 1]).then_inc(b_zed.sem, 1)

            def Cp(h, off, s, k):
                ci = s - 1
                if s == 0 and k < PB:
                    act.wait_ge(*c_kt.at(h, off, k + 1))
                    act.wait_ge(*c_sl.at(h, off - 1))
                    nc.scalar.activation(chunks(kst, k).rearrange("p g n -> p (g n)"), bank_c[k][:], ACT.Copy).then_inc(c_kst.sem, 1)
                if 0 <= ci < NC_ and k == 1:
                    act.wait_ge(*c_ul.at(h, off, ci + 1))
                    act.wait_ge(*(c_ol.at(h, off, ci) if ci else c_ol.at(h, off - 1)))
                    nc.scalar.activation(u[:].rearrange("p b n -> p (b n)"), bank_c[1][:, 0:PB * P], ACT.Copy).then_inc(c_u.sem, 1)
                if 0 <= ci < NC_ and k == 2:
                    act.wait_ge(*c_ol.at(h, off, ci + 1))
                    if ci == 0:
                        act.wait_ge(*c_wl.at(h, off - 1))
                    nc.scalar.activation(o[:, :, ci * CH:(ci + 1) * CH], bank_c[0][:, 0:PB * P].rearrange("p (b n) -> p b n", b=PB), ACT.Copy).then_inc(c_o.sem, 1)
                if s == NC_ + 1 and k < PB:
                    b = k
                    act.wait_ge(*c_o.at(h, off))
                    act.wait_ge(*c_nl.at(h, off - 1, b + 1))
                    nc.scalar.activation(osq[:, b, :], o[:, b, :], ACT.Square).then_inc(c_sq.sem, 1)
                    act.wait_ge(*c_nl.at(h, off, b + 1))
                    act.wait_ge(*c_nrm.at(h, off - 1, b + 1))
                    nc.scalar.activation(ors[:, b, :], bank_c[b][:], ACT.Ln, bias=eps5).then_inc(c_log.sem, 1)
                    act.wait_ge(*c_log.at(h, off, b + 1))
                    nc.scalar.activation(ors[:, b, :], ors[:, b, :], ACT.Exp, scale=-0.5).then_inc(c_rs.sem, 1)

            act.wait_ge(cleared, 3)
            for s in range(STEPS):
                for k in range(3):
                    A(0, 0, s, k)
            with act.Fori(0, HEADS) as h:
                for s in range(STEPS):
                    for k in range(3):
                        Bp(h, 0, s, k)
                        A(h, 1, s, k)
                for s in range(STEPS):
                    for k in range(3):
                        Bp(h, 1, s, k)
                        Cp(h, 0, s, k)
                for s in range(STEPS):
                    for k in range(3):
                        Cp(h, 1, s, k)
                        A(h, 2, s, k)

        @block.vector
        def _(dve):
            for x in all_tallies["dve"]:
                x.prime(dve)
            for buf in (mt[0], mt[1], z):
                nc.vector.memset(buf[:], 0.0).then_inc(cleared, 1)
            dve.wait_ge(cleared, 3)
            dve.wait_ge(mask_in, 16)

            def A(h, off, s, k):
                p = off % 2
                if s <= 2 and k < PB:
                    b, n = k, 2 * s + k
                    if n == 0:
                        dve.wait_ge(*c_ol.at(h, off - 2))
                        if p == 0:
                            dve.wait_ge(*w_in.now(h + off // 2 if off else h))
                    if s == 2:
                        dve.wait_ge(*a_lin.at(h, off - 1, VT0 + b + 1))
                    y = (kq[p][:, 1, tok(b)], kq[p][:, 0, tok(b)], vc[:, tok(b)])[s]
                    taps = (H_CQ, H_CK, H_CV)[s]
                    x = raw[:, n % 3, :]
                    dve.wait_ge(*a_took.at(h, off, n + 1))
                    nc.vector.tensor_scalar(y, x, w_c[:, taps + KTAPS - 1:taps + KTAPS], None, ALU.mult).then_inc(a_conv.sem, 1)
                    for d in range(1, KTAPS):
                        dve.wait_ge(*a_conv.at(h, off, KTAPS * n + d))
                        tap = w_c[:, taps + KTAPS - 1 - d:taps + KTAPS - d]
                        nc.vector.scalar_tensor_tensor(y[:, d:T], x[:, 0:T - d], tap, y[:, d:T], ALU.mult, ALU.add).then_inc(a_conv.sem, 1)
                if s == 5 and k < PB:
                    b = k
                    dve.wait_ge(*a_soft.at(h, off, b + 1))
                    dve.wait_ge(*a_sp.at(h, off - 1, 3 * b + 1))
                    nc.vector.tensor_scalar(less[:, b, :], soft[:, b, :], 1.0, -1.0, ALU.add, ALU.add).then_inc(a_less.sem, 1)

            def Bp(h, off, s, k):
                p = off % 2
                l = s - 1
                if k == 0 and s <= LEVELS:
                    for b in range(PB):
                        dve.wait_ge(*b_kk.at(h, off, 2 * s + b + 1))
                        if s == 0:
                            if b == 0:
                                dve.wait_ge(*c_ol.at(h, off - 2))
                            nc.vector.tensor_tensor(chunks(bt[p], b), bank_k[b][:].rearrange("p (g n) -> p g n", g=NC_), bcast(eye, 1, NC_), ALU.mult).then_inc(b_got.sem, 1)
                            continue
                        both = bank_k[b][:].rearrange("p (g m n h) -> p g m n h", g=NC_, m=2, h=1 << l)
                        mask = bcast(level_mask[:, l, :].rearrange("p (n h) -> p n h", h=1 << l), 1, NC_)
                        n = 2 * l + b
                        dve.wait_ge(*(b_zl.at(h, off, n - 3) if l >= 2 else b_zl.at(h, off - 1)))
                        dve.wait_ge(*b_got.at(h, off, n + 1))
                        nc.vector.tensor_tensor(half_cols(mt[l % 2], b, l, 1), both[:, :, 0], mask, ALU.mult).then_inc(b_m.sem, 1)
                        nc.vector.copy_predicated(half_cols(bt[p], b, l, 1), mask.bitcast(U32), both[:, :, 1]).then_inc(b_got.sem, 1)
                l = s - 2
                if k == 2 and l >= 0:
                    for b in range(PB):
                        n = 2 * l + b
                        dve.wait_ge(*b_tl.at(h, off, n + 1))
                        got = bank_t[b][:].rearrange("p (two g h) -> p two g h", two=2, h=1 << l)
                        if l < LEVELS - 1:
                            part = half_flat(tm, b, l, 0)
                            dve.wait_ge(*(b_tm.at(h, off, n - 1) if l else b_init.at(h, off)))
                            nc.vector.tensor_tensor(part, part, got[:, 0], ALU.add).then_inc(b_tm.sem, 1)
                        part = half_flat(tt[p], b, l, 1)
                        dve.wait_ge(*(b_tt.at(h, off, n - 1) if l else b_init.at(h, off)))
                        nc.vector.scalar_tensor_tensor(part, got[:, 1], K.small[:, EVEN0 + l:EVEN0 + l + 1], part, ALU.mult, ALU.add).then_inc(b_tt.sem, 1)

            def Cp(h, off, s, k):
                p = off % 2
                ci = s - 1
                if 1 <= ci < NC_ and k == 0:
                    dve.wait_ge(*c_rl.at(h, off, ci))
                    dve.wait_ge(*(c_ul.at(h, off, ci) if ci > 1 else c_ul.at(h, off - 1)))
                    v_ = vtok[p][:].rearrange("p (b g) n -> p b g n", b=PB)[:, :, ci, :]
                    nc.vector.tensor_tensor(r[:], v_, bank_c[0][:, 0:PB * P].rearrange("p (b n) -> p b n", b=PB), ALU.subtract).then_inc(c_r.sem, 1)
                if 0 <= ci < NC_ - 1 and k == 2:
                    dve.wait_ge(*c_sl.at(h, off, ci + 1))
                    dve.wait_ge(*c_ol.at(h, off, ci + 1))
                    dve.wait_ge(*b_dec.at(h, off))
                    for b in range(PB):
                        src = bank_c[1][:, b * P:(b + 1) * P]
                        if ci == 0:
                            st = nc.vector.tensor_copy(state[:, b, :], src)
                        else:
                            if b == 0:
                                dve.wait_ge(*c_s.at(h, off, PB * ci))
                            g = b * NC_ + ci
                            st = nc.vector.scalar_tensor_tensor(state[:, b, :], state[:, b, :], dec[p][LEVELS][:, g:g + 1], src, ALU.mult, ALU.add)
                        st.then_inc(c_s.sem, 1)
                if s == NC_ + 1 and k < PB:
                    b = k
                    dve.wait_ge(*c_rs.at(h, off, b + 1))
                    nc.vector.scalar_tensor_tensor(o[:, b, :], o[:, b, :], w_on, ors[:, b, :], ALU.mult, ALU.mult).then_inc(c_nrm.sem, 1)
                if s in (NC_ + 2, NC_ + 3) and k < KC:
                    b, m = s - NC_ - 2, k
                    dve.wait_ge(*c_wl.at(h, off, b * KC + m + 1))
                    dve.wait_ge(*c_add.at(h, off - 2, b * KC + m + 1))
                    gb = p * PB + b
                    part = X[:, m, gb * T:(gb + 1) * T]
                    nc.vector.tensor_tensor(part, part, bank_c[m][:], ALU.add).then_inc(c_add.sem, 1)

            w_on = K.vec[:, V_ON, 0:1]
            for s in range(STEPS):
                for k in range(3):
                    A(0, 0, s, k)
            with dve.Fori(0, HEADS) as h:
                for s in range(STEPS):
                    for k in range(3):
                        Bp(h, 0, s, k)
                        A(h, 1, s, k)
                for s in range(STEPS):
                    for k in range(3):
                        Bp(h, 1, s, k)
                        Cp(h, 0, s, k)
                for s in range(STEPS):
                    for k in range(3):
                        Cp(h, 1, s, k)
                        A(h, 2, s, k)

        @block.gpsimd
        def _(pool):
            for x in all_tallies["pool"]:
                x.prime(pool)

            def A(h, off, s, k):
                p = off % 2
                if s == 6 and k < PB:
                    b = k
                    pool.wait_ge(*a_less.at(h, off, b + 1))
                    pool.wait_ge(*a_ln.at(h, off, b + 1))
                    nc.gpsimd.tensor_tensor(soft[:, b, :], soft[:, b, :], less[:, b, :], ALU.subtract).then_inc(a_sp.sem, 1)
                    for n, more in ((1, softln), (2, relu)):
                        pool.wait_ge(*a_sp.at(h, off, 3 * b + n))
                        if n == 2:
                            pool.wait_ge(*a_took.at(h, off, G0 + b + 1))
                        nc.gpsimd.tensor_tensor(soft[:, b, :], soft[:, b, :], more[:, b, :], ALU.add).then_inc(a_sp.sem, 1)
                if s == 7 and k < PB:
                    for n in (0, 2):
                        y = kq[p][:, 1 if n == 0 else 0, tok(k)]
                        pool.wait_ge(*a_rs.at(h, off, n + k + 1))
                        pool.wait_ge(*a_sq.at(h, off, n + k + 1))
                        if n == 0:
                            nc.gpsimd.tensor_tensor(y, y, rs[:, n + k, :], ALU.mult).then_inc(a_nrm.sem, 1)
                        else:
                            nc.gpsimd.tensor_tensor(y, y, rs[:, n + k, :], ALU.mult).then_inc(a_nrm_k.sem, 1)
                if s == 8 and k < PB:
                    if k == 0:
                        pool.wait_ge(*w_in.now(h + off // 2 if off else h))
                    pool.wait_ge(*a_nrm_k.at(h, off, k + 1))
                    pool.wait_ge(*c_kt.at(h, off - 2, k + 1))
                    gb = p * PB + k
                    nc.gpsimd.tensor_tensor(ks[p][:, tok(k)], kq[p][:, 0, tok(k)], beta[:, gb * T:(gb + 1) * T], ALU.mult).then_inc(a_ks.sem, 1)

            def Bp(h, off, s, k):
                p = off % 2
                if k == 0 and s <= LEVELS:
                    for b in range(PB):
                        l = s - 1
                        pool.wait_ge(*b_kk.at(h, off, 2 * s + b + 1))
                        both = kq[p][:, :, tok(b)]
                        if s == 0:
                            pool.wait_ge(*a_dec.at(h, off, b + 1))
                            pool.wait_ge(*a_ks.at(h, off, b + 1))
                            nc.gpsimd.tensor_tensor(both, both, bcast(dec[p][0][:, tok(b)], 1, 2), ALU.mult).then_inc(b_kq.sem, 1)
                            continue
                        half = 1 << l
                        nb = T // (2 * half)
                        d = dec[p][l][:, b * 2 * nb:(b + 1) * 2 * nb].rearrange("p (n two) -> p n two", two=2)
                        pool.wait_ge(*b_kq.at(h, off, 2 * s + b - 1))
                        if l:
                            pool.wait_ge(*b_dec.at(h, off, 2 * (l - 1) + b + 1))
                            pool.wait_ge(*b_ks.at(h, off, 2 * (l - 1) + b + 1))
                        second = both.rearrange("p m (n two h) -> p m n two h", two=2, h=half)[:, :, :, 1, :]
                        nc.gpsimd.tensor_tensor(second, second, bcast(bcast(d[:, :, 0], 2, half), 1, 2), ALU.mult).then_inc(b_kq.sem, 1)
                        first = ks[p][:, tok(b)].rearrange("p (n two h) -> p n two h", two=2, h=half)[:, :, 0, :]
                        nc.gpsimd.tensor_tensor(first, first, bcast(d[:, :, 1], 2, half), ALU.mult).then_inc(b_ks.sem, 1)
                        if l == LEVELS - 1:
                            pool.wait_ge(*c_s.at(h, off - 2))
                        nc.gpsimd.tensor_tensor(dec[p][l + 1][:, b * nb:(b + 1) * nb], d[:, :, 0], d[:, :, 1], ALU.mult).then_inc(b_dec.sem, 1)

            def Cp(h, off, s, k):
                p = off % 2
                if s == NC_ + 1 and k < PB:
                    pool.wait_ge(*c_nrm.at(h, off, k + 1))
                    nc.gpsimd.tensor_tensor(o[:, k, :], o[:, k, :], gate[p][:, tok(k)], ALU.mult).then_inc(c_gate.sem, 1)

            for s in range(STEPS):
                for k in range(3):
                    A(0, 0, s, k)
            with pool.Fori(0, HEADS) as h:
                for s in range(STEPS):
                    for k in range(3):
                        Bp(h, 0, s, k)
                        A(h, 1, s, k)
                for s in range(STEPS):
                    for k in range(3):
                        Bp(h, 1, s, k)
                        Cp(h, 0, s, k)
                for s in range(STEPS):
                    for k in range(3):
                        Cp(h, 1, s, k)
                        A(h, 2, s, k)
class Constants:
    pass


def program(nc, dram, out_dram):
    with ExitStack() as ctx:
        signals = ctx.enter_context(Signals(nc))
        def sb(n, shape, dt=F32):
            return ctx.enter_context(nc.sbuf_tensor(n, shape, dt))

        K = Constants()
        X = sb("X", [P, KC, N])
        XN = sb("XN", [P, KC, N])
        K.mats = sb("mats", [P, N_MATS, P])
        K.small = sb("small", [P, N_SMALL])
        K.vec = sb("vec", [P, V_COUNT, KC])
        with nc.semaphore("loaded") as loaded, nc.Block() as block:
            @block.sync
            def _(sp):
                sp.dma_start(X[:], dram["x"][:]).then_inc(loaded, 16)
                sp.dma_start(K.mats[:], dram["mats"][:]).then_inc(loaded, 16)
                sp.dma_start(K.small[:], dram["small"][:]).then_inc(loaded, 16)
                sp.dma_start(K.vec[:], dram["vec"][:]).then_inc(loaded, 16)
                sp.wait_ge(loaded, 64)

        norm_stage(nc, "ln0", K, X, XN, True, EPS5, None)
        memory_stage(nc, K, X, XN, dram["l0w"])
        with nc.sbuf_tensor("HID", [P, KC, N], F32) as HID:
            norm_stage(nc, "ln1", K, X, HID, True, EPS5, None)
            norm_stage(nc, "rms1", K, HID, XN, False, EPS6, V_LN1)
            attention_stage(nc, K, HID, XN, dram["attn_w"])
            norm_stage(nc, "rms2", K, HID, XN, False, EPS6, V_LN2)
            swiglu_stage(nc, "moe", K, X, XN, J0, dram["ff0_up"], dram["ff0_down"], HID, dram["gate_w"], dram["expert_of"], dram["earlier"])
        norm_stage(nc, "ln2", K, X, XN, True, EPS5, None)
        delta_stage(nc, K, X, XN, dram)
        norm_stage(nc, "ln3", K, X, XN, True, EPS5, None)
        swiglu_stage(nc, "ffn", K, X, XN, J1, dram["ff1_up"], dram["ff1_down"])
        with nc.semaphore("stored") as stored, nc.Block() as block:
            @block.sync
            def _(sp):
                sp.dma_start(out_dram[:], X[:]).then_inc(stored, 16)
                sp.wait_ge(stored, 16)


def constants():
    i = np.arange(P)
    mats = np.zeros((P, N_MATS, P), np.float32)
    mats[:, EYE] = np.eye(P)
    mats[:, MEAN_C] = 1.0 / C
    mats[:, MEAN_D] = (i[:, None] // D0 == i[None, :] // D0) / D0
    mats[:, MEAN_P] = 1.0 / P
    mats[:, ONES] = 1.0
    mats[:, CAUSAL_OUT] = -1e9 * (i[None, :] > i[:, None])
    small = np.zeros((P, N_SMALL), np.float32)
    small[:, EPS5], small[:, EPS6] = 1e-5, 1e-6
    small[:, ONE] = 1.0
    small[:, L2BACK] = 20.0 * np.log(2.0)
    small[:, QSCALE] = np.log(128.0) * -0.5
    for l in range(LEVELS):
        odd = i >> l & 1
        small[:, ODD0 + l] = -odd.astype(np.float32)
        small[:, EVEN0 + l] = 1 - odd
    level_mask = np.zeros((P, LEVELS, P // 2), np.float32)
    for l in range(LEVELS):
        seconds = i[(i >> l & 1) == 1]
        level_mask[:, l] = ((i[:, None] >> l & 1) == 0) & (i[:, None] >> l + 1 == seconds[None, :] >> l + 1)
    ch = np.arange(J0 * P)
    expert_of = (np.minimum(ch // I, E)[None, :] == np.arange(SELROWS)[:, None]).astype(np.float32)
    earlier = np.broadcast_to(np.tri(E, k=-1, dtype=np.float32), (P, E, E))
    return {"earlier": earlier, "mats": mats, "small": small, "level_mask": level_mask,
            "expert_of": expert_of.reshape(SELROWS, J0, P)}


def halves(w):
    return w.reshape(KC, P, -1).transpose(1, 0, 2)


def columns(v):
    return v.reshape(KC, P).T


def hidden_blocks(gate, up, down, blocks):
    def padded(w):
        out = np.zeros((blocks * P, C), np.float32)
        out[:w.shape[0]] = w
        return out
    ups = np.stack([padded(w).reshape(blocks, P, KC, P).transpose(3, 0, 2, 1) for w in (gate, up)], axis=3)
    return ups, padded(down).reshape(blocks, P, C).transpose(1, 0, 2)


def layouts(a):
    a = {k: np.asarray(v) for k, v in a.items()}
    L0, F0, L1, F1 = ({k[len(p):]: v for k, v in a.items() if k.startswith(p)} for p in ("L0_attn_", "L0_ffn_", "L1_attn_", "L1_ffn_"))
    out = constants()
    out["x"] = halves(L0["x"].reshape(N, C).T)
    mats = [L0["Wq"], L0["Wk"], L0["Wv"], L0["ig_w"], L0["og_w"], np.repeat(L0["gamma_w"], D0, axis=0), L0["Wo"]]
    out["l0w"] = np.stack([halves(m.T) for m in mats], axis=1)
    taps = [L0["conv_w"][:, 0, i] for i in range(KTAPS)]
    vec = taps + [L0["conv_b"], L0["ig_b"], L0["og_b"], np.repeat(L0["gamma_b"], D0)]
    vec += [np.tile(L0[n], HEADS) for n in ("vn_g", "vn_b", "mn_g", "mn_b")] + [L0["gn_g"], L0["gn_b"], F0["ln1_w"], F0["ln2_w"], np.tile(L1["o_norm_w"], KC)]
    out["vec"] = np.stack([columns(v) for v in vec], axis=1)
    qw = F0["q_w"].reshape(HEADS, QHD, C)[:, :P]
    kw = F0["kv_w"][:HEADS * P].reshape(HEADS, P, C)
    vw = F0["kv_w"][HEADS * P:2 * HEADS * P].reshape(HEADS, P, C)
    qkv = np.stack([w.reshape(HEADS, P, KC, P).transpose(0, 3, 2, 1) for w in (qw, kw, vw)], axis=2)
    ow = F0["o_w"].reshape(C, HEADS, VD).transpose(1, 2, 0)
    out["attn_w"] = np.concatenate([qkv.reshape(HEADS, P, -1), ow], axis=2)
    w1, w2 = F0["w1"], F0["w2"]
    gate = np.concatenate([w1[:, :I].reshape(E * I, C), F0["sh_gu_w"][:SHI]])
    up = np.concatenate([w1[:, I:].reshape(E * I, C), F0["sh_gu_w"][SHI:]])
    down = np.concatenate([w2.transpose(0, 2, 1).reshape(E * I, C), F0["sh_down_w"].T])
    out["ff0_up"], out["ff0_down"] = hidden_blocks(gate, up, down, J0)
    out["gate_w"] = halves(F0["gate_w"].T)
    out["ff1_up"], out["ff1_down"] = hidden_blocks(F1["w_gate"], F1["w_up"], F1["w_down"].T, J1)
    def by_head(w):
        return w.reshape(KC, P, HEADS, P).transpose(2, 1, 0, 3).reshape(HEADS, P, KC * P)
    cols = [L1[n].reshape(HEADS, P, KTAPS) for n in ("conv_q", "conv_k", "conv_v")]
    cols += [L1["dt_bias"].reshape(HEADS, P, 1), L1["bg"].reshape(HEADS, P, 1), np.broadcast_to(L1["A_log"][:, None, None], (HEADS, P, 1)),
             np.zeros((HEADS, P, 1), np.float32)]
    delta_w = np.concatenate([by_head(L1["Wq"]), by_head(L1["Wk"]), by_head(L1["Wv"]), by_head(L1["Wg"]),
                                     L1["Wf2"].reshape(P, HEADS, P).transpose(1, 0, 2), L1["Wo"].reshape(HEADS, P, C)] + cols, axis=2)
    out["delta_w"] = np.concatenate([delta_w, np.zeros_like(delta_w[:1])])
    out["delta_f1"] = halves(L1["Wf1"])
    out["delta_b"] = halves(L1["Wb"])
    return {k: np.ascontiguousarray(v) for k, v in out.items()}


def kernel(**inputs):
    import concourse.bacc as bacc
    from concourse.bass_utils import run_bass_kernel_spmd

    arrays = layouts(inputs)
    nc = bacc.Bacc("TRN2", target_bir_lowering=False, num_devices=1)
    dram = {k: nc.dram_tensor("in_" + k, v.shape, mybir.dt.from_np(v.dtype), kind="ExternalInput").ap() for k, v in arrays.items()}
    out = nc.dram_tensor("out", [P, KC, N], F32, kind="ExternalOutput").ap()
    program(nc, dram, out)
    r = run_bass_kernel_spmd(nc, [{"in_" + k: v for k, v in arrays.items()}], core_ids=[0])
    y = r.results[0]["out"]
    return y.transpose(1, 0, 2).reshape(C, N).T.reshape(B, T, C)
```

```python
from contextlib import ExitStack

import numpy as np

import concourse.bass as bass
from concourse import mybir
from concourse.alu_op_type import AluOpType as ALU

F32 = mybir.dt.float32
U32 = mybir.dt.uint32
ACT = mybir.ActivationFunctionType
LN_EXP = "natural_log_exp_and_others"
AXX = mybir.AxisListType.X

P = 128
B, T, C = 4, 512, 256
N = B * T
KC = C // P
TILE = 512
NT = N // TILE
HEADS = 16
KTAPS = 4
D0 = C // HEADS

EYE, MEAN_C, MEAN_D, MEAN_P, ONES, CAUSAL_OUT = range(6)
N_MATS = 6
(ZERO, EPS5, EPS6, L2BACK, QSCALE, ODD0) = range(6)
EVEN0 = ODD0 + 7
ONE = EVEN0 + 7
N_SMALL = ONE + 1

L0_MATS = 7
(W_Q, W_K, W_V, W_I, W_OG, W_GAM, W_O) = range(L0_MATS)
(V_TAP0, V_TAP1, V_TAP2, V_TAP3, V_CONVB, V_IB, V_OB, V_GB, V_VG, V_VB, V_MG, V_MB, V_GG, V_GNB, V_LN1,
 V_LN2, V_ON, V_COUNT) = range(18)

QHD, VD = 192, 128
ATTN_SCALE = float(QHD) ** -0.5
ATTN_W = 3 * KC * P + C

E, I, TOPK, SHI = 16, 176, 4, 352
FF0 = E * I + SHI
J0 = (FF0 + P - 1) // P
FF1 = 1024
J1 = FF1 // P
SELROWS = E + 1

CH = 128
NC_ = T // CH
LEVELS = 7
(H_CQ, H_CK, H_CV, H_DT, H_BG, H_ALOG, _, H_COLS) = (0, 4, 8, 12, 13, 14, 15, 16)


class Signals:

    def __init__(self, nc):
        self.nc, self.sems = nc, []

    def __enter__(self):
        return self

    def __call__(self, name):
        self.sems.append(self.nc.alloc_semaphore(name))
        return self.sems[-1]

    def __exit__(self, *_):
        self.nc.clear_and_free_semaphores(self.sems)
        self.nc.all_engine_barrier()


class Tally:

    def __init__(self, sem, per):
        self.sem, self.per = sem, per

    def prime(self, eng):
        eng.sem_inc(self.sem, self.per)

    def now(self, turn, n=None):
        return self.sem, turn * self.per + (self.per + (self.per if n is None else n))

    def last(self, turn, n=None):
        return self.sem, turn * self.per + (self.per if n is None else n)


def bcast(ap, dim, count):
    wide = ap.unsqueeze(dim)
    shape = list(wide.shape)
    shape[dim] = count
    return wide.broadcast_to(shape)


def norm_stage(nc, name, K, src, dst, centred, eps_col, weight_col):
    with ExitStack() as ctx:
        signals = ctx.enter_context(Signals(nc))
        def sb(n, shape):
            return ctx.enter_context(nc.sbuf_tensor(f"{name}_{n}", shape, F32))

        def sem(n):
            return signals(f"{name}_{n}")

        squares = sb("squares", [P, KC, N])
        logvar = sb("logvar", [P, N])
        rstd = sb("rstd", [P, N])
        ps_mean = [ctx.enter_context(nc.psum_tensor(f"{name}_psm{t}", [P, TILE], F32)) for t in range(NT)]
        ps_var = [ctx.enter_context(nc.psum_tensor(f"{name}_psv{t}", [P, TILE], F32)) for t in range(NT)]
        mean_ready, centre_ready, square_ready, var_ready = (sem(n) for n in ("mean", "centre", "square", "var"))
        logvar_ready, rstd_ready, normed = (sem(n) for n in ("logvar", "rstd", "normed"))
        block = ctx.enter_context(nc.Block())
        mean_mat = K.mats[:, MEAN_C, :]
        body = dst if centred else src

        def tok(t):
            return slice(t * TILE, (t + 1) * TILE)

        @block.tensor
        def _(pe):
            if centred:
                for t in range(NT):
                    for k in range(KC):
                        mm = nc.tensor.matmul(ps_mean[t][:], mean_mat, src[:, k, tok(t)], start=k == 0, stop=k == KC - 1)
                    mm.then_inc(mean_ready, 1)
            for t in range(NT):
                pe.wait_ge(square_ready, t + 1)
                for k in range(KC):
                    mm = nc.tensor.matmul(ps_var[t][:], mean_mat, squares[:, k, tok(t)], start=k == 0, stop=k == KC - 1)
                mm.then_inc(var_ready, 1)

        @block.scalar
        def _(act):
            for t in range(NT):
                if centred:
                    act.wait_ge(centre_ready, t + 1)
                nc.scalar.activation(squares[:, :, tok(t)], body[:, :, tok(t)], ACT.Square).then_inc(square_ready, 1)
            nc.scalar.preload_act_table_set(LN_EXP)
            for t in range(NT):
                act.wait_ge(var_ready, t + 1)
                nc.scalar.activation(logvar[:, tok(t)], ps_var[t][:], ACT.Ln, bias=K.small[:, eps_col:eps_col + 1]).then_inc(logvar_ready, 1)
                act.wait_ge(logvar_ready, t + 1)
                nc.scalar.activation(rstd[:, tok(t)], logvar[:, tok(t)], ACT.Exp, scale=-0.5).then_inc(rstd_ready, 1)

        @block.vector
        def _(dve):
            if centred:
                for t in range(NT):
                    dve.wait_ge(mean_ready, t + 1)
                    nc.vector.tensor_tensor(dst[:, :, tok(t)], src[:, :, tok(t)], bcast(ps_mean[t][:], 1, KC), ALU.subtract).then_inc(centre_ready, 1)
            for t in range(NT):
                dve.wait_ge(rstd_ready, t + 1)
                if centred:
                    nc.vector.tensor_tensor(dst[:, :, tok(t)], dst[:, :, tok(t)], bcast(rstd[:, tok(t)], 1, KC), ALU.mult).then_inc(normed, 1)
                else:
                    for k in range(KC):
                        nc.vector.scalar_tensor_tensor(dst[:, k, tok(t)], src[:, k, tok(t)], K.vec[:, weight_col, k:k + 1], rstd[:, tok(t)], ALU.mult, ALU.mult).then_inc(normed, 1)


def memory_stage(nc, K, X, XN, weights_dram):
    with ExitStack() as ctx:
        signals = ctx.enter_context(Signals(nc))
        def sb(n, shape=(P, KC, T)):
            return ctx.enter_context(nc.sbuf_tensor("mem_" + n, list(shape), F32))

        def tallies(names):
            return [Tally(signals("mem_" + n), 1) for n in names.split()]

        w = sb("w", [P, L0_MATS, KC, C])
        conv, xc, q_raw, k_raw, v_raw, q_sq, k_sq, v_sq = (sb(f"b{n}") for n in range(8))
        q_rs, k_rs, v_rs, q, k, v, ig, gam, og = (sb(f"c{n}") for n in range(9))
        mem, mem_sq, mem_rs, out, out_sq, out_rs, og_kept = (sb(f"d{n}") for n in range(7))
        pa, pb, pc, pd = (ctx.enter_context(nc.psum_tensor(f"mem_p{i}", [P, KC, T], F32)) for i in range(4))
        (q_lin, k_lin, v_lin, q_sum, k_sum, v_mean, v_var, ig_lin, gam_lin, og_lin, mem_mean, mem_var, out_mean,
         out_var, o_lin) = pe_made = tallies("q_lin k_lin v_lin q_sum k_sum v_mean v_var ig_lin gam_lin og_lin mem_mean mem_var out_mean out_var o_lin")
        (q_got, k_got, v_got, q_sqd, k_sqd, v_sqd, xc_got, q_log, q_rsd, k_log, k_rsd, v_log, v_rsd, ig_got, gam_got,
         og_got, mem_sqd, mem_log, mem_rsd, out_sqd, out_log, out_rsd, og_moved) = act_made = tallies(
            "q_got k_got v_got q_sqd k_sqd v_sqd xc_got q_log q_rsd k_log k_rsd v_log v_rsd ig_got gam_got og_got mem_sqd mem_log mem_rsd out_sqd out_log out_rsd og_moved")
        (q_floor, k_floor, v_cent, q_nrm, k_nrm, v_nrm, v_aff, kv, ikv, scanned, mem_cent, mem_nrm, mem_aff,
         mem_q, out_cent, out_nrm, out_aff, gated, added) = dve_made = tallies(
            "q_floor k_floor v_cent q_nrm k_nrm v_nrm v_aff kv ikv scanned mem_cent mem_nrm mem_aff mem_q out_cent out_nrm out_aff gated added")
        conv_step = Tally(signals("mem_conv_step"), KTAPS)
        w_in = signals("mem_w_in")
        block = ctx.enter_context(nc.Block())
        head_mean = K.mats[:, MEAN_D, :]
        zero, eps5 = K.small[:, ZERO:ZERO + 1], K.small[:, EPS5:EPS5 + 1]
        floor_back = K.small[:, L2BACK:L2BACK + 1]

        def col(n, h):
            return K.vec[:, n, h:h + 1]

        def linear(out, mat, rhs):
            for m in range(KC):
                for c in range(KC):
                    mm = nc.tensor.matmul(out[:, m, :], w[:, mat, c, m * P:(m + 1) * P], rhs(c), start=c == 0, stop=c == KC - 1)
            return mm

        def head_means(out, of):
            for m in range(KC):
                mm = nc.tensor.matmul(out[:, m, :], head_mean, of[:, m, :], start=True, stop=True)
            return mm

        @block.sync
        def _(sp):
            sp.dma_start(w[:], weights_dram[:]).then_inc(w_in, 16)

        @block.tensor
        def _(pe):
            for x in pe_made:
                x.prime(pe)
            pe.wait_ge(w_in, 16)

            def turn(b, t):
                def xn(c):
                    return XN[:, c, bass.ds(t * T, T)]

                if b is not None:
                    pe.wait_ge(*scanned.now(b))
                    pe.wait_ge(*added.last(b))
                    head_means(pd, mem).then_inc(mem_mean.sem, 1)
                if t is not None:
                    pe.wait_ge(*v_log.last(t))
                    linear(pa, W_Q, xn).then_inc(q_lin.sem, 1)
                    pe.wait_ge(*og_got.last(t))
                    linear(pb, W_K, xn).then_inc(k_lin.sem, 1)
                if b is not None:
                    pe.wait_ge(*mem_sqd.now(b))
                    head_means(pd, mem_sq).then_inc(mem_var.sem, 1)
                if t is not None:
                    linear(pc, W_V, xn).then_inc(v_lin.sem, 1)
                    pe.wait_ge(*q_got.now(t))
                    head_means(pa, q_sq).then_inc(q_sum.sem, 1)
                    pe.wait_ge(*k_got.now(t))
                    head_means(pb, k_sq).then_inc(k_sum.sem, 1)
                    pe.wait_ge(*v_got.now(t))
                    head_means(pc, v_raw).then_inc(v_mean.sem, 1)
                    pe.wait_ge(*xc_got.now(t))
                    pe.wait_ge(*q_floor.now(t))
                    linear(pa, W_I, lambda c: xc[:, c, :]).then_inc(ig_lin.sem, 1)
                    pe.wait_ge(*k_floor.now(t))
                    linear(pb, W_GAM, lambda c: xc[:, c, :]).then_inc(gam_lin.sem, 1)
                if b is not None:
                    pe.wait_ge(*mem_log.now(b))
                    pe.wait_ge(*mem_q.now(b))
                    head_means(pd, out).then_inc(out_mean.sem, 1)
                if t is not None:
                    pe.wait_ge(*v_cent.now(t))
                    linear(pc, W_OG, lambda c: xc[:, c, :]).then_inc(og_lin.sem, 1)
                if b is not None:
                    pe.wait_ge(*out_sqd.now(b))
                    head_means(pd, out_sq).then_inc(out_var.sem, 1)
                if t is not None:
                    pe.wait_ge(*v_sqd.now(t))
                    pe.wait_ge(*ig_got.now(t))
                    head_means(pa, v_sq).then_inc(v_var.sem, 1)
                if b is not None:
                    pe.wait_ge(*gated.now(b))
                    linear(pd, W_O, lambda c: out[:, c, :]).then_inc(o_lin.sem, 1)

            turn(None, 0)
            with pe.Fori(0, B - 1) as b:
                turn(b, b + 1)
            turn(B - 1, None)

        @block.scalar
        def _(act):
            for x in act_made:
                x.prime(act)

            def rsqrt(dst, src, var, log, rsd, turn, **of):
                act.wait_ge(*var.now(turn))
                nc.scalar.activation(dst[:], src[:], ACT.Ln, scale=of.get("scale", 1.0), bias=of.get("bias", eps5)).then_inc(log.sem, 1)
                act.wait_ge(*log.now(turn))
                nc.scalar.activation(dst[:], dst[:], ACT.Exp, scale=-0.5, bias=of.get("back", zero)).then_inc(rsd.sem, 1)

            def turn(b, t):
                if b is not None:
                    act.wait_ge(*og_got.now(b))
                    act.wait_ge(*gated.last(b))
                    nc.scalar.activation(og_kept[:], og[:], ACT.Copy).then_inc(og_moved.sem, 1)
                    act.wait_ge(*mem_cent.now(b))
                    nc.scalar.activation(mem_sq[:], mem[:], ACT.Square).then_inc(mem_sqd.sem, 1)
                if t is not None:
                    act.wait_ge(*q_lin.now(t))
                    act.wait_ge(*q_nrm.last(t))
                    nc.scalar.activation(q_sq[:], pa[:], ACT.Square).then_inc(q_sqd.sem, 1)
                    nc.scalar.activation(q_raw[:], pa[:], ACT.Copy).then_inc(q_got.sem, 1)
                    act.wait_ge(*k_lin.now(t))
                    act.wait_ge(*k_nrm.last(t))
                    nc.scalar.activation(k_sq[:], pb[:], ACT.Square).then_inc(k_sqd.sem, 1)
                    nc.scalar.activation(k_raw[:], pb[:], ACT.Copy).then_inc(k_got.sem, 1)
                if b is not None:
                    nc.scalar.preload_act_table_set(LN_EXP)
                    rsqrt(mem_rs, pd, mem_var, mem_log, mem_rsd, b)
                if t is not None:
                    act.wait_ge(*v_lin.now(t))
                    act.wait_ge(*v_cent.last(t))
                    nc.scalar.activation(v_raw[:], pc[:], ACT.Copy).then_inc(v_got.sem, 1)
                    act.wait_ge(*conv_step.now(t))
                    nc.scalar.activation(xc[:], conv[:], ACT.Silu).then_inc(xc_got.sem, 1)
                    act.wait_ge(*v_cent.now(t))
                    nc.scalar.activation(v_sq[:], v[:], ACT.Square).then_inc(v_sqd.sem, 1)
                if b is not None:
                    act.wait_ge(*out_cent.now(b))
                    nc.scalar.activation(out_sq[:], out[:], ACT.Square).then_inc(out_sqd.sem, 1)
                if t is not None:
                    act.wait_ge(*scanned.last(t))
                    if b is not None:
                        act.wait_ge(*og_moved.now(b))
                    for lin, src, dst, bias, got in ((ig_lin, pa, ig, V_IB, ig_got), (gam_lin, pb, gam, V_GB, gam_got), (og_lin, pc, og, V_OB, og_got)):
                        act.wait_ge(*lin.now(t))
                        for h in range(KC):
                            a = nc.scalar.activation(dst[:, h, :], src[:, h, :], ACT.Sigmoid, bias=col(bias, h))
                        a.then_inc(got.sem, 1)
                nc.scalar.preload_act_table_set(LN_EXP)
                if b is not None:
                    rsqrt(out_rs, pd, out_var, out_log, out_rsd, b)
                if t is not None:
                    rsqrt(k_rs, k_rs, k_floor, k_log, k_rsd, t, scale=2.0 ** 20 * D0, bias=zero, back=floor_back)
                    rsqrt(v_rs, pa, v_var, v_log, v_rsd, t)
                    rsqrt(q_rs, q_rs, q_floor, q_log, q_rsd, t, scale=2.0 ** 20 * D0, bias=zero, back=floor_back)

            turn(None, 0)
            with act.Fori(0, B - 1) as b:
                turn(b, b + 1)
            turn(B - 1, None)

        @block.vector
        def _(dve):
            for x in dve_made + [conv_step]:
                x.prime(dve)

            def affine(dst, src, g, bias, sem):
                for h in range(KC):
                    v_ = nc.vector.tensor_scalar(dst[:, h, :], src[:, h, :], col(g, h), col(bias, h), ALU.mult, ALU.add)
                v_.then_inc(sem, 1)

            def turn(b, t):
                if b is not None:
                    dve.wait_ge(*mem_mean.now(b))
                    dve.wait_ge(*scanned.now(b))
                    nc.vector.tensor_tensor(mem[:], mem[:], pd[:], ALU.subtract).then_inc(mem_cent.sem, 1)
                if t is not None:
                    dve.wait_ge(*xc_got.last(t))
                    for h in range(KC):
                        c_ = nc.vector.tensor_scalar(conv[:, h, :], XN[:, h, bass.ds(t * T, T)], col(V_TAP3, h), col(V_CONVB, h), ALU.mult, ALU.add)
                    c_.then_inc(conv_step.sem, 1)
                    for s in range(1, KTAPS):
                        dve.wait_ge(*conv_step.now(t, s))
                        for h in range(KC):
                            c_ = nc.vector.scalar_tensor_tensor(conv[:, h, s:T], XN[:, h, bass.ds(t * T, T - s)], col(V_TAP3 - s, h), conv[:, h, s:T], ALU.mult, ALU.add)
                        c_.then_inc(conv_step.sem, 1)
                if b is not None:
                    dve.wait_ge(*mem_rsd.now(b))
                    dve.wait_ge(*mem_cent.now(b))
                    nc.vector.tensor_tensor(mem[:], mem[:], mem_rs[:], ALU.mult).then_inc(mem_nrm.sem, 1)
                    dve.wait_ge(*mem_nrm.now(b))
                    affine(mem, mem, V_MG, V_MB, mem_aff.sem)
                    dve.wait_ge(*mem_aff.now(b))
                    dve.wait_ge(*q_nrm.now(b))
                    nc.vector.tensor_tensor(out[:], mem[:], q[:], ALU.mult).then_inc(mem_q.sem, 1)
                if t is not None:
                    dve.wait_ge(*q_sum.now(t))
                    nc.vector.tensor_scalar(q_rs[:], pa[:], 1e-24 / D0, None, ALU.max).then_inc(q_floor.sem, 1)
                    dve.wait_ge(*k_sum.now(t))
                    nc.vector.tensor_scalar(k_rs[:], pb[:], 1e-24 / D0, None, ALU.max).then_inc(k_floor.sem, 1)
                    dve.wait_ge(*v_mean.now(t))
                    dve.wait_ge(*v_got.now(t))
                    nc.vector.tensor_tensor(v[:], v_raw[:], pc[:], ALU.subtract).then_inc(v_cent.sem, 1)
                if b is not None:
                    dve.wait_ge(*out_mean.now(b))
                    dve.wait_ge(*mem_q.now(b))
                    nc.vector.tensor_tensor(out[:], out[:], pd[:], ALU.subtract).then_inc(out_cent.sem, 1)
                    dve.wait_ge(*out_rsd.now(b))
                    dve.wait_ge(*out_cent.now(b))
                    nc.vector.tensor_tensor(out[:], out[:], out_rs[:], ALU.mult).then_inc(out_nrm.sem, 1)
                    dve.wait_ge(*out_nrm.now(b))
                    affine(out, out, V_GG, V_GNB, out_aff.sem)
                    dve.wait_ge(*out_aff.now(b))
                    dve.wait_ge(*og_moved.now(b))
                    nc.vector.tensor_tensor(out[:], out[:], og_kept[:], ALU.mult).then_inc(gated.sem, 1)
                if t is not None:
                    dve.wait_ge(*k_rsd.now(t))
                    dve.wait_ge(*k_got.now(t))
                    nc.vector.tensor_tensor(k[:], k_raw[:], k_rs[:], ALU.mult).then_inc(k_nrm.sem, 1)
                    dve.wait_ge(*v_rsd.now(t))
                    dve.wait_ge(*v_sqd.now(t))
                    dve.wait_ge(*v_cent.now(t))
                    nc.vector.tensor_tensor(v[:], v[:], v_rs[:], ALU.mult).then_inc(v_nrm.sem, 1)
                    dve.wait_ge(*v_nrm.now(t))
                    affine(v, v, V_VG, V_VB, v_aff.sem)
                    dve.wait_ge(*v_aff.now(t))
                    dve.wait_ge(*k_nrm.now(t))
                    nc.vector.tensor_tensor(k[:], k[:], v[:], ALU.mult).then_inc(kv.sem, 1)
                    dve.wait_ge(*kv.now(t))
                    dve.wait_ge(*ig_got.now(t))
                    nc.vector.tensor_tensor(ig[:], ig[:], k[:], ALU.mult).then_inc(ikv.sem, 1)
                    dve.wait_ge(*q_rsd.now(t))
                    dve.wait_ge(*q_got.now(t))
                    nc.vector.tensor_tensor(q[:], q_raw[:], q_rs[:], ALU.mult).then_inc(q_nrm.sem, 1)
                    dve.wait_ge(*ikv.now(t))
                    dve.wait_ge(*gam_got.now(t))
                    for h in range(KC):
                        s_ = nc.vector.tensor_tensor_scan(mem[:, h, :], gam[:, h, :], ig[:, h, :], 0.0, ALU.mult, ALU.add)
                    s_.then_inc(scanned.sem, 1)
                if b is not None:
                    dve.wait_ge(*o_lin.now(b))
                    nc.vector.tensor_tensor(X[:, :, bass.ds(b * T, T)], X[:, :, bass.ds(b * T, T)], pd[:], ALU.add).then_inc(added.sem, 1)

            turn(None, 0)
            with dve.Fori(0, B - 1) as b:
                turn(b, b + 1)
            turn(B - 1, None)

def attention_stage(nc, K, HID, XN, weights_dram):
    QT = T // P
    UNITS = 2 * B
    TURNS = HEADS // 2
    with ExitStack() as ctx:
        signals = ctx.enter_context(Signals(nc))
        def sb(n, shape):
            return ctx.enter_context(nc.sbuf_tensor("att_" + n, shape, F32))

        def pb(n):
            return ctx.enter_context(nc.psum_tensor("att_" + n, [P, TILE], F32))

        def tally(n, per):
            return Tally(signals("att_" + n), per)

        w = [sb(f"w{s}", [P, ATTN_W]) for s in range(2)]
        w_qkv = [x[:, 0:3 * KC * P].rearrange("p (m c n) -> p m c n", m=3, c=KC) for x in w]
        w_o = [x[:, 3 * KC * P:ATTN_W] for x in w]
        q, k = (sb(n, [P, 2, T]) for n in ("q", "k"))
        v = sb("v", [P, 4, QT, VD])
        prob = sb("prob", [P, 2, T])
        probT = sb("probT", [P, 2, QT, T])
        negmax, total, inv = (sb(n, [P, 2, QT]) for n in ("negmax", "total", "inv"))
        o = sb("o", [P, 2, T])
        ps_lin, ps_s, ps_t = ([pb(f"{n}{i}") for i in range(2)] for n in ("lin", "s", "t"))
        ps_pv, ps_o = pb("pv"), pb("o_ps")
        lin, got = tally("lin", 3 * UNITS), tally("got", 3 * UNITS)
        scored, masked, maxed, expd, normed = (tally(n, QT * UNITS) for n in ("scored", "masked", "maxed", "expd", "normed"))
        inverted, turned, spread = (tally(n, QT * UNITS) for n in ("inverted", "turned", "spread"))
        pv_done, o_got = tally("pv_done", UNITS), tally("o_got", UNITS)
        o_lin, added = tally("o_lin", KC * UNITS), tally("added", KC * UNITS)
        w_in = [tally(f"w_in{s}", 16) for s in range(2)]
        block = ctx.enter_context(nc.Block())
        causal, eye = K.mats[:, CAUSAL_OUT, :], K.mats[:, EYE, :]

        @block.sync
        def _(sp):
            for x in w_in:
                x.prime(sp)
            with sp.Fori(0, TURNS) as t:
                for s in range(2):
                    sp.wait_ge(*o_lin.last(t, KC * B * (s + 1)))
                    sp.dma_start(w[s][:], weights_dram[bass.ds(t * 2 + s, 1), :, :].rearrange("o p n -> p (o n)")).then_inc(w_in[s].sem, 16)

        @block.tensor
        def _(pe):
            for x in (lin, scored, turned, pv_done, o_lin):
                x.prime(pe)

            def unit(t, u, first=False, more=True):
                def project(u, m):
                    n, b, s = 3 * u + m, u % B, u // B % 2
                    wm = w_qkv[s]
                    if b == 0 and m == 0:
                        pe.wait_ge(*w_in[s].now(t + 1 if u == UNITS else t))
                    pe.wait_ge(*got.now(t, n - 1))
                    out = ps_lin[n % 2]
                    if m < 2:
                        for c in range(KC):
                            mm = nc.tensor.matmul(out[:], wm[:, m, c, :], XN[:, c, b * T:(b + 1) * T], start=c == 0, stop=c == KC - 1)
                    else:
                        for j in range(QT):
                            for c in range(KC):
                                mm = nc.tensor.matmul(out[:, j * VD:(j + 1) * VD], XN[:, c, b * T + j * P:b * T + (j + 1) * P], wm[:, m, c, :],
                                                      start=c == 0, stop=c == KC - 1)
                    mm.then_inc(lin.sem, 1)

                def score(u, i):
                    n = QT * u + i
                    if i == 0:
                        pe.wait_ge(*got.now(t, 3 * u + 2))
                    pe.wait_ge(*expd.now(t, n - 1))
                    nc.tensor.matmul(ps_s[n % 2][:, 0:(i + 1) * P], q[:, u % 2, i * P:(i + 1) * P], k[:, u % 2, 0:(i + 1) * P],
                                     start=True, stop=True).then_inc(scored.sem, 1)

                def turn(u, i):
                    n = QT * u + i
                    pe.wait_ge(*normed.now(t, n + 1))
                    pe.wait_ge(*spread.now(t, n - 1))
                    for j in range(i + 1):
                        mm = nc.tensor.transpose(ps_t[n % 2][:, j * P:(j + 1) * P], prob[:, n % 2, j * P:(j + 1) * P], eye)
                    mm.then_inc(turned.sem, 1)

                def values(u):
                    pe.wait_ge(*got.now(t, 3 * u + 3))
                    pe.wait_ge(*spread.now(t, QT * (u + 1)))
                    pe.wait_ge(*o_got.now(t, u))
                    for j in range(QT):
                        mm = nc.tensor.matmul(ps_pv[:, j * P:T], v[:, u % 4, j, :], probT[:, u % 2, j, j * P:T], start=j == 0, stop=j == QT - 1)
                    mm.then_inc(pv_done.sem, 1)

                def output(u):
                    pe.wait_ge(*o_got.now(t, u + 1))
                    for c in range(KC):
                        n = KC * u + c
                        pe.wait_ge(*added.now(t, n))
                        nc.tensor.matmul(ps_o[:], w_o[u // B % 2][:, c * P:(c + 1) * P], o[:, u % 2, :], start=True, stop=True).then_inc(o_lin.sem, 1)

                if first:
                    for m in range(3):
                        project(u, m)
                score(u, 0)
                score(u, 1)
                if more:
                    project(u + 1, 0)
                turn(u, 0)
                score(u, 2)
                if not first:
                    values(u - 1)
                turn(u, 1)
                score(u, 3)
                if more:
                    project(u + 1, 1)
                turn(u, 2)
                if not first:
                    output(u - 1)
                if more:
                    project(u + 1, 2)
                turn(u, 3)
                if not more:
                    values(u)
                    output(u)

            unit(0, 0, first=True)
            with pe.Fori(0, TURNS - 1) as t:
                for u in range(1, UNITS + 1):
                    unit(t, u)
            for u in range(1, UNITS):
                unit(TURNS - 1, u, more=u + 1 < UNITS)

        @block.scalar
        def _(act):
            for x in (got, expd, o_got):
                x.prime(act)

            def unit(t, u, first=False, more=True):
                def take(u, m):
                    n = 3 * u + m
                    act.wait_ge(*lin.now(t, n + 1))
                    src = ps_lin[n % 2]
                    if m == 0:
                        act.wait_ge(*scored.now(t, QT * (u - 1)))
                        a = nc.scalar.activation(q[:, u % 2, :], src[:], ACT.Copy, scale=ATTN_SCALE)
                    elif m == 1:
                        a = nc.scalar.activation(k[:, u % 2, :], src[:], ACT.Copy)
                    else:
                        act.wait_ge(*pv_done.now(t, u - 3))
                        a = nc.scalar.activation(v[:, u % 4, :, :].rearrange("p j n -> p (j n)"), src[:], ACT.Copy)
                    a.then_inc(got.sem, 1)

                def exponent(u, i):
                    n = QT * u + i
                    act.wait_ge(*maxed.now(t, n + 1))
                    act.wait_ge(*turned.now(t, n - 1))
                    act.wait_ge(*inverted.now(t, n - 1))
                    nc.scalar.activation(prob[:, n % 2, 0:(i + 1) * P], ps_s[n % 2][:, 0:(i + 1) * P], ACT.Exp, bias=negmax[:, u % 2, i:i + 1],
                                         accum_out=total[:, u % 2, i:i + 1]).then_inc(expd.sem, 1)

                def out(u):
                    act.wait_ge(*pv_done.now(t, u + 1))
                    act.wait_ge(*o_lin.now(t, KC * (u - 1)))
                    nc.scalar.activation(o[:, u % 2, :], ps_pv[:], ACT.Copy).then_inc(o_got.sem, 1)

                if first:
                    for m in range(3):
                        take(u, m)
                exponent(u, 0)
                exponent(u, 1)
                if more:
                    take(u + 1, 0)
                if not first:
                    out(u - 1)
                exponent(u, 2)
                exponent(u, 3)
                if more:
                    take(u + 1, 1)
                    take(u + 1, 2)
                else:
                    out(u)

            unit(0, 0, first=True)
            with act.Fori(0, TURNS - 1) as t:
                for u in range(1, UNITS + 1):
                    unit(t, u)
            for u in range(1, UNITS):
                unit(TURNS - 1, u, more=u + 1 < UNITS)

        @block.gpsimd
        def _(pool):
            normed.prime(pool)
            with pool.Fori(0, TURNS) as t:
                for n in range(QT * UNITS):
                    u, i = n // QT, n % QT
                    pool.wait_ge(*inverted.now(t, n + 1))
                    part = prob[:, n % 2, 0:(i + 1) * P]
                    nc.gpsimd.tensor_tensor(part, part, inv[:, u % 2, i:i + 1].broadcast_to([P, (i + 1) * P]), ALU.mult).then_inc(normed.sem, 1)

        @block.vector
        def _(dve):
            for x in (masked, maxed, inverted, spread, added):
                x.prime(dve)

            def unit(t, u, first=False, more=True):
                def most(u, i):
                    n = QT * u + i
                    dve.wait_ge(*scored.now(t, n + 1))
                    diag = ps_s[n % 2][:, i * P:(i + 1) * P]
                    nc.vector.tensor_tensor(diag, diag, causal, ALU.add).then_inc(masked.sem, 1)
                    dve.wait_ge(*masked.now(t, n + 1))
                    nc.vector.tensor_reduce(negmax[:, u % 2, i:i + 1], ps_s[n % 2][:, 0:(i + 1) * P], AXX, ALU.max, negate=True).then_inc(maxed.sem, 1)

                def invert(u, i):
                    n = QT * u + i
                    dve.wait_ge(*expd.now(t, n + 1))
                    dve.wait_ge(*normed.now(t, n - 2 * QT + 1))
                    nc.vector.reciprocal(inv[:, u % 2, i:i + 1], total[:, u % 2, i:i + 1]).then_inc(inverted.sem, 1)

                def keep(u, i):
                    n = QT * u + i
                    dve.wait_ge(*turned.now(t, n + 1))
                    if i == 0:
                        dve.wait_ge(*pv_done.now(t, u - 1))
                    nc.vector.tensor_copy(probT[:, u % 2, 0:i + 1, i * P:(i + 1) * P],
                                          ps_t[n % 2][:, 0:(i + 1) * P].rearrange("p (j q) -> p j q", q=P)).then_inc(spread.sem, 1)

                def add(u):
                    b = u % B
                    for c in range(KC):
                        dve.wait_ge(*o_lin.now(t, KC * u + c + 1))
                        part = HID[:, c, b * T:(b + 1) * T]
                        dve.wait_ge(*added.now(t, KC * (u - B) + c + 1))
                        nc.vector.tensor_tensor(part, part, ps_o[:], ALU.add).then_inc(added.sem, 1)

                most(u, 0)
                most(u, 1)
                invert(u, 0)
                invert(u, 1)
                keep(u, 0)
                most(u, 2)
                invert(u, 2)
                keep(u, 1)
                most(u, 3)
                invert(u, 3)
                keep(u, 2)
                if not first:
                    add(u - 1)
                keep(u, 3)
                if not more:
                    add(u)

            unit(0, 0, first=True)
            with dve.Fori(0, TURNS - 1) as t:
                for u in range(1, UNITS + 1):
                    unit(t, u)
            for u in range(1, UNITS):
                unit(TURNS - 1, u, more=u + 1 < UNITS)


def swiglu_stage(nc, name, K, X, XN, blocks, up_dram, down_dram, HID=None, gate_dram=None, expert_dram=None, before_dram=None):
    LOADS = 5
    TT = N // P
    with ExitStack() as ctx:
        signals = ctx.enter_context(Signals(nc))
        def sb(n, shape):
            return ctx.enter_context(nc.sbuf_tensor(f"{name}_{n}", shape, F32))

        def sem(n):
            return signals(f"{name}_{n}")

        def tally(n, per):
            return Tally(sem(n), per)

        up = sb("up", [P, blocks, KC, 2, P])
        down = sb("down", [P, blocks, C])
        silu, hid = sb("silu", [P, 2, TILE]), sb("hid", [P, 2, TILE])
        ps_g, ps_u, ps_w, ps_out = ([ctx.enter_context(nc.psum_tensor(f"{name}_{n}{i}", [P, TILE], F32)) for i in range(2)] for n in "guwo")
        edges = [blocks * i // LOADS for i in range(LOADS + 1)]
        loads = [sem(f"load{i}") for i in range(LOADS)]
        gate_lin, up_lin, weigh_lin, silud, made = (tally(n, blocks) for n in ("gate_lin", "up_lin", "weigh_lin", "silud", "made"))
        weighed, used = tally("weighed", blocks), tally("used", blocks)
        added = tally("added", KC)
        if HID is not None:
            added_hid = tally("added_hid", KC)
            gate_w = sb("gate_w", [P, KC, E])
            expert_of = sb("expert_of", [SELROWS, blocks, P])
            earlier = sb("earlier", [P, E, E])
            logit, expo, weight = (sb(n, [P, TT, E]) for n in ("logit", "expo", "weight"))
            greater, equal = (sb(n, [P, TT, E, E]) for n in ("greater", "equal"))
            rank = sb("rank", [P, TT, E])
            top, total, inv = (sb(n, [P, TT]) for n in ("top", "total", "inv"))
            route = sb("route", [P, TT, SELROWS])
            routeT = sb("routeT", [SELROWS, N])
            router_in, logits, exps, routed, routeT_ready = (sem(n) for n in ("router_in", "logits", "exps", "routed", "routeT_ready"))
            chain = sem("chain")
        block = ctx.enter_context(nc.Block())

        @block.sync
        def _(sp):
            if HID is not None:
                sp.dma_start(gate_w[:], gate_dram[:]).then_inc(router_in, 16)
                sp.dma_start(expert_of[:], expert_dram[:]).then_inc(router_in, 16)
                sp.dma_start(earlier[:], before_dram[:]).then_inc(router_in, 16)
            for i in range(LOADS):
                a, z = edges[i], edges[i + 1]
                sp.dma_start(up[:, a:z], up_dram[:, a:z]).then_inc(loads[i], 16)
                sp.dma_start(down[:, a:z], down_dram[:, a:z]).then_inc(loads[i], 16)

        @block.tensor
        def _(pe):
            for x in (gate_lin, up_lin, weigh_lin, used):
                x.prime(pe)
            if HID is not None:
                pe.wait_ge(router_in, 48)
                for t in range(TT):
                    for c in range(KC):
                        mm = nc.tensor.matmul(ps_w[0][:, t * E:(t + 1) * E], XN[:, c, t * P:(t + 1) * P], gate_w[:, c, :], start=c == 0, stop=c == KC - 1)
                mm.then_inc(logits, 1)
                pe.wait_ge(routed, 1)
                for g in range(NT):
                    out = (ps_w[1], ps_g[0], ps_g[1], ps_u[0])[g]
                    for t in range(TILE // P):
                        mm = nc.tensor.transpose(out[0:SELROWS, t * P:(t + 1) * P], route[:, g * (TILE // P) + t, :], K.mats[:, EYE, :])
                    mm.then_inc(logits, 1)
                pe.wait_ge(routeT_ready, NT)
            for i in range(LOADS):
                pe.wait_ge(loads[i], 32)
            with pe.Fori(0, NT) as t:
                def free(tl, j):
                    pe.wait_ge(*(tl.now(t, j - 1) if j >= 2 else tl.last(t, blocks - 1 + j)))

                def open_(j):
                    free(silud, j)
                    for c in range(KC):
                        mm = nc.tensor.matmul(ps_g[j % 2][:], up[:, j, c, 0, :], XN[:, c, bass.ds(t * TILE, TILE)], start=c == 0, stop=c == KC - 1)
                    mm.then_inc(gate_lin.sem, 1)
                    free(made if HID is None else weighed, j)
                    for c in range(KC):
                        mm = nc.tensor.matmul(ps_u[j % 2][:], up[:, j, c, 1, :], XN[:, c, bass.ds(t * TILE, TILE)], start=c == 0, stop=c == KC - 1)
                    mm.then_inc(up_lin.sem, 1)
                    if HID is not None:
                        nc.tensor.matmul(ps_w[j % 2][:], expert_of[:, j, :], routeT[:, bass.ds(t * TILE, TILE)], start=True, stop=True).then_inc(weigh_lin.sem, 1)

                def close(j):
                    pe.wait_ge(*(weighed if HID is not None else made).now(t, j + 1))
                    if j == 0:
                        pe.wait_ge(*added.last(t))
                    for m in range(KC):
                        mm = nc.tensor.matmul(ps_out[m][:], down[:, j, m * P:(m + 1) * P], hid[:, j % 2, :], start=j == 0, stop=j == blocks - 1)
                    mm.then_inc(used.sem, 1)

                open_(0)
                for j in range(1, blocks):
                    open_(j)
                    close(j - 1)
                close(blocks - 1)

        @block.scalar
        def _(act):
            silud.prime(act)
            if HID is not None:
                act.wait_ge(chain, 2)
                nc.scalar.activation(expo[:], expo[:], ACT.Exp).then_inc(exps, 1)
                for g in range(NT):
                    act.wait_ge(logits, 2 + g)
                    src = (ps_w[1], ps_g[0], ps_g[1], ps_u[0])[g]
                    nc.scalar.activation(routeT[:, g * TILE:(g + 1) * TILE], src[0:SELROWS, :], ACT.Copy).then_inc(routeT_ready, 1)
            with act.Fori(0, NT) as t:
                for j in range(blocks):
                    act.wait_ge(*gate_lin.now(t, j + 1))
                    act.wait_ge(*(made.now(t, j - 1) if j >= 2 else made.last(t, blocks - 1 + j)))
                    nc.scalar.activation(silu[:, j % 2, :], ps_g[j % 2][:], ACT.Silu).then_inc(silud.sem, 1)

        @block.vector
        def _(dve):
            for x in [made, weighed, added] + ([added_hid] if HID is not None else []):
                x.prime(dve)
            if HID is not None:
                steps = [0]

                def link(ins):
                    steps[0] += 1
                    ins.then_inc(chain, 1)
                    dve.wait_ge(chain, steps[0])

                dve.wait_ge(logits, 1)
                dve.wait_ge(router_in, 48)
                all_logits = ps_w[0][:, 0:TT * E].rearrange("p (t e) -> p t e", e=E)
                link(nc.vector.tensor_reduce(top[:], all_logits, AXX, ALU.max))
                link(nc.vector.tensor_tensor(expo[:], all_logits, bcast(top[:], 2, E), ALU.subtract))
                link(nc.vector.tensor_copy(logit[:], all_logits))
                other, own = bcast(logit[:], 2, E), bcast(logit[:], 3, E)
                nc.vector.tensor_tensor(greater[:], other, own, ALU.is_gt)
                link(nc.vector.tensor_tensor(equal[:], other, own, ALU.is_equal))
                link(nc.vector.tensor_tensor(equal[:], equal[:], bcast(earlier[:], 1, TT), ALU.mult))
                link(nc.vector.tensor_tensor(greater[:], greater[:], equal[:], ALU.add))
                link(nc.vector.tensor_reduce(rank[:], greater[:], AXX, ALU.add))
                dve.wait_ge(exps, 1)
                link(nc.vector.scalar_tensor_tensor(weight[:], rank[:], float(TOPK) - 0.5, expo[:], ALU.is_lt, ALU.mult))
                link(nc.vector.tensor_reduce(total[:], weight[:], AXX, ALU.add))
                link(nc.vector.reciprocal(inv[:], total[:]))
                link(nc.vector.memset(route[:, :, E:SELROWS], 1.0))
                nc.vector.tensor_tensor(route[:, :, 0:E], weight[:], bcast(inv[:], 2, E), ALU.mult).then_inc(routed, 1)
            with dve.Fori(0, NT) as t:
                for j in range(blocks):
                    dve.wait_ge(*up_lin.now(t, j + 1))
                    dve.wait_ge(*silud.now(t, j + 1))
                    dve.wait_ge(*(used.now(t, j - 1) if j >= 2 else used.last(t, blocks - 1 + j)))
                    nc.vector.tensor_tensor(hid[:, j % 2, :], silu[:, j % 2, :], ps_u[j % 2][:], ALU.mult).then_inc(made.sem, 1)
                    if HID is not None:
                        dve.wait_ge(*weigh_lin.now(t, j + 1))
                        dve.wait_ge(*made.now(t, j + 1))
                        nc.vector.tensor_tensor(hid[:, j % 2, :], hid[:, j % 2, :], ps_w[j % 2][:], ALU.mult).then_inc(weighed.sem, 1)
                dve.wait_ge(*used.now(t))
                for m in range(KC):
                    part = X[:, m, bass.ds(t * TILE, TILE)]
                    nc.vector.tensor_tensor(part, part, ps_out[m][:], ALU.add).then_inc(added.sem, 1)
                if HID is not None:
                    for m in range(KC):
                        part = X[:, m, bass.ds(t * TILE, TILE)]
                        dve.wait_ge(*added.now(t, m + 1))
                        nc.vector.tensor_tensor(part, part, HID[:, m, bass.ds(t * TILE, TILE)], ALU.add).then_inc(added_hid.sem, 1)

def delta_inputs_stage(nc, K, XN, F1, f1_dram, b_dram, beta_dram):
    with ExitStack() as ctx:
        signals = ctx.enter_context(Signals(nc))
        w_f1 = ctx.enter_context(nc.sbuf_tensor("dp_w_f1", [P, KC, P], F32))
        w_b = ctx.enter_context(nc.sbuf_tensor("dp_w_b", [P, KC, HEADS], F32))
        beta = ctx.enter_context(nc.sbuf_tensor("dp_beta", [HEADS, N], F32))
        ps_f = [ctx.enter_context(nc.psum_tensor(f"dp_f{t}", [P, TILE], F32)) for t in range(NT)]
        ps_b = [ctx.enter_context(nc.psum_tensor(f"dp_b{t}", [P, TILE], F32)) for t in range(NT)]
        w_in, lin, f1_got, beta_got, stored = (signals("dp_" + n) for n in ("w_in", "lin", "f1_got", "beta_got", "stored"))
        block = ctx.enter_context(nc.Block())

        @block.sync
        def _(sp):
            sp.dma_start(w_f1[:], f1_dram[:]).then_inc(w_in, 16)
            sp.dma_start(w_b[:], b_dram[:]).then_inc(w_in, 16)
            sp.wait_ge(beta_got, NT)
            sp.dma_start(beta_dram[:], beta[:]).then_inc(stored, 16)
            sp.wait_ge(stored, 16)

        @block.tensor
        def _(pe):
            pe.wait_ge(w_in, 32)
            for t in range(NT):
                for c in range(KC):
                    mm = nc.tensor.matmul(ps_b[t][0:HEADS, :], w_b[:, c, :], XN[:, c, t * TILE:(t + 1) * TILE], start=c == 0, stop=c == KC - 1)
                mm.then_inc(lin, 1)
            for t in range(NT):
                for c in range(KC):
                    mm = nc.tensor.matmul(ps_f[t][:], w_f1[:, c, :], XN[:, c, t * TILE:(t + 1) * TILE], start=c == 0, stop=c == KC - 1)
                mm.then_inc(lin, 1)

        @block.scalar
        def _(act):
            for t in range(NT):
                act.wait_ge(lin, t + 1)
                nc.scalar.activation(beta[:, t * TILE:(t + 1) * TILE], ps_b[t][0:HEADS, :], ACT.Sigmoid).then_inc(beta_got, 1)
            for t in range(NT):
                act.wait_ge(lin, NT + t + 1)
                nc.scalar.activation(F1[:, t * TILE:(t + 1) * TILE], ps_f[t][:], ACT.Copy).then_inc(f1_got, 1)


class PairTally:

    def __init__(self, sem, per):
        self.sem, self.per = sem, per

    def prime(self, eng):
        eng.sem_inc(self.sem, 3 * self.per)

    def at(self, head, off, n=None):
        return self.sem, head * (2 * self.per) + ((off + 3) * self.per + (self.per if n is None else n))


def delta_stage(nc, K, X, XN, dram):
    PB = B // 2
    PT = PB * T
    G = PB * NC_
    HALF = CH // 2
    STEPS = LEVELS + 2
    TURNS = HEADS
    (Q0, K0, V0, G0, QS0, KS0, VT0, GT0) = range(0, 16, 2)
    with ExitStack() as ctx:
        signals = ctx.enter_context(Signals(nc))
        def sb(n, shape):
            return ctx.enter_context(nc.sbuf_tensor("dl_" + n, shape, F32))

        def pb(n):
            return ctx.enter_context(nc.psum_tensor("dl_" + n, [P, TILE], F32))

        F1 = sb("F1", [P, N])
        beta_dram = nc.dram_tensor("beta_rows", [HEADS, N], F32, kind="Internal").ap()
        delta_inputs_stage(nc, K, XN, F1, dram["delta_f1"], dram["delta_b"], beta_dram)

        all_tallies = {}

        def tallies(engine, **per):
            made = {n: PairTally(signals("dl_" + n), c) for n, c in per.items()}
            all_tallies.setdefault(engine, []).extend(made.values())
            return made.values()

        w_p = sb("w_p", [P, 4, KC, P])
        w_f2 = sb("w_f2", [P, P])
        w_c = sb("w_c", [P, H_COLS])
        w_o = sb("w_o", [P, C])
        beta = sb("beta", [P, N])
        level_mask = sb("level_mask", [P, LEVELS, HALF])
        raw = sb("raw", [P, 3, T])
        kq = [sb(f"kq{p}", [P, 2, PT]) for p in range(2)]
        ks = [sb(f"ks{p}", [P, PT]) for p in range(2)]
        dec = [[sb(f"dec{p}_{l}", [P, PT >> l]) for l in range(LEVELS + 1)] for p in range(2)]
        vc = sb("vc", [P, PT])
        vtok = [sb(f"vtok{p}", [P, G, P]) for p in range(2)]
        gate_raw = [sb(f"gate_raw{p}", [P, PT]) for p in range(2)]
        gate = sb("gate", [P, PT])
        y = sb("y", [P, 2, PT])
        norm = sb("norm", [P, 4, T])
        soft, softln, relu, less = (sb(n, [P, PB, T]) for n in ("soft", "softln", "relu", "less"))
        nega = sb("nega", [P, 2])
        mt = [sb(f"mt{i}", [P, G, CH]) for i in range(2)]
        z, tm = sb("z", [P, G, CH]), sb("tm", [P, G, CH])
        tt = [sb(f"tt{p}", [P, G, CH]) for p in range(2)]
        bt = [sb(f"bt{p}", [P, G, CH]) for p in range(2)]
        kst = sb("kst", [P, G, P])
        r, u, state = (sb(n, [P, PB, P]) for n in ("r", "u", "state"))
        o = sb("o", [P, PB, T])
        onorm = sb("onorm", [P, PB, T])
        bank_a, bank_k, bank_t, bank_c = ([pb(f"{n}{i}") for i in range(2)] for n in "aktc")

        a_lin, b_kk, b_turned, b_zl, b_tl, c_kt, c_rl, c_ul, c_ol, c_sl, c_nl, c_wl = tallies(
            "pe", a_lin=16, b_kk=2 * (LEVELS + 1), b_turned=2 * (LEVELS - 2), b_zl=2 * LEVELS, b_tl=2 * (LEVELS - 1), c_kt=PB, c_rl=NC_ - 1, c_ul=NC_, c_ol=NC_,
            c_sl=NC_ - 1, c_nl=PB, c_wl=PB * KC)
        (a_took, a_silu, a_sq, a_rs, a_abs, a_soft, a_ln, a_nega, a_dec, b_init, b_tt, b_zed, c_kst, c_gs, c_u, c_o, c_sq, c_log, c_rs) = tallies(
            "act", a_took=16, a_silu=6, a_sq=4, a_rs=4, a_abs=PB, a_soft=PB, a_ln=PB, a_nega=2, a_dec=PB, b_init=2, b_tt=2 * (LEVELS - 2), b_zed=2 * (LEVELS - 1),
            c_kst=PB, c_gs=PB, c_u=NC_, c_o=NC_, c_sq=PB, c_log=PB, c_rs=PB)
        a_conv, a_less, b_m, b_got, b_tm, b_tt_ends, c_r, c_s, c_nrm, c_add = tallies(
            "dve", a_conv=6 * KTAPS, a_less=PB, b_m=2 * LEVELS, b_got=2 * (LEVELS + 1), b_tm=2 * (LEVELS - 1), b_tt_ends=4, c_r=NC_ - 1,
            c_s=PB * (NC_ - 1), c_nrm=PB, c_add=PB * KC)
        a_sp, a_nrm, a_nrm_k, a_ks, b_kq, b_ks, b_dec, c_gate = tallies(
            "pool", a_sp=3 * PB, a_nrm=PB, a_nrm_k=PB, a_ks=PB, b_kq=2 * (LEVELS + 1), b_ks=2 * LEVELS, b_dec=2 * LEVELS, c_gate=PB)
        w_in = Tally(signals("dl_w_in"), 48)
        w_o_in = Tally(signals("dl_w_o_in"), 16)
        beta_in = Tally(signals("dl_beta_in"), 16)
        mask_in = signals("dl_mask_in")
        cleared = signals("dl_cleared")
        block = ctx.enter_context(nc.Block())
        eye, ones, mean = K.mats[:, EYE, :], K.mats[:, ONES, :], K.mats[:, MEAN_P, :]
        zero, eps5, eps6, qscale = (K.small[:, n:n + 1] for n in (ZERO, EPS5, EPS6, QSCALE))

        CLEAR = (mt[0], mt[1], z)
        CLEARED = len(CLEAR)

        def tok(b):
            return slice(b * T, (b + 1) * T)

        def chunks(ap, b):
            return ap[:, b * NC_:(b + 1) * NC_]

        def half_cols(ap, b, l, second):
            half = 1 << l
            return chunks(ap, b).rearrange("p g (n two h) -> p g n two h", two=2, h=half)[:, :, :, second, :]

        def half_flat(ap, b, l, second):
            half = 1 << l
            return chunks(ap, b).rearrange("p g (n two h) -> p (g n) two h", two=2, h=half)[:, :, second, :]

        @block.sync
        def _(sp):
            w_in.prime(sp)
            beta_in.prime(sp)
            w_o_in.prime(sp)
            w = dram["delta_w"]

            def load_projections(head):
                def row(a, z):
                    return w[bass.ds(head, 1), :, a:z].rearrange("o p n -> p (o n)")
                a, z = 4 * KC * P, 4 * KC * P + P
                sp.dma_start(w_p[:].rearrange("p m c n -> p (m c n)"), row(0, a)).then_inc(w_in.sem, 16)
                sp.dma_start(w_f2[:], row(a, z)).then_inc(w_in.sem, 16)
                sp.dma_start(w_c[:], row(z + C, z + C + H_COLS)).then_inc(w_in.sem, 16)

            def load_output_weights(head):
                sp.dma_start(w_o[:], w[bass.ds(head, 1), :, 4 * KC * P + P:4 * KC * P + P + C].rearrange("o p n -> p (o n)")).then_inc(w_o_in.sem, 16)

            def load_beta(head):
                sp.dma_start(beta[:], beta_dram[bass.ds(head, 1), :].broadcast_to([P, N])).then_inc(beta_in.sem, 16)

            sp.dma_start(level_mask[:], dram["level_mask"][:]).then_inc(mask_in, 16)
            load_projections(0)
            load_beta(0)
            load_output_weights(0)
            with sp.Fori(0, TURNS - 1) as h:
                sp.wait_ge(*a_lin.at(h, 1))
                sp.wait_ge(*a_dec.at(h, 1))
                sp.wait_ge(*a_took.at(h, 1))
                sp.wait_ge(*a_conv.at(h, 1))
                load_projections(h + 1)
                sp.wait_ge(*a_ks.at(h, 1))
                load_beta(h + 1)
                sp.wait_ge(*c_wl.at(h, 1))
                load_output_weights(h + 1)

        @block.tensor
        def _(pe):
            for x in all_tallies["pe"]:
                x.prime(pe)

            def A(h, off, s, k):
                p = off % 2
                if s == 0 and k == 0 and p == 0:
                    pe.wait_ge(*w_in.now(h + off // 2 if off > 1 else h))
                order = [Q0, K0, V0, G0, QS0, KS0, VT0, GT0, None]
                e0 = order[s]
                if e0 is None or k > 1:
                    return
                e, b = e0 + k, k
                gb = p * PB + b
                if e >= 2:
                    pe.wait_ge(*a_took.at(h, off, e - 1))
                else:
                    pe.wait_ge(*a_took.at(h, off - 1, 15 + e))
                out = bank_a[b]
                if e0 in (Q0, K0, V0, GT0):
                    for c in range(KC):
                        mm = nc.tensor.matmul(out[:], w_p[:, min(e0 // 2, 3), c, :], XN[:, c, gb * T:(gb + 1) * T], start=c == 0, stop=c == KC - 1)
                elif e0 == G0:
                    mm = nc.tensor.matmul(out[:], w_f2[:], F1[:, gb * T:(gb + 1) * T], start=True, stop=True)
                elif e0 in (QS0, KS0):
                    n = e - QS0
                    pe.wait_ge(*a_sq.at(h, off, n + 1))
                    mm = nc.tensor.matmul(out[:], ones, norm[:, n, :], start=True, stop=True)
                else:
                    pe.wait_ge(*a_silu.at(h, off, 5 + b))
                    for c in range(NC_):
                        mm = nc.tensor.transpose(out[:, c * P:(c + 1) * P], vc[:, b * T + c * P:b * T + (c + 1) * P], eye)
                mm.then_inc(a_lin.sem, 1)

            def Bp(h, off, s, k):
                p = off % 2
                if k == 0 and s <= LEVELS:
                    for b in range(PB):
                        n = 2 * s + b
                        if s == 0:
                            pe.wait_ge(*a_ks.at(h, off, b + 1))
                            pe.wait_ge(*a_nrm.at(h, off, b + 1))
                            pe.wait_ge(*b_got.at(h, off - 1, 2 * LEVELS + b + 1))
                        else:
                            pe.wait_ge(*b_kq.at(h, off, n - 1))
                            if s >= 2:
                                pe.wait_ge(*b_ks.at(h, off, n - 3))
                            pe.wait_ge(*b_got.at(h, off, n - 1))
                        for c in range(NC_):
                            at = slice(b * T + c * CH, b * T + (c + 1) * CH)
                            if s == 0:
                                mm = nc.tensor.matmul(bank_k[b][:, c * CH:(c + 1) * CH], ks[p][:, at], kq[p][:, 1, at], start=True, stop=True)
                            else:
                                second = kq[p][:, :, at].rearrange("p m (n two h) -> p m n two h", two=2, h=1 << s - 1)[:, :, :, 1, :]
                                mm = nc.tensor.matmul(bank_k[b][:, c * CH:(c + 1) * CH], ks[p][:, at], second, start=True, stop=True)
                        mm.then_inc(b_kk.sem, 1)
                l = s - 2
                if k == 0 and l >= 2:
                    for b in range(PB):
                        pe.wait_ge(*b_tm.at(h, off, 2 * (l - 1) + b + 1))
                        for c in range(NC_):
                            mm = nc.tensor.transpose(bank_t[b][:, c * CH:(c + 1) * CH], chunks(tm, b)[:, c, :], eye)
                        mm.then_inc(b_turned.sem, 1)
                if k == 1 and l >= 0:
                    for b in range(PB):
                        n = 2 * l + b
                        pe.wait_ge(*b_m.at(h, off, n + 1))
                        if l == 0:
                            pe.wait_ge(*b_tt_ends.at(h, off - 1, 2 + b + 1))
                            for c in range(NC_):
                                mm = nc.tensor.transpose(bank_t[b][:, c * CH:(c + 1) * CH], chunks(mt[0], b)[:, c, :], eye)
                            mm.then_inc(b_zl.sem, 1)
                            continue
                        if l == 1:
                            pe.wait_ge(*b_tt_ends.at(h, off, b + 1))
                            pe.wait_ge(*b_tm.at(h, off, b + 1))
                        else:
                            pe.wait_ge(*b_tt.at(h, off, 2 * (l - 2) + b + 1))
                        firsts = half_cols(tm, b, l, 0)
                        for c in range(NC_):
                            mm = nc.tensor.matmul(bank_t[b][:, c * HALF:(c + 1) * HALF], chunks(mt[l % 2], b)[:, c, :], firsts[:, c], start=True, stop=True)
                        mm.then_inc(b_zl.sem, 1)
                if k == 2 and l >= 1:
                    for b in range(PB):
                        n = 2 * (l - 1) + b
                        pe.wait_ge(*b_zed.at(h, off, n + 1))
                        zf, ts = half_cols(z, b, l, 0), half_cols(tt[p], b, l, 1)
                        for c in range(NC_):
                            if l < LEVELS - 1:
                                mm = nc.tensor.matmul(bank_t[b][:, c * HALF:(c + 1) * HALF], chunks(tt[p], b)[:, c, :], zf[:, c], start=True, stop=True)
                            else:
                                mm = nc.tensor.matmul(bank_t[b][:, (NC_ + c) * HALF:(NC_ + c + 1) * HALF], chunks(z, b)[:, c, :], ts[:, c], start=True, stop=True)
                        mm.then_inc(b_tl.sem, 1)

            def Cp(h, off, s, k):
                p = off % 2
                ci = s - 1
                if s == 0 and k < PB:
                    b = k
                    pe.wait_ge(*b_ks.at(h, off, 2 * (LEVELS - 1) + b + 1))
                    pe.wait_ge(*c_add.at(h, off - 1, PB * KC - 1 + b))
                    for c in range(NC_):
                        mm = nc.tensor.transpose(bank_c[b][:, c * P:(c + 1) * P], ks[p][:, b * T + c * P:b * T + (c + 1) * P], eye)
                    mm.then_inc(c_kt.sem, 1)
                if 0 <= ci < NC_:
                    def at(b):
                        return slice(b * T + ci * CH, b * T + (ci + 1) * CH)
                    if k == 0 and ci == 0:
                        pe.wait_ge(*b_kq.at(h, off))
                        pe.wait_ge(*b_tt_ends.at(h, off))
                        pe.wait_ge(*a_took.at(h, off))
                    if k == 0 and ci > 0:
                        pe.wait_ge(*c_s.at(h, off, PB * ci))
                        pe.wait_ge(*c_o.at(h, off, ci))
                        for b in range(PB):
                            mm = nc.tensor.matmul(bank_c[0][:, b * P:(b + 1) * P], kq[p][:, 0, at(b)], state[:, b, :], start=True, stop=True)
                        mm.then_inc(c_rl.sem, 1)
                    if k == 1:
                        if ci > 0:
                            pe.wait_ge(*c_r.at(h, off, ci))
                        else:
                            pe.wait_ge(*c_kst.at(h, off, 2))
                        for b in range(PB):
                            mm = nc.tensor.matmul(bank_c[1][:, b * P:(b + 1) * P], chunks(tt[p], b)[:, ci, :], r[:, b, :] if ci else chunks(vtok[p], b)[:, ci, :],
                                                  start=True, stop=True)
                        mm.then_inc(c_ul.sem, 1)
                    if k == 2:
                        pe.wait_ge(*c_u.at(h, off, ci + 1))
                        if ci == 0:
                            pe.wait_ge(*c_kst.at(h, off, 1))
                        if ci < NC_ - 1:
                            for b in range(PB):
                                mm = nc.tensor.matmul(bank_c[1][:, b * P:(b + 1) * P], chunks(kst, b)[:, ci, :], u[:, b, :], start=True, stop=True)
                            mm.then_inc(c_sl.sem, 1)
                        for b in range(PB):
                            if ci:
                                nc.tensor.matmul(bank_c[0][:, b * P:(b + 1) * P], state[:, b, :], kq[p][:, 1, at(b)], start=True, stop=False)
                            mm = nc.tensor.matmul(bank_c[0][:, b * P:(b + 1) * P], u[:, b, :], chunks(bt[p], b)[:, ci, :], start=ci == 0, stop=True)
                        mm.then_inc(c_ol.sem, 1)
                if s == NC_ + 1 and k < PB:
                    b = k
                    pe.wait_ge(*c_sq.at(h, off, b + 1))
                    nc.tensor.matmul(bank_c[b][:], mean, onorm[:, b, :], start=True, stop=True).then_inc(c_nl.sem, 1)
                if s in (NC_ + 2, NC_ + 3) and k < KC:
                    b, m = s - NC_ - 2, k
                    n = b * KC + m
                    pe.wait_ge(*c_gate.at(h, off, b + 1))
                    if n == 0:
                        pe.wait_ge(*w_o_in.now(h))
                    if n < 2:
                        pe.wait_ge(*c_log.at(h, off, n + 1))
                    else:
                        pe.wait_ge(*c_add.at(h, off, n - 1))
                    nc.tensor.matmul(bank_c[m][:], w_o[:, m * P:(m + 1) * P], o[:, b, :], start=True, stop=True).then_inc(c_wl.sem, 1)

            def steps(h, a=None, b=None, c=None):
                for s in range(STEPS):
                    for k in range(3):
                        if b is not None:
                            Bp(h, b, s, k)
                        if c is not None:
                            Cp(h, c, s, k)
                        if a is not None:
                            A(h, a, s, k)

            steps(0, a=0)
            steps(0, a=1, b=0)
            with pe.Fori(0, TURNS - 1) as h:
                steps(h, a=2, b=1, c=0)
                steps(h, a=3, b=2, c=1)
            steps(TURNS - 1, b=1, c=0)
            steps(TURNS - 1, c=1)

        @block.scalar
        def _(act):
            for x in all_tallies["act"]:
                x.prime(act)

            def column(n):
                return w_c[:, n:n + 1]

            def A(h, off, s, k):
                p = off % 2
                b = k
                def take(e):
                    act.wait_ge(*a_lin.at(h, off, e + 1))
                if s == 0 and k == 0 and p == 0:
                    act.wait_ge(*w_in.now(h + off // 2 if off > 1 else h))
                if s <= 2 and k < PB:
                    n = 2 * s + b
                    take(n)
                    if n >= 3:
                        act.wait_ge(*a_conv.at(h, off, KTAPS * (n - 2)))
                    else:
                        act.wait_ge(*a_conv.at(h, off - 1, KTAPS * (n + 4)))
                    nc.scalar.activation(raw[:, n % 3, :], bank_a[b][:], ACT.Copy).then_inc(a_took.sem, 1)
                if 1 <= s <= 3 and k < PB:
                    n = 2 * (s - 1) + b
                    act.wait_ge(*a_conv.at(h, off, KTAPS * (n + 1)))
                    body = (y[:, 1, tok(b)], y[:, 0, tok(b)], vc[:, tok(b)])[s - 1]
                    nc.scalar.activation(body, body, ACT.Silu).then_inc(a_silu.sem, 1)
                    if s <= 2:
                        act.wait_ge(*a_silu.at(h, off, n + 1))
                        act.wait_ge(*(a_nrm, a_nrm_k)[s - 1].at(h, off - 1, b + 1))
                        nc.scalar.activation(norm[:, n, :], body, ACT.Square).then_inc(a_sq.sem, 1)
                if s == 3 and k < PB:
                    take(G0 + b)
                    act.wait_ge(*a_dec.at(h, off - 1, b + 1))
                    nc.scalar.activation(soft[:, b, :], bank_a[b][:], ACT.Abs, bias=column(H_DT)).then_inc(a_abs.sem, 1)
                    act.wait_ge(*a_sp.at(h, off - 1))
                    nc.scalar.activation(relu[:, b, :], bank_a[b][:], ACT.Relu, bias=column(H_DT)).then_inc(a_took.sem, 1)
                if s in (4, 5) and k < PB:
                    n = 2 * (s - 4) + b
                    take(QS0 + n)
                    nc.scalar.activation(norm[:, n, :], bank_a[b][:], ACT.Ln, bias=eps6).then_inc(a_took.sem, 1)
                    act.wait_ge(*a_took.at(h, off, QS0 + n + 1))
                    nc.scalar.activation(norm[:, n, :], norm[:, n, :], ACT.Exp, scale=-0.5, bias=(qscale, zero)[s - 4]).then_inc(a_rs.sem, 1)
                if s == 4 and k < PB:
                    act.wait_ge(*a_abs.at(h, off, b + 1))
                    nc.scalar.activation(soft[:, b, :], soft[:, b, :], ACT.Exp, scale=-1.0).then_inc(a_soft.sem, 1)
                    act.wait_ge(*a_soft.at(h, off, b + 1))
                    nc.scalar.activation(softln[:, b, :], soft[:, b, :], ACT.Ln, bias=K.small[:, ONE:ONE + 1]).then_inc(a_ln.sem, 1)
                if s == 4 and k == 2:
                    act.wait_ge(*a_dec.at(h, off - 1))
                    nc.scalar.activation(nega[:, 0:1], column(H_ALOG), ACT.Exp).then_inc(a_nega.sem, 1)
                    act.wait_ge(*a_nega.at(h, off, 1))
                    nc.scalar.activation(nega[:, 1:2], nega[:, 0:1], ACT.Copy, scale=-1.0).then_inc(a_nega.sem, 1)
                if s == 6 and k < PB:
                    take(VT0 + b)
                    act.wait_ge(*c_r.at(h, off - 2))
                    act.wait_ge(*c_ul.at(h, off - 2, 1))
                    nc.scalar.activation(chunks(vtok[p], b).rearrange("p g n -> p (g n)"), bank_a[b][:], ACT.Copy).then_inc(a_took.sem, 1)
                    act.wait_ge(*a_nega.at(h, off))
                    act.wait_ge(*a_sp.at(h, off, 3 * (b + 1)))
                    act.wait_ge(*b_dec.at(h, off - 2, 2 + b))
                    act.wait_ge(*b_ks.at(h, off - 2, 2 + b))
                    act.wait_ge(*b_kq.at(h, off - 2, 4))
                    nc.scalar.activation(dec[p][0][:, tok(b)], soft[:, b, :], ACT.Exp, scale=nega[:, 1:2]).then_inc(a_dec.sem, 1)
                if s == 7 and k < PB:
                    take(GT0 + b)
                    act.wait_ge(*c_gs.at(h, off - 2, b + 1))
                    nc.scalar.activation(gate_raw[p][:, tok(b)], bank_a[b][:], ACT.Identity, bias=column(H_BG)).then_inc(a_took.sem, 1)

            def Bp(h, off, s, k):
                p = off % 2
                l = s - 2
                if s == 1 and k == 2:
                    act.wait_ge(*b_tl.at(h, off - 1))
                    act.wait_ge(*b_zl.at(h, off - 1))
                    nc.scalar.activation(tm[:], bcast(eye, 1, G), ACT.Copy).then_inc(b_init.sem, 1)
                    act.wait_ge(*c_ul.at(h, off - 2))
                    nc.scalar.activation(tt[p][:], bcast(eye, 1, G), ACT.Copy).then_inc(b_init.sem, 1)
                if k == 0 and l >= 2:
                    for b in range(PB):
                        act.wait_ge(*b_turned.at(h, off, 2 * (l - 2) + b + 1))
                        nc.scalar.activation(chunks(tt[p], b).rearrange("p g n -> p (g n)"), bank_t[b][:], ACT.Copy).then_inc(b_tt.sem, 1)
                if k == 1 and l >= 1:
                    for b in range(PB):
                        n = 2 * (l - 1) + b
                        act.wait_ge(*b_zl.at(h, off, 2 * l + b + 1))
                        act.wait_ge(*(b_tl.at(h, off, n - 1) if l > 1 else b_tl.at(h, off - 1)))
                        nc.scalar.activation(half_cols(z, b, l, 0), bank_t[b][:, 0:NC_ * HALF].rearrange("p (g n h) -> p g n h", g=NC_, h=1 << l),
                                             ACT.Copy, scale=K.small[:, ODD0 + l:ODD0 + l + 1]).then_inc(b_zed.sem, 1)

            def Cp(h, off, s, k):
                ci = s - 1
                if s == 0 and k < PB:
                    act.wait_ge(*c_kt.at(h, off, k + 1))
                    act.wait_ge(*c_sl.at(h, off - 1))
                    nc.scalar.activation(chunks(kst, k).rearrange("p g n -> p (g n)"), bank_c[k][:], ACT.Copy).then_inc(c_kst.sem, 1)
                if s == 1 and k < PB:
                    act.wait_ge(*a_took.at(h, off, GT0 + k + 1))
                    act.wait_ge(*c_gate.at(h, off - 1, k + 1))
                    nc.scalar.activation(gate[:, tok(k)], gate_raw[off % 2][:, tok(k)], ACT.Silu).then_inc(c_gs.sem, 1)
                if 0 <= ci < NC_ and k == 1:
                    act.wait_ge(*c_ul.at(h, off, ci + 1))
                    act.wait_ge(*(c_ol.at(h, off, ci) if ci else c_ol.at(h, off - 1)))
                    nc.scalar.activation(u[:].rearrange("p b n -> p (b n)"), bank_c[1][:, 0:PB * P], ACT.Copy).then_inc(c_u.sem, 1)
                if 0 <= ci < NC_ and k == 2:
                    act.wait_ge(*c_ol.at(h, off, ci + 1))
                    if ci == 0:
                        act.wait_ge(*c_wl.at(h, off - 1))
                    nc.scalar.activation(o[:, :, ci * CH:(ci + 1) * CH], bank_c[0][:, 0:PB * P].rearrange("p (b n) -> p b n", b=PB), ACT.Copy).then_inc(c_o.sem, 1)
                if s == NC_ and k == 2:
                    act.wait_ge(*c_o.at(h, off))
                    act.wait_ge(*c_nrm.at(h, off - 1))
                    for b in range(PB):
                        nc.scalar.activation(onorm[:, b, :], o[:, b, :], ACT.Square).then_inc(c_sq.sem, 1)
                if s == NC_ + 1 and k < PB:
                    b = k
                    act.wait_ge(*c_nl.at(h, off, b + 1))
                    nc.scalar.activation(onorm[:, b, :], bank_c[b][:], ACT.Ln, bias=eps5).then_inc(c_log.sem, 1)
                    act.wait_ge(*c_log.at(h, off, b + 1))
                    nc.scalar.activation(onorm[:, b, :], onorm[:, b, :], ACT.Exp, scale=-0.5).then_inc(c_rs.sem, 1)

            act.wait_ge(cleared, CLEARED)

            def logs_next(s, k):
                if s == 4 and k == 0:
                    nc.scalar.preload_act_table_set(LN_EXP)

            def steps(h, a=None, b=None, c=None):
                for s in range(STEPS):
                    for k in range(3):
                        logs_next(s, k)
                        if b is not None:
                            Bp(h, b, s, k)
                        if c is not None:
                            Cp(h, c, s, k)
                        if a is not None:
                            A(h, a, s, k)

            steps(0, a=0)
            steps(0, a=1, b=0)
            with act.Fori(0, TURNS - 1) as h:
                steps(h, a=2, b=1, c=0)
                steps(h, a=3, b=2, c=1)
            steps(TURNS - 1, b=1, c=0)
            steps(TURNS - 1, c=1)

        @block.vector
        def _(dve):
            for x in all_tallies["dve"]:
                x.prime(dve)
            for buf in CLEAR:
                nc.vector.memset(buf[:], 0.0).then_inc(cleared, 1)
            dve.wait_ge(cleared, CLEARED)
            dve.wait_ge(mask_in, 16)

            def A(h, off, s, k):
                p = off % 2
                if s <= 2 and k > 0:
                    b = k - 1
                    n = 2 * s + b
                    if n == 0 and p == 0:
                        dve.wait_ge(*w_in.now(h + off // 2 if off > 1 else h))
                    if s <= 1:
                        dve.wait_ge(*(a_nrm, a_nrm_k)[s].at(h, off - 1, b + 1))
                    if s == 2:
                        dve.wait_ge(*a_lin.at(h, off - 1, VT0 + b + 1))
                    body = (y[:, 1, tok(b)], y[:, 0, tok(b)], vc[:, tok(b)])[s]
                    taps = (H_CQ, H_CK, H_CV)[s]
                    x = raw[:, n % 3, :]
                    dve.wait_ge(*a_took.at(h, off, n + 1))
                    nc.vector.tensor_scalar(body, x, w_c[:, taps + KTAPS - 1:taps + KTAPS], None, ALU.mult).then_inc(a_conv.sem, 1)
                    for d in range(1, KTAPS):
                        dve.wait_ge(*a_conv.at(h, off, KTAPS * n + d))
                        tap = w_c[:, taps + KTAPS - 1 - d:taps + KTAPS - d]
                        nc.vector.scalar_tensor_tensor(body[:, d:T], x[:, 0:T - d], tap, body[:, d:T], ALU.mult, ALU.add).then_inc(a_conv.sem, 1)
                if s == 4 and k < PB:
                    b = k
                    dve.wait_ge(*a_soft.at(h, off, b + 1))
                    dve.wait_ge(*a_sp.at(h, off - 1, 3 * b + 1))
                    nc.vector.tensor_scalar(less[:, b, :], soft[:, b, :], 1.0, -1.0, ALU.add, ALU.add).then_inc(a_less.sem, 1)

            def Bp(h, off, s, k):
                p = off % 2
                l = s - 1
                if k == 0 and s <= LEVELS:
                    for b in range(PB):
                        dve.wait_ge(*b_kk.at(h, off, 2 * s + b + 1))
                        if s == 0:
                            if b == 0:
                                dve.wait_ge(*c_ol.at(h, off - 2))
                            nc.vector.tensor_tensor(chunks(bt[p], b), bank_k[b][:].rearrange("p (g n) -> p g n", g=NC_), bcast(eye, 1, NC_), ALU.mult).then_inc(b_got.sem, 1)
                            continue
                        both = bank_k[b][:].rearrange("p (g m n h) -> p g m n h", g=NC_, m=2, h=1 << l)
                        mask = bcast(level_mask[:, l, :].rearrange("p (n h) -> p n h", h=1 << l), 1, NC_)
                        n = 2 * l + b
                        if l == 2:
                            dve.wait_ge(*b_tt_ends.at(h, off, b + 1))
                        dve.wait_ge(*(b_zl.at(h, off, n - 3) if l >= 2 else b_zl.at(h, off - 1)))
                        dve.wait_ge(*b_got.at(h, off, n + 1))
                        nc.vector.tensor_tensor(half_cols(mt[l % 2], b, l, 1), both[:, :, 0], mask, ALU.mult).then_inc(b_m.sem, 1)
                        nc.vector.copy_predicated(half_cols(bt[p], b, l, 1), mask.bitcast(U32), both[:, :, 1]).then_inc(b_got.sem, 1)
                l = s - 2
                if k == 2 and l >= 0:
                    for b in range(PB):
                        n = 2 * l + b
                        if l == 0:
                            if b == 0:
                                dve.wait_ge(*b_init.at(h, off))
                            dve.wait_ge(*b_zl.at(h, off, b + 1))
                            turned = bank_t[b][:].rearrange("p (n two) -> p n two", two=2)[:, :, 0]
                            part = chunks(tm, b).rearrange("p g (n two) -> p (g n) two", two=2)[:, :, 0]
                            nc.vector.scalar_tensor_tensor(part, turned, K.small[:, ODD0:ODD0 + 1], part, ALU.mult, ALU.add).then_inc(b_tm.sem, 1)
                            part = chunks(tt[p], b).rearrange("p g (n two) -> p (g n) two", two=2)[:, :, 1]
                            m_ = chunks(mt[0], b).rearrange("p g (n two) -> p (g n) two", two=2)[:, :, 1]
                            nc.vector.tensor_tensor(part, part, m_, ALU.subtract).then_inc(b_tt_ends.sem, 1)
                            continue
                        dve.wait_ge(*b_tl.at(h, off, n - 1))
                        got = bank_t[b][:].rearrange("p (two g h) -> p two g h", two=2, h=1 << l)
                        if l < LEVELS - 1:
                            part = half_flat(tm, b, l, 0)
                            dve.wait_ge(*b_tm.at(h, off, n - 1))
                            nc.vector.tensor_tensor(part, part, got[:, 0], ALU.add).then_inc(b_tm.sem, 1)
                        else:
                            part = half_flat(tt[p], b, l, 1)
                            dve.wait_ge(*b_tt.at(h, off))
                            nc.vector.scalar_tensor_tensor(part, got[:, 1], K.small[:, EVEN0 + l:EVEN0 + l + 1], part, ALU.mult, ALU.add).then_inc(b_tt_ends.sem, 1)

            def Cp(h, off, s, k):
                p = off % 2
                ci = s - 1
                if 1 <= ci < NC_ and k == 0:
                    dve.wait_ge(*c_rl.at(h, off, ci))
                    dve.wait_ge(*(c_ul.at(h, off, ci) if ci > 1 else c_ul.at(h, off - 1)))
                    v_ = vtok[p][:].rearrange("p (b g) n -> p b g n", b=PB)[:, :, ci, :]
                    nc.vector.tensor_tensor(r[:], v_, bank_c[0][:, 0:PB * P].rearrange("p (b n) -> p b n", b=PB), ALU.subtract).then_inc(c_r.sem, 1)
                if 0 <= ci < NC_ - 1 and k == 2:
                    dve.wait_ge(*c_sl.at(h, off, ci + 1))
                    dve.wait_ge(*c_ol.at(h, off, ci + 1))
                    dve.wait_ge(*b_dec.at(h, off))
                    for b in range(PB):
                        src = bank_c[1][:, b * P:(b + 1) * P]
                        if ci == 0:
                            st = nc.vector.tensor_copy(state[:, b, :], src)
                        else:
                            if b == 0:
                                dve.wait_ge(*c_s.at(h, off, PB * ci))
                            g = b * NC_ + ci
                            st = nc.vector.scalar_tensor_tensor(state[:, b, :], state[:, b, :], dec[p][LEVELS][:, g:g + 1], src, ALU.mult, ALU.add)
                        st.then_inc(c_s.sem, 1)
                if s == NC_ + 1 and k < PB:
                    b = k
                    dve.wait_ge(*c_rs.at(h, off, b + 1))
                    nc.vector.scalar_tensor_tensor(o[:, b, :], o[:, b, :], w_on, onorm[:, b, :], ALU.mult, ALU.mult).then_inc(c_nrm.sem, 1)
                if s in (NC_ + 2, NC_ + 3) and k < KC:
                    b, m = s - NC_ - 2, k
                    dve.wait_ge(*c_wl.at(h, off, b * KC + m + 1))
                    dve.wait_ge(*c_add.at(h, off - 2, b * KC + m + 1))
                    gb = p * PB + b
                    part = X[:, m, gb * T:(gb + 1) * T]
                    nc.vector.tensor_tensor(part, part, bank_c[m][:], ALU.add).then_inc(c_add.sem, 1)

            w_on = K.vec[:, V_ON, 0:1]
            def steps(h, a=None, b=None, c=None):
                for s in range(STEPS):
                    for k in range(3):
                        if c is not None and k == 0:
                            Cp(h, c, s, k)
                        if b is not None:
                            Bp(h, b, s, k)
                        if c is not None and k > 0:
                            Cp(h, c, s, k)
                        if a is not None:
                            A(h, a, s, k)

            steps(0, a=0)
            steps(0, a=1, b=0)
            with dve.Fori(0, TURNS - 1) as h:
                steps(h, a=2, b=1, c=0)
                steps(h, a=3, b=2, c=1)
            steps(TURNS - 1, b=1, c=0)
            steps(TURNS - 1, c=1)

        @block.gpsimd
        def _(pool):
            for x in all_tallies["pool"]:
                x.prime(pool)

            def A(h, off, s, k):
                p = off % 2
                if s == 5 and k < PB:
                    b = k
                    pool.wait_ge(*a_less.at(h, off, b + 1))
                    pool.wait_ge(*a_ln.at(h, off, b + 1))
                    nc.gpsimd.tensor_tensor(soft[:, b, :], soft[:, b, :], less[:, b, :], ALU.subtract).then_inc(a_sp.sem, 1)
                    for n, more in ((1, softln), (2, relu)):
                        pool.wait_ge(*a_sp.at(h, off, 3 * b + n))
                        if n == 2:
                            pool.wait_ge(*a_took.at(h, off, G0 + b + 1))
                        nc.gpsimd.tensor_tensor(soft[:, b, :], soft[:, b, :], more[:, b, :], ALU.add).then_inc(a_sp.sem, 1)
                if s == 6 and k < PB:
                    for n in (0, 2):
                        m = 1 if n == 0 else 0
                        pool.wait_ge(*a_rs.at(h, off, n + k + 1))
                        pool.wait_ge(*c_ol.at(h, off - 2))
                        if n == 0:
                            nc.gpsimd.tensor_tensor(kq[p][:, m, tok(k)], y[:, m, tok(k)], norm[:, n + k, :], ALU.mult).then_inc(a_nrm.sem, 1)
                        else:
                            nc.gpsimd.tensor_tensor(kq[p][:, m, tok(k)], y[:, m, tok(k)], norm[:, n + k, :], ALU.mult).then_inc(a_nrm_k.sem, 1)
                if s == 7 and k < PB:
                    if k == 0 and p == 0:
                        pool.wait_ge(*beta_in.now(h + off // 2 if off > 1 else h))
                    pool.wait_ge(*a_nrm_k.at(h, off, k + 1))
                    pool.wait_ge(*c_kt.at(h, off - 2, k + 1))
                    nc.gpsimd.tensor_tensor(ks[p][:, tok(k)], kq[p][:, 0, tok(k)], beta[:, tok(p * PB + k)], ALU.mult).then_inc(a_ks.sem, 1)

            def Bp(h, off, s, k):
                p = off % 2
                if k == 0 and s <= LEVELS:
                    for b in range(PB):
                        l = s - 1
                        pool.wait_ge(*b_kk.at(h, off, 2 * s + b + 1))
                        both = kq[p][:, :, tok(b)]
                        if s == 0:
                            pool.wait_ge(*a_dec.at(h, off, b + 1))
                            pool.wait_ge(*a_ks.at(h, off, b + 1))
                            nc.gpsimd.tensor_tensor(both, both, bcast(dec[p][0][:, tok(b)], 1, 2), ALU.mult).then_inc(b_kq.sem, 1)
                            continue
                        half = 1 << l
                        nb = T // (2 * half)
                        d = dec[p][l][:, b * 2 * nb:(b + 1) * 2 * nb].rearrange("p (n two) -> p n two", two=2)
                        pool.wait_ge(*b_kq.at(h, off, 2 * s + b - 1))
                        if l:
                            pool.wait_ge(*b_dec.at(h, off, 2 * (l - 1) + b + 1))
                            pool.wait_ge(*b_ks.at(h, off, 2 * (l - 1) + b + 1))
                        second = both.rearrange("p m (n two h) -> p m n two h", two=2, h=half)[:, :, :, 1, :]
                        nc.gpsimd.tensor_tensor(second, second, bcast(bcast(d[:, :, 0], 2, half), 1, 2), ALU.mult).then_inc(b_kq.sem, 1)
                        first = ks[p][:, tok(b)].rearrange("p (n two h) -> p n two h", two=2, h=half)[:, :, 0, :]
                        nc.gpsimd.tensor_tensor(first, first, bcast(d[:, :, 1], 2, half), ALU.mult).then_inc(b_ks.sem, 1)
                        if l == LEVELS - 1:
                            pool.wait_ge(*c_s.at(h, off - 2))
                        nc.gpsimd.tensor_tensor(dec[p][l + 1][:, b * nb:(b + 1) * nb], d[:, :, 0], d[:, :, 1], ALU.mult).then_inc(b_dec.sem, 1)

            def Cp(h, off, s, k):
                p = off % 2
                if s == NC_ + 1 and k < PB:
                    pool.wait_ge(*c_gs.at(h, off, k + 1))
                    pool.wait_ge(*c_nrm.at(h, off, k + 1))
                    nc.gpsimd.tensor_tensor(o[:, k, :], o[:, k, :], gate[:, tok(k)], ALU.mult).then_inc(c_gate.sem, 1)

            def steps(h, a=None, b=None, c=None):
                for s in range(STEPS):
                    for k in range(3):
                        if b is not None:
                            Bp(h, b, s, k)
                        if c is not None:
                            Cp(h, c, s, k)
                        if a is not None:
                            A(h, a, s, k)

            steps(0, a=0)
            steps(0, a=1, b=0)
            with pool.Fori(0, TURNS - 1) as h:
                steps(h, a=2, b=1, c=0)
                steps(h, a=3, b=2, c=1)
            steps(TURNS - 1, b=1, c=0)
            steps(TURNS - 1, c=1)
class Constants:
    pass


def program(nc, dram, out_dram):
    with ExitStack() as ctx:
        signals = ctx.enter_context(Signals(nc))
        def sb(n, shape, dt=F32):
            return ctx.enter_context(nc.sbuf_tensor(n, shape, dt))

        K = Constants()
        X = sb("X", [P, KC, N])
        XN = sb("XN", [P, KC, N])
        K.mats = sb("mats", [P, N_MATS, P])
        K.small = sb("small", [P, N_SMALL])
        K.vec = sb("vec", [P, V_COUNT, KC])
        with nc.semaphore("loaded") as loaded, nc.Block() as block:
            @block.sync
            def _(sp):
                sp.dma_start(X[:], dram["x"][:]).then_inc(loaded, 16)
                sp.dma_start(K.mats[:], dram["mats"][:]).then_inc(loaded, 16)
                sp.dma_start(K.small[:], dram["small"][:]).then_inc(loaded, 16)
                sp.dma_start(K.vec[:], dram["vec"][:]).then_inc(loaded, 16)
                sp.wait_ge(loaded, 64)

        norm_stage(nc, "ln0", K, X, XN, True, EPS5, None)
        memory_stage(nc, K, X, XN, dram["l0w"])
        with nc.sbuf_tensor("HID", [P, KC, N], F32) as HID:
            norm_stage(nc, "ln1", K, X, HID, True, EPS5, None)
            norm_stage(nc, "rms1", K, HID, XN, False, EPS6, V_LN1)
            attention_stage(nc, K, HID, XN, dram["attn_w"])
            norm_stage(nc, "rms2", K, HID, XN, False, EPS6, V_LN2)
            swiglu_stage(nc, "moe", K, X, XN, J0, dram["ff0_up"], dram["ff0_down"], HID, dram["gate_w"], dram["expert_of"], dram["earlier"])
        norm_stage(nc, "ln2", K, X, XN, True, EPS5, None)
        delta_stage(nc, K, X, XN, dram)
        norm_stage(nc, "ln3", K, X, XN, True, EPS5, None)
        swiglu_stage(nc, "ffn", K, X, XN, J1, dram["ff1_up"], dram["ff1_down"])
        with nc.semaphore("stored") as stored, nc.Block() as block:
            @block.sync
            def _(sp):
                sp.dma_start(out_dram[:], X[:]).then_inc(stored, 16)
                sp.wait_ge(stored, 16)


def constants():
    i = np.arange(P)
    mats = np.zeros((P, N_MATS, P), np.float32)
    mats[:, EYE] = np.eye(P)
    mats[:, MEAN_C] = 1.0 / C
    mats[:, MEAN_D] = (i[:, None] // D0 == i[None, :] // D0) / D0
    mats[:, MEAN_P] = 1.0 / P
    mats[:, ONES] = 1.0
    mats[:, CAUSAL_OUT] = -1e9 * (i[None, :] > i[:, None])
    small = np.zeros((P, N_SMALL), np.float32)
    small[:, EPS5], small[:, EPS6] = 1e-5, 1e-6
    small[:, ONE] = 1.0
    small[:, L2BACK] = 10.0 * np.log(2.0)
    small[:, QSCALE] = np.log(128.0) * -0.5
    for l in range(LEVELS):
        odd = i >> l & 1
        small[:, ODD0 + l] = -odd.astype(np.float32)
        small[:, EVEN0 + l] = 1 - odd
    level_mask = np.zeros((P, LEVELS, P // 2), np.float32)
    for l in range(LEVELS):
        seconds = i[(i >> l & 1) == 1]
        level_mask[:, l] = ((i[:, None] >> l & 1) == 0) & (i[:, None] >> l + 1 == seconds[None, :] >> l + 1)
    ch = np.arange(J0 * P)
    expert_of = (np.minimum(ch // I, E)[None, :] == np.arange(SELROWS)[:, None]).astype(np.float32)
    earlier = np.broadcast_to(np.tri(E, k=-1, dtype=np.float32), (P, E, E))
    return {"earlier": earlier, "mats": mats, "small": small, "level_mask": level_mask,
            "expert_of": expert_of.reshape(SELROWS, J0, P)}


def halves(w):
    return w.reshape(KC, P, -1).transpose(1, 0, 2)


def columns(v):
    return v.reshape(KC, P).T


def hidden_blocks(gate, up, down, blocks):
    def padded(w):
        out = np.zeros((blocks * P, C), np.float32)
        out[:w.shape[0]] = w
        return out
    ups = np.stack([padded(w).reshape(blocks, P, KC, P).transpose(3, 0, 2, 1) for w in (gate, up)], axis=3)
    return ups, padded(down).reshape(blocks, P, C).transpose(1, 0, 2)


def layouts(a):
    a = {k: np.asarray(v) for k, v in a.items()}
    L0, F0, L1, F1 = ({k[len(p):]: v for k, v in a.items() if k.startswith(p)} for p in ("L0_attn_", "L0_ffn_", "L1_attn_", "L1_ffn_"))
    out = constants()
    out["x"] = halves(L0["x"].reshape(N, C).T)
    mats = [L0["Wq"], L0["Wk"], L0["Wv"], L0["ig_w"], L0["og_w"], np.repeat(L0["gamma_w"], D0, axis=0), L0["Wo"]]
    out["l0w"] = np.stack([halves(m.T) for m in mats], axis=1)
    taps = [L0["conv_w"][:, 0, i] for i in range(KTAPS)]
    vec = taps + [L0["conv_b"], L0["ig_b"], L0["og_b"], np.repeat(L0["gamma_b"], D0)]
    vec += [np.tile(L0[n], HEADS) for n in ("vn_g", "vn_b", "mn_g", "mn_b")] + [L0["gn_g"], L0["gn_b"], F0["ln1_w"], F0["ln2_w"], np.tile(L1["o_norm_w"], KC)]
    out["vec"] = np.stack([columns(v) for v in vec], axis=1)
    qw = F0["q_w"].reshape(HEADS, QHD, C)[:, :P]
    kw = F0["kv_w"][:HEADS * P].reshape(HEADS, P, C)
    vw = F0["kv_w"][HEADS * P:2 * HEADS * P].reshape(HEADS, P, C)
    qkv = np.stack([w.reshape(HEADS, P, KC, P).transpose(0, 3, 2, 1) for w in (qw, kw, vw)], axis=2)
    ow = F0["o_w"].reshape(C, HEADS, VD).transpose(1, 2, 0)
    out["attn_w"] = np.concatenate([qkv.reshape(HEADS, P, -1), ow], axis=2)
    w1, w2 = F0["w1"], F0["w2"]
    gate = np.concatenate([w1[:, :I].reshape(E * I, C), F0["sh_gu_w"][:SHI]])
    up = np.concatenate([w1[:, I:].reshape(E * I, C), F0["sh_gu_w"][SHI:]])
    down = np.concatenate([w2.transpose(0, 2, 1).reshape(E * I, C), F0["sh_down_w"].T])
    out["ff0_up"], out["ff0_down"] = hidden_blocks(gate, up, down, J0)
    out["gate_w"] = halves(F0["gate_w"].T)
    out["ff1_up"], out["ff1_down"] = hidden_blocks(F1["w_gate"], F1["w_up"], F1["w_down"].T, J1)
    def by_head(w):
        return w.reshape(KC, P, HEADS, P).transpose(2, 1, 0, 3).reshape(HEADS, P, KC * P)
    cols = [L1[n].reshape(HEADS, P, KTAPS) for n in ("conv_q", "conv_k", "conv_v")]
    cols += [L1["dt_bias"].reshape(HEADS, P, 1), L1["bg"].reshape(HEADS, P, 1), np.broadcast_to(L1["A_log"][:, None, None], (HEADS, P, 1)),
             np.zeros((HEADS, P, 1), np.float32)]
    out["delta_w"] = np.concatenate([by_head(L1["Wq"]), by_head(L1["Wk"]), by_head(L1["Wv"]), by_head(L1["Wg"]),
                                     L1["Wf2"].reshape(P, HEADS, P).transpose(1, 0, 2), L1["Wo"].reshape(HEADS, P, C)] + cols, axis=2)
    out["delta_f1"] = halves(L1["Wf1"])
    out["delta_b"] = halves(L1["Wb"])
    return {k: np.ascontiguousarray(v) for k, v in out.items()}


def kernel(**inputs):
    import concourse.bacc as bacc
    from concourse.bass_utils import run_bass_kernel_spmd

    arrays = layouts(inputs)
    nc = bacc.Bacc("TRN2", target_bir_lowering=False, num_devices=1)
    dram = {k: nc.dram_tensor("in_" + k, v.shape, mybir.dt.from_np(v.dtype), kind="ExternalInput").ap() for k, v in arrays.items()}
    out = nc.dram_tensor("out", [P, KC, N], F32, kind="ExternalOutput").ap()
    program(nc, dram, out)
    r = run_bass_kernel_spmd(nc, [{"in_" + k: v for k, v in arrays.items()}], core_ids=[0])
    y = r.results[0]["out"]
    return y.transpose(1, 0, 2).reshape(C, N).T.reshape(B, T, C)
```
